# Optimizing a Trainium2 kernel written in Bass

```python
import numpy as np
import jax
import jax.numpy as jnp

def _softmax(x, axis=-1):
    return jax.nn.softmax(x, axis=axis)

def _gelu(x):
    return jax.nn.gelu(x, approximate=True)

def _silu(x):
    return jax.nn.silu(x)

def _sigmoid(x):
    return jax.nn.sigmoid(x)

def _layernorm(x, axis=-1, eps=1e-05):
    m = jnp.mean(x, axis=axis, keepdims=True)
    v = jnp.var(x, axis=axis, keepdims=True)
    return (x - m) / jnp.sqrt(v + eps)

def _scatter_add(tgt, idx, src, axis=0):
    return tgt.at[idx].add(src)

def _segment_sum(src, seg, n):
    return jax.ops.segment_sum(src, seg, n)
kernel_name = 'mk_adaln_d2_jaxref_r4_48ee40'

def setup_inputs(seed: int=0):
    np.random.seed(seed)
    _w = jnp.asarray

    def _L0_attn_setup():
        import jax, jax.numpy as jnp
        import numpy as np
        B, N, C = (8, 1024, 256)
        key = jax.random.key(seed)
        k1, k2, k3 = jax.random.split(key, 3)
        x = jax.random.normal(k1, (B, N, C), dtype=jnp.float32)
        w_qkv = jax.random.normal(k2, (3 * C, C), dtype=jnp.float32) * C ** (-0.5)
        w_conv1 = jax.random.normal(k3, (C,), dtype=jnp.float32) * C ** (-0.5)
        return {'x': x, 'w_qkv': w_qkv, 'w_conv1': w_conv1}
    _L0_attn_in = _L0_attn_setup()

    def _L0_ffn_setup():
        import jax, jax.numpy as jnp
        import numpy as np
        CAP_FACTOR = 1.5
        key = jax.random.key(seed)
        ks = jax.random.split(key, 6)
        E, S, D, M = (48, 4, 256, 256)
        K = D // S
        x = jax.random.normal(ks[0], (4, 1024, D), dtype=jnp.float32)
        Wr = jax.random.normal(ks[1], (E, D), dtype=jnp.float32) * 0.02
        W1 = jax.random.normal(ks[2], (E, S, D, M), dtype=jnp.float32) * (1.0 / np.sqrt(D))
        b1 = jnp.zeros((E, S, M), dtype=jnp.float32)
        W2 = jax.random.normal(ks[3], (E, S, M, K), dtype=jnp.float32) * (1.0 / np.sqrt(M))
        b2 = jnp.zeros((E, S, K), dtype=jnp.float32)
        return {'x': x, 'Wr': Wr, 'W1': W1, 'b1': b1, 'W2': W2, 'b2': b2}
    _L0_ffn_in = _L0_ffn_setup()
    _L0_c = _w((lambda *s: np.random.randn(*s).astype(np.float32) * 0.05)(4, 256))
    _L0_wmod = _w((lambda *s: np.random.randn(*s).astype(np.float32) * 0.05)(256, 6 * 256) * 256 ** (-0.5))

    def _L1_attn_setup():
        import jax, jax.numpy as jnp
        import numpy as np
        B, N, D = (4, 1024, 256)
        H, DH = (16, 64)
        DFF = 1024
        M = 64
        EPS_KERN = 1e-06
        EPS_LN = 1e-06

        def _softmax_kernel_feats(data, proj, is_query):
            dn = 1.0 / jnp.sqrt(jnp.sqrt(jnp.float32(data.shape[-1])))
            ratio = 1.0 / jnp.sqrt(jnp.float32(proj.shape[0]))
            data_dash = jnp.einsum('bnhd,md->bnhm', data * dn, proj)
            diag = jnp.sum(jnp.square(data), axis=-1, keepdims=True) * (dn * dn) / 2.0
            if is_query:
                mx = jnp.max(data_dash, axis=-1, keepdims=True)
            else:
                mx = jnp.max(data_dash)
            return ratio * (jnp.exp(data_dash - diag - mx) + EPS_KERN)

        def _layernorm(x, g, b):
            mu = jnp.mean(x, axis=-1, keepdims=True)
            var = jnp.mean(jnp.square(x - mu), axis=-1, keepdims=True)
            return (x - mu) * jax.lax.rsqrt(var + EPS_LN) * g + b

        def _encoder_forward(x, Wq, Wk, Wv, Wo, proj, W1, b1, W2, b2, ln1_g, ln1_b, ln2_g, ln2_b):
            q = jnp.einsum('bnd,dhk->bnhk', x, Wq)
            k = jnp.einsum('bnd,dhk->bnhk', x, Wk)
            v = jnp.einsum('bnd,dhk->bnhk', x, Wv)
            qf = _softmax_kernel_feats(q, proj, True)
            kf = _softmax_kernel_feats(k, proj, False)
            kv = jnp.einsum('bnhm,bnhd->bhmd', kf, v)
            num = jnp.einsum('bnhm,bhmd->bnhd', qf, kv)
            den = jnp.einsum('bnhm,bhm->bnh', qf, jnp.sum(kf, axis=1))
            attn = num / den[..., None]
            attn_out = jnp.einsum('bnhd,hdo->bno', attn, Wo)
            out1 = _layernorm(x + attn_out, ln1_g, ln1_b)
            h = jax.nn.elu(out1 @ W1 + b1)
            ffn_out = h @ W2 + b2
            return _layernorm(out1 + ffn_out, ln2_g, ln2_b)
        key = jax.random.key(seed)
        ks = jax.random.split(key, 12)
        s = 0.02
        inp = {'x': jax.random.normal(ks[0], (B, N, D), jnp.float32), 'Wq': jax.random.normal(ks[1], (D, H, DH), jnp.float32) * s, 'Wk': jax.random.normal(ks[2], (D, H, DH), jnp.float32) * s, 'Wv': jax.random.normal(ks[3], (D, H, DH), jnp.float32) * s, 'Wo': jax.random.normal(ks[4], (H, DH, D), jnp.float32) * s, 'proj': jax.random.normal(ks[5], (M, DH), jnp.float32), 'W1': jax.random.normal(ks[6], (D, DFF), jnp.float32) * s, 'b1': jnp.zeros((DFF,), jnp.float32), 'W2': jax.random.normal(ks[7], (DFF, D), jnp.float32) * s, 'b2': jnp.zeros((D,), jnp.float32), 'ln1_g': jnp.ones((D,), jnp.float32), 'ln1_b': jnp.zeros((D,), jnp.float32), 'ln2_g': jnp.ones((D,), jnp.float32), 'ln2_b': jnp.zeros((D,), jnp.float32)}
        return inp
    _L1_attn_in = _L1_attn_setup()

    def _L1_ffn_setup():
        import jax, jax.numpy as jnp
        import numpy as np
        B, S, D_MODEL, D_FF = (4, 512, 256, 1024)

        def _quantum_transform(hidden, theta, w_real, w_imag):
            imag = w_imag * jnp.sin(theta + hidden * 0.1)
            quantum_phase = jnp.cos(theta) * w_real + jnp.sin(theta) * w_imag
            return hidden + quantum_phase * imag * 0.1
        key = jax.random.key(seed)
        ks = jax.random.split(key, 8)
        return {'x': jax.random.normal(ks[0], (B, S, D_MODEL), dtype=jnp.float32), 'W1': jax.random.normal(ks[1], (D_MODEL, D_FF), dtype=jnp.float32) * (1.0 / np.sqrt(D_MODEL)), 'b1': jnp.zeros((D_FF,), dtype=jnp.float32), 'quantum_phases': jax.random.normal(ks[2], (D_FF,), dtype=jnp.float32) * (2.0 * np.pi), 'quantum_weights_real': jax.random.normal(ks[3], (D_FF,), dtype=jnp.float32) * 0.1, 'quantum_weights_imag': jax.random.normal(ks[4], (D_FF,), dtype=jnp.float32) * 0.1, 'W2': jax.random.normal(ks[5], (D_FF, D_MODEL), dtype=jnp.float32) * (1.0 / np.sqrt(D_FF)), 'b2': jnp.zeros((D_MODEL,), dtype=jnp.float32)}
    _L1_ffn_in = _L1_ffn_setup()
    _L1_c = _w((lambda *s: np.random.randn(*s).astype(np.float32) * 0.05)(4, 256))
    _L1_wmod = _w((lambda *s: np.random.randn(*s).astype(np.float32) * 0.05)(256, 6 * 256) * 256 ** (-0.5))
    _d = {'L0_attn_x': _L0_attn_in['x'], 'L0_attn_w_qkv': _L0_attn_in['w_qkv'], 'L0_attn_w_conv1': _L0_attn_in['w_conv1'], 'L0_ffn_Wr': _L0_ffn_in['Wr'], 'L0_ffn_W1': _L0_ffn_in['W1'], 'L0_ffn_b1': _L0_ffn_in['b1'], 'L0_ffn_W2': _L0_ffn_in['W2'], 'L0_ffn_b2': _L0_ffn_in['b2'], 'L0_c': _L0_c, 'L0_wmod': _L0_wmod, 'L1_attn_Wq': _L1_attn_in['Wq'], 'L1_attn_Wk': _L1_attn_in['Wk'], 'L1_attn_Wv': _L1_attn_in['Wv'], 'L1_attn_Wo': _L1_attn_in['Wo'], 'L1_attn_proj': _L1_attn_in['proj'], 'L1_attn_W1': _L1_attn_in['W1'], 'L1_attn_b1': _L1_attn_in['b1'], 'L1_attn_W2': _L1_attn_in['W2'], 'L1_attn_b2': _L1_attn_in['b2'], 'L1_attn_ln1_g': _L1_attn_in['ln1_g'], 'L1_attn_ln1_b': _L1_attn_in['ln1_b'], 'L1_attn_ln2_g': _L1_attn_in['ln2_g'], 'L1_attn_ln2_b': _L1_attn_in['ln2_b'], 'L1_ffn_W1': _L1_ffn_in['W1'], 'L1_ffn_b1': _L1_ffn_in['b1'], 'L1_ffn_quantum_phases': _L1_ffn_in['quantum_phases'], 'L1_ffn_quantum_weights_real': _L1_ffn_in['quantum_weights_real'], 'L1_ffn_quantum_weights_imag': _L1_ffn_in['quantum_weights_imag'], 'L1_ffn_W2': _L1_ffn_in['W2'], 'L1_ffn_b2': _L1_ffn_in['b2'], 'L1_c': _L1_c, 'L1_wmod': _L1_wmod}
    _x0 = _d['L0_attn_x']
    _d['L0_attn_x'] = jax.random.normal(jax.random.fold_in(jax.random.key(seed), 1), (4, 1024, 256), dtype=_x0.dtype)
    del _x0
    return _d

def reference(L0_attn_x, L0_attn_w_qkv, L0_attn_w_conv1, L0_ffn_Wr, L0_ffn_W1, L0_ffn_b1, L0_ffn_W2, L0_ffn_b2, L0_c, L0_wmod, L1_attn_Wq, L1_attn_Wk, L1_attn_Wv, L1_attn_Wo, L1_attn_proj, L1_attn_W1, L1_attn_b1, L1_attn_W2, L1_attn_b2, L1_attn_ln1_g, L1_attn_ln1_b, L1_attn_ln2_g, L1_attn_ln2_b, L1_ffn_W1, L1_ffn_b1, L1_ffn_quantum_phases, L1_ffn_quantum_weights_real, L1_ffn_quantum_weights_imag, L1_ffn_W2, L1_ffn_b2, L1_c, L1_wmod):

    def _L0_attn_ref(x, w_qkv, w_conv1):
        import jax, jax.numpy as jnp
        import numpy as np
        B, N, C = (8, 1024, 256)
        b, n, c = x.shape
        scale = c ** (-0.5)
        qkv = jnp.einsum('bnc,dc->bnd', x, w_qkv)
        q = qkv[..., :c]
        k = qkv[..., c:2 * c]
        v = qkv[..., 2 * c:]
        agent = jnp.einsum('bnc,c->bn', q, w_conv1)
        agent_attn = jax.nn.softmax(jnp.einsum('bn,bnc->bc', agent * scale, k), axis=-1)
        agent_v = jax.nn.softmax(jnp.einsum('bc,bnc->bn', agent_attn, v), axis=-1)
        agent_v = jnp.einsum('bn,bnc->bc', agent_v, v)
        agent_tok = jax.nn.softmax(agent[:, :, None], axis=-1)
        return agent_tok * agent_v[:, None, :]

    def _L0_ffn_ref(x, Wr, W1, b1, W2, b2):
        import jax, jax.numpy as jnp
        import numpy as np
        CAP_FACTOR = 1.5
        orig_shape = x.shape
        D = x.shape[-1]
        E = Wr.shape[0]
        xf = x.reshape(-1, D)
        T = xf.shape[0]
        cap = int(CAP_FACTOR * T / E)
        logits = xf @ Wr.T
        vals, idx = jax.lax.top_k(logits.T, cap)
        w = jax.nn.softmax(vals, axis=-1)
        xg = xf[idx]
        h = jax.nn.gelu(jnp.einsum('ecd,esdm->ecsm', xg, W1) + b1[:, None], approximate=False)
        y = jnp.einsum('ecsm,esmk->ecsk', h, W2) + b2[:, None]
        y = y.reshape(E, cap, D) * w[..., None]
        out = jnp.zeros_like(xf).at[idx.reshape(-1)].add(y.reshape(-1, D))
        return out.reshape(orig_shape)

    def _L1_attn_ref(x, Wq, Wk, Wv, Wo, proj, W1, b1, W2, b2, ln1_g, ln1_b, ln2_g, ln2_b):
        import jax, jax.numpy as jnp
        import numpy as np
        B, N, D = (4, 1024, 256)
        H, DH = (16, 64)
        DFF = 1024
        M = 64
        EPS_KERN = 1e-06
        EPS_LN = 1e-06

        def _softmax_kernel_feats(data, proj, is_query):
            dn = 1.0 / jnp.sqrt(jnp.sqrt(jnp.float32(data.shape[-1])))
            ratio = 1.0 / jnp.sqrt(jnp.float32(proj.shape[0]))
            data_dash = jnp.einsum('bnhd,md->bnhm', data * dn, proj)
            diag = jnp.sum(jnp.square(data), axis=-1, keepdims=True) * (dn * dn) / 2.0
            if is_query:
                mx = jnp.max(data_dash, axis=-1, keepdims=True)
            else:
                mx = jnp.max(data_dash)
            return ratio * (jnp.exp(data_dash - diag - mx) + EPS_KERN)

        def _layernorm(x, g, b):
            mu = jnp.mean(x, axis=-1, keepdims=True)
            var = jnp.mean(jnp.square(x - mu), axis=-1, keepdims=True)
            return (x - mu) * jax.lax.rsqrt(var + EPS_LN) * g + b

        def _encoder_forward(x, Wq, Wk, Wv, Wo, proj, W1, b1, W2, b2, ln1_g, ln1_b, ln2_g, ln2_b):
            q = jnp.einsum('bnd,dhk->bnhk', x, Wq)
            k = jnp.einsum('bnd,dhk->bnhk', x, Wk)
            v = jnp.einsum('bnd,dhk->bnhk', x, Wv)
            qf = _softmax_kernel_feats(q, proj, True)
            kf = _softmax_kernel_feats(k, proj, False)
            kv = jnp.einsum('bnhm,bnhd->bhmd', kf, v)
            num = jnp.einsum('bnhm,bhmd->bnhd', qf, kv)
            den = jnp.einsum('bnhm,bhm->bnh', qf, jnp.sum(kf, axis=1))
            attn = num / den[..., None]
            attn_out = jnp.einsum('bnhd,hdo->bno', attn, Wo)
            out1 = _layernorm(x + attn_out, ln1_g, ln1_b)
            h = jax.nn.elu(out1 @ W1 + b1)
            ffn_out = h @ W2 + b2
            return _layernorm(out1 + ffn_out, ln2_g, ln2_b)
        return _encoder_forward(x, Wq, Wk, Wv, Wo, proj, W1, b1, W2, b2, ln1_g, ln1_b, ln2_g, ln2_b)

    def _L1_ffn_ref(x, W1, b1, quantum_phases, quantum_weights_real, quantum_weights_imag, W2, b2):
        import jax, jax.numpy as jnp
        import numpy as np
        B, S, D_MODEL, D_FF = (4, 512, 256, 1024)

        def _quantum_transform(hidden, theta, w_real, w_imag):
            imag = w_imag * jnp.sin(theta + hidden * 0.1)
            quantum_phase = jnp.cos(theta) * w_real + jnp.sin(theta) * w_imag
            return hidden + quantum_phase * imag * 0.1
        hidden = jnp.einsum('bsd,df->bsf', x, W1) + b1
        q = _quantum_transform(hidden, quantum_phases, quantum_weights_real, quantum_weights_imag)
        act = jax.nn.relu(q)
        return jnp.einsum('bsf,fd->bsd', act, W2) + b2
    x = L0_attn_x
    mod = (_silu(L0_c) @ L0_wmod).reshape(L0_c.shape[0], 6, 1, -1)
    sa, ca, ga, sb, cb, gb = (mod[:, 0], mod[:, 1], mod[:, 2], mod[:, 3], mod[:, 4], mod[:, 5])
    ga = (2 * (ga >= 0) - 1) * jnp.maximum(jnp.abs(ga), 0.25)
    gb = (2 * (gb >= 0) - 1) * jnp.maximum(jnp.abs(gb), 0.25)
    h = _layernorm(x, axis=-1) * (1 + ca) + sa
    x = x + ga * _L0_attn_ref(h, L0_attn_w_qkv, L0_attn_w_conv1)
    h = _layernorm(x, axis=-1) * (1 + cb) + sb
    x = x + gb * _L0_ffn_ref(h, L0_ffn_Wr, L0_ffn_W1, L0_ffn_b1, L0_ffn_W2, L0_ffn_b2)
    mod = (_silu(L1_c) @ L1_wmod).reshape(L1_c.shape[0], 6, 1, -1)
    sa, ca, ga, sb, cb, gb = (mod[:, 0], mod[:, 1], mod[:, 2], mod[:, 3], mod[:, 4], mod[:, 5])
    ga = (2 * (ga >= 0) - 1) * jnp.maximum(jnp.abs(ga), 0.25)
    gb = (2 * (gb >= 0) - 1) * jnp.maximum(jnp.abs(gb), 0.25)
    h = _layernorm(x, axis=-1) * (1 + ca) + sa
    x = x + ga * _L1_attn_ref(h, L1_attn_Wq, L1_attn_Wk, L1_attn_Wv, L1_attn_Wo, L1_attn_proj, L1_attn_W1, L1_attn_b1, L1_attn_W2, L1_attn_b2, L1_attn_ln1_g, L1_attn_ln1_b, L1_attn_ln2_g, L1_attn_ln2_b)
    h = _layernorm(x, axis=-1) * (1 + cb) + sb
    x = x + gb * _L1_ffn_ref(h, L1_ffn_W1, L1_ffn_b1, L1_ffn_quantum_phases, L1_ffn_quantum_weights_real, L1_ffn_quantum_weights_imag, L1_ffn_W2, L1_ffn_b2)
    return x

_drawn_inputs = setup_inputs


def setup_inputs(seed=0):
    import zlib

    import numpy as np

    out = dict(_drawn_inputs(seed))
    spreads = {'L0_ffn_b1': (0.0, 0.8),
     'L0_ffn_b2': (0.0, 2.0),
     'L1_attn_b1': (0.0, 1.594),
     'L1_attn_b2': (0.0, 0.352),
     'L1_attn_ln1_g': (1.0, 0.567),
     'L1_attn_ln1_b': (0.0, 0.355),
     'L1_attn_ln2_g': (1.0, 0.6),
     'L1_attn_ln2_b': (0.0, 0.333),
     'L1_ffn_b1': (0.0, 0.48),
     'L1_ffn_b2': (0.0, 0.322)}
    factors = {'L0_ffn_Wr': 8.0,
     'L0_ffn_W1': 8.0,
     'L0_ffn_W2': 8.0,
     'L1_attn_Wq': 64.0,
     'L1_attn_Wk': 8.0,
     'L1_attn_Wv': 6.716,
     'L1_attn_Wo': 6.695,
     'L1_attn_proj': 64.0,
     'L1_ffn_quantum_phases': 64.0,
     'L1_ffn_quantum_weights_real': 64.0,
     'L1_ffn_quantum_weights_imag': 64.0,
     'L1_attn_W1': 2.704}
    for name, (base, spread) in spreads.items():
        noise = np.random.default_rng([zlib.crc32(name.encode()), seed]).standard_normal(out[name].shape)
        drawn = base * np.exp(spread * noise) if base else spread * noise
        out[name] = jnp.asarray(drawn.astype(out[name].dtype))
    for name, factor in factors.items():
        out[name] = (out[name] * factor).astype(out[name].dtype)
    return out
```

```python
from contextlib import ExitStack

import concourse.bass as bass
from concourse import mybir

ALU = mybir.AluOpType
ACT = mybir.ActivationFunctionType
AX = mybir.AxisListType
F32 = mybir.dt.float32
F32R = mybir.dt.float32r
U32 = mybir.dt.uint32

P = 128
B, N, D = 4, 1024, 256
T = B * N
NT = T // P
TB = N // P
KD = D // P
G = 4
GT = G * P
NG = NT // G
E, S, M = 48, 4, 256
KS = D // S
CAP = int(1.5 * T / E)
H, DH, MF = 16, 64, 64
HD = H * DH
CH = HD // P
DFF = 1024
CF = DFF // P
LN_EPS = 1e-5
ENC_EPS = 1e-6
KERN_EPS = 1e-6
DN = float(DH) ** -0.25
GATE_MIN = 0.25
SA, CA, GA, SB, CB, GB = range(6)
PI2_HI, PI2_LO = 6.28125, 0.0019353071795864769
ROUND = 12582912.0
LOWEST = -3.0e38


class Steps:

    def __init__(self, eng, sem, base=0):
        self.eng, self.sem, self.base, self.n = eng, sem, base, 0

    def mark(self, ins):
        self.n += 1
        ins.then_inc(self.sem, 1)

    def sync(self):
        self.eng.wait_ge(self.sem, self.base + self.n)

    def __call__(self, ins):
        self.mark(ins)
        self.sync()


def batches(eng, body):
    with eng.Fori(0, B - 1) as b:
        body(b, False)
    body(B - 1, True)


class Maker:

    def __init__(self, nc, ctx):
        self.nc, self.ctx, self.signals = nc, ctx, []

    def sb(self, name, shape, dt=F32):
        return self.ctx.enter_context(self.nc.sbuf_tensor(name, shape, dt))

    def ps(self, name, shape, dt=F32):
        return self.ctx.enter_context(self.nc.psum_tensor(name, shape, dt))

    def sem(self, name):
        handle = self.nc.alloc_semaphore(name=name)
        self.signals.append(handle)
        return handle

    def clear_signals(self):
        self.nc.clear_and_free_semaphores(self.signals)
        self.signals = []
        self.nc.all_engine_barrier()


def layer_norm_stats(v, mv_spare, st, mv, var, tiles, x_tile, eps, var_ready):
    for j in range(tiles):
        v.mark(v.eng.bn_stats(st[:, j, :], x_tile(j)))
    v.sync()
    v.eng.memset(mv_spare[:], 0.0)
    for j in range(tiles):
        v.mark(v.eng.bn_aggr(mv[:, j, :], st[:, j, :]))
    v.sync()
    v.eng.tensor_scalar(var[:, 0:tiles], mv[:, 0:tiles, 1], eps, None, ALU.add).then_inc(var_ready, 1)


def rsqrt_rows(pool, rstd, var, minus_half, tiles, rstd_ready):
    pool.tensor_tensor(rstd[:, 0:tiles], var[:, 0:tiles], minus_half[:, 0:tiles], ALU.pow).then_inc(rstd_ready, 1)


def setup(nc, mk, g, a):
    with ExitStack() as ctx:
        t = Maker(nc, ctx)
        c_rows = t.sb("c_rows", [B, 2, D])
        c_exp = t.sb("c_exp", [B, 2, D])
        c_silu = t.sb("c_silu", [B, 2, D])
        cT = t.sb("cT", [P, 2, KD, B])
        wmod = t.sb("wmod", [P, 2, KD, 6 * D])
        rows = t.sb("rows", [B, 2, 6, D])
        size = t.sb("size", [B, 2, 2, D])
        sign = t.sb("sign", [B, 2, 2, D])
        cT_ps = t.ps("cT_ps", [P, 2, KD, B])
        mod_ps = t.ps("mod_ps", [P, 2, 6 * D])

        c_in, wmod_in, x_in, w_in = mk.sem("c_in"), mk.sem("wmod_in"), mk.sem("x_in"), mk.sem("w_in")
        zeroed, ident_done, exp_done = mk.sem("zeroed"), mk.sem("ident_done"), mk.sem("exp_done")
        silu_done, cT_done, cT_copied = mk.sem("silu_done"), mk.sem("cT_done"), mk.sem("cT_copied")
        mod_done, rows_done, rows_out, modb_in = (mk.sem("mod_done"), mk.sem("rows_done"), mk.sem("rows_out"),
                                                  mk.sem("modb_in"))
        own = mk.sem("setup_dve")

        with nc.Block() as block:
            @block.sync
            def _(sp):
                sp.dma_start(c_rows[:, 0, :], a["L0_c"]).then_inc(c_in, 16)
                sp.dma_start(c_rows[:, 1, :], a["L1_c"]).then_inc(c_in, 16)
                for l in range(2):
                    sp.dma_start(wmod[:, l, :, :], a[f"L{l}_wmod"].rearrange("(k p) n -> p k n", p=P)).then_inc(wmod_in, 16)
                sp.dma_start(g.x[:], a["L0_attn_x"].rearrange("b (t p) d -> p (b t) d", p=P)).then_inc(x_in, 16)
                sp.wait_ge(rows_done, 1)
                sp.dma_start(g.mod_dram.rearrange("l b n -> b l n"), rows[:].rearrange("b l s d -> b l (s d)")).then_inc(rows_out, 16)
                sp.wait_ge(rows_out, 16)
                sp.dma_start(g.modb[:], g.mod_dram[0].partition_broadcast(P)).then_inc(modb_in, 16)
                sp.wait_ge(modb_in, 16)
                sp.wait_ge(x_in, 16)

            @block.scalar
            def _(act):
                act.dma_start(g.wqkv[:], a["L0_attn_w_qkv"].rearrange("(j p) c -> p j c", p=P)).then_inc(w_in, 16)
                act.dma_start(g.wconv[:], a["L0_attn_w_conv1"].rearrange("(j p) -> p j", p=P),
                              allow_slow_non_contiguous=True).then_inc(w_in, 16)
                act.wait_ge(c_in, 32)
                act.activation(c_exp[:], c_rows[:], ACT.Exp, scale=-1.0).then_inc(exp_done, 1)
                act.wait_ge(w_in, 32)

            @block.gpsimd
            def _(pool):
                pool.memset(g.ident[:], 0.0).then_inc(zeroed, 1)
                pool.memset(g.flip[:], 0.0).then_inc(zeroed, 1)
                pool.memset(g.ones[:], 1.0)
                pool.memset(g.minus_half[:], -0.5)
                pool.memset(g.eye_b[:], 0.0).then_inc(zeroed, 1)
                pool.wait_ge(zeroed, 3)
                pool.affine_select(out=g.ident[:], in_=g.ident[:], compare_op=ALU.not_equal, fill=1.0, base=0,
                                   pattern=[[-1, P]], channel_multiplier=1).then_inc(ident_done, 1)
                pool.affine_select(out=g.flip[:], in_=g.flip[:], compare_op=ALU.not_equal, fill=1.0, base=1 - P,
                                   pattern=[[1, P]], channel_multiplier=1).then_inc(ident_done, 1)
                pool.affine_select(out=g.eye_b[:], in_=g.eye_b[:], compare_op=ALU.not_equal, fill=1.0, base=0,
                                   pattern=[[1, B], [-1, B]], channel_multiplier=0).then_inc(ident_done, 1)
                pool.wait_ge(ident_done, 3)

            @block.vector
            def _(dve):
                v = Steps(dve, own)
                dve.wait_ge(exp_done, 1)
                v(dve.tensor_scalar(c_exp[:], c_exp[:], 1.0, None, ALU.add))
                v(dve.reciprocal(c_exp[:], c_exp[:]))
                dve.tensor_tensor(c_silu[:], c_rows[:], c_exp[:], ALU.mult).then_inc(silu_done, 1)
                dve.wait_ge(cT_done, 1)
                dve.tensor_copy(cT[:], cT_ps[:]).then_inc(cT_copied, 1)
                dve.wait_ge(mod_done, 1)
                v(dve.tensor_copy(rows[:].rearrange("b l s d -> b l (s d)"), mod_ps[0:B]))
                gates, shifts = rows[:, :, GA::3, :], rows[:, :, CA::3, :]
                for l in range(2):
                    v.mark(dve.tensor_scalar(shifts[:, l], shifts[:, l], 1.0, None, ALU.add))
                    v.mark(dve.scalar_tensor_tensor(size[:, l], gates[:, l], -1.0, gates[:, l], ALU.mult, ALU.max))
                    v.mark(dve.tensor_scalar(sign[:, l], gates[:, l], 0.0, 2.0, ALU.is_ge, ALU.mult))
                v.sync()
                v(dve.tensor_scalar(size[:], size[:], GATE_MIN, None, ALU.max))
                for l in range(2):
                    v.mark(dve.scalar_tensor_tensor(gates[:, l], sign[:, l], -1.0, size[:, l], ALU.add, ALU.mult))
                v.sync()
                dve.sem_inc(rows_done, 1)

            @block.tensor
            def _(pe):
                pe.wait_ge(ident_done, 1)
                pe.wait_ge(silu_done, 1)
                for l in range(2):
                    for k in range(KD):
                        last = pe.transpose(cT_ps[:, l, k, :], c_silu[:, l, k * P:(k + 1) * P], g.ident[0:B, 0:B])
                last.then_inc(cT_done, 1)
                pe.wait_ge(cT_copied, 1)
                pe.wait_ge(wmod_in, 32)
                for l in range(2):
                    for n in range(3):
                        cols = slice(n * 512, (n + 1) * 512)
                        for k in range(KD):
                            last = pe.matmul(mod_ps[0:B, l, cols], cT[:, l, k, :], wmod[:, l, k, cols],
                                             start=(k == 0), stop=(k == KD - 1))
                last.then_inc(mod_done, 1)


def agent_attention(nc, mk, g):
    with ExitStack() as ctx:
        t = Maker(nc, ctx)
        h = t.sb("h0", [P, NT, D])
        prod = t.sb("prod", [P, TB, D])
        st, mv, var, rstd = (t.sb("st0", [P, TB, 6]), t.sb("mv0", [P, TB, 2]), t.sb("var0", [P, TB]),
                             t.sb("rstd0", [P, TB]))
        wconv_b = t.sb("wconv_b", [P, KD, P])
        wkT, wvT = t.sb("wkT", [P, KD, D]), t.sb("wvT", [P, KD, D])
        probe = t.sb("probe", [P, D])
        agent = t.sb("agent", [P, NT])
        score = t.sb("score", [P, NT])
        tok = t.sb("tok", [P, NT])
        masked = t.sb("masked", [P, 2, TB, B])
        mix = t.sb("mix", [B, D])
        mixT = t.sb("mixT", [P, KD, B])
        mixT_b = t.sb("mixT_b", [P, KD, B, P])
        keys = t.sb("keys", [B, D])
        small = t.sb("small", [P, 8])
        value_probe = t.sb("value_probe", [P, B, D])
        peak, peak_diag, neg_peak = t.sb("peak", [P, B]), t.sb("peak_diag", [B, B]), t.sb("neg_peak", [P, B])
        peak_row = t.sb("peak_row", [B, 1])
        part_sum, inv_sum = t.sb("part_sum", [P, B]), t.sb("inv_sum", [P, B])
        gated = t.sb("gated", [P, B, D])
        w_ps = t.ps("w_ps", [P, 2, 512])
        probe_ps = t.ps("probe_ps", [P, 512])
        mix_ps = t.ps("mix_ps", [P, 512])
        wide_ps = t.ps("wide_ps", [P, B, D])
        tiny_ps = t.ps("tiny_ps", [P, 512])

        own, wb = mk.sem("aa_dve"), mk.sem("wconv_b_done")
        w_done, w_copied, probe_done = mk.sem("wT_done"), mk.sem("wT_copied"), mk.sem("probe_done")
        var_ready, rstd_ready, masked_ready, mix_done = (mk.sem("aa_var"), mk.sem("aa_rstd"), mk.sem("aa_masked"),
                                                         mk.sem("aa_mix"))
        mod = g.modb[:].rearrange("p b (s d) -> p b s d", s=6)

        with nc.Block() as block:
            @block.vector
            def _(dve):
                v = Steps(dve, own)
                for k in range(KD):
                    v.mark(dve.tensor_scalar(wconv_b[:, k, :], g.ones[:], g.wconv[:, k:k + 1], None, ALU.mult))
                v.mark(dve.memset(mix[:], 0.0))
                v.sync()
                dve.sem_inc(wb, 1)
                dve.wait_ge(probe_done, 1)
                v(dve.tensor_copy(probe[:], probe_ps[:, 0:D]))
                per = 3 * TB + 6
                first = v.n
                with dve.Fori(0, B) as b:
                    v = Steps(dve, own, b * per + first)
                    layer_norm_stats(v, g.spare, st, mv, var, TB, lambda j: g.x[:, bass.ds(b * TB + j, 1), :], LN_EPS, var_ready)
                    dve.wait_ge(rstd_ready, b + 1)
                    rows = h[:, bass.ds(b * TB, TB), :]
                    for j in range(TB):
                        v.mark(dve.tensor_scalar(h[:, bass.ds(b * TB + j, 1), :], g.x[:, bass.ds(b * TB + j, 1), :],
                                                 mv[:, j, 0:1], rstd[:, j:j + 1], ALU.subtract, ALU.mult))
                    v.sync()
                    v(dve.tensor_tensor(rows, rows, mod[:, bass.ds(b, 1), CA, :].to_broadcast([P, TB, D]), ALU.mult))
                    v(dve.tensor_tensor(rows, rows, mod[:, bass.ds(b, 1), SA, :].to_broadcast([P, TB, D]), ALU.add))
                    v(dve.tensor_tensor(prod[:], rows, probe[:].unsqueeze(1).to_broadcast([P, TB, D]), ALU.mult))
                    v(dve.tensor_reduce(agent[:, bass.ds(b * TB, TB)], prod[:], AX.X, ALU.add))
                    v(dve.tensor_tensor(masked[:, 0], agent[:, bass.ds(b * TB, TB)].unsqueeze(2).to_broadcast([P, TB, B]),
                                        g.eye_b[:, bass.ds(b, 1), :].to_broadcast([P, TB, B]), ALU.mult))
                    dve.tensor_scalar(masked[:, 1], masked[:, 0], float(D) ** -0.5, None, ALU.mult).then_inc(masked_ready, 1)
                    dve.wait_ge(mix_done, b + 1)
                    v(dve.tensor_tensor(mix[:], mix[:], mix_ps[0:B, 0:D], ALU.add))
                    assert v.n == per

            @block.gpsimd
            def _(pool):
                with pool.Fori(0, B) as b:
                    pool.wait_ge(var_ready, b + 1)
                    rsqrt_rows(pool, rstd, var, g.minus_half, TB, rstd_ready)

            @block.scalar
            def _(act):
                act.wait_ge(w_done, 1)
                act.activation(wkT[:], w_ps[:, 0, :].rearrange("p (k d) -> p k d", k=KD), ACT.Copy).then_inc(w_copied, 1)
                act.activation(wvT[:], w_ps[:, 1, :].rearrange("p (k d) -> p k d", k=KD), ACT.Copy).then_inc(w_copied, 1)

            @block.tensor
            def _(pe):
                for half in range(2):
                    for k in range(KD):
                        for j in range(KD):
                            last = pe.transpose(w_ps[:, half, k * D + j * P:k * D + (j + 1) * P],
                                                g.wqkv[:, 2 + 2 * half + j, k * P:(k + 1) * P], g.ident[:])
                last.then_inc(w_done, 1)
                pe.wait_ge(wb, 1)
                for k in range(KD):
                    last = pe.matmul(probe_ps[:, 0:D], wconv_b[:, k, :], g.wqkv[:, k, :], start=(k == 0), stop=(k == KD - 1))
                last.then_inc(probe_done, 1)
                with pe.Fori(0, B) as b:
                    pe.wait_ge(masked_ready, b + 1)
                    for j in range(TB):
                        last = pe.matmul(mix_ps[0:B, 0:D], masked[:, 1, j, :], h[:, bass.ds(b * TB + j, 1), :],
                                         start=(j == 0), stop=(j == TB - 1))
                    last.then_inc(mix_done, 1)

        own = mk.sem("ab_dve")
        tp_done, tp_copied, keys_done, exp_done, attn_done, attnT_done = (
            mk.sem("mixT_done"), mk.sem("mixT_copied"), mk.sem("keys_done"), mk.sem("keys_exp"), mk.sem("attn_done"),
            mk.sem("attnT_done"))
        spread_done, probe2_done = mk.sem("spread_done"), mk.sem("value_probe_done")
        score_max, row_max, peak_ready, peak_done, neg_ready, score_exp, sums_done, masked2, mix2 = (
            mk.sem("score_max"), mk.sem("row_max"), mk.sem("peak_ready"), mk.sem("peak_done"), mk.sem("neg_ready"),
            mk.sem("score_exp"), mk.sem("sums_done"), mk.sem("masked2"), mk.sem("mix2"))
        mixT2_done, spread2_done, value_done, tok_exp, tok_diff = (
            mk.sem("mixT2_done"), mk.sem("spread2_done"), mk.sem("value_done"), mk.sem("tok_exp"), mk.sem("tok_diff"))

        def spread(v, dve):
            for k in range(KD):
                v.mark(dve.tensor_copy(mixT_b[:, k], mixT[:, k, :].unsqueeze(2).to_broadcast([P, B, P])))
            v.sync()

        with nc.Block() as block:
            @block.vector
            def _(dve):
                v = Steps(dve, own)
                dve.wait_ge(tp_done, 1)
                dve.tensor_copy(mixT[:], tiny_ps[:, 0:KD * B].rearrange("p (k b) -> p k b", k=KD)).then_inc(tp_copied, 1)
                dve.wait_ge(keys_done, 1)
                v(dve.reduce_max(small[0:B, 0:1], wide_ps[0:B, 0, :], AX.X))
                v(dve.tensor_scalar(small[0:B, 1:2], small[0:B, 0:1], -1.0, None, ALU.mult))
                dve.sem_inc(attn_done, 1)
                dve.wait_ge(exp_done, 1)
                v(dve.reciprocal(small[0:B, 3:4], small[0:B, 2:3]))
                v(dve.tensor_scalar(keys[:], keys[:], small[0:B, 3:4], None, ALU.mult))
                dve.sem_inc(attn_done, 1)
                dve.wait_ge(attnT_done, 1)
                v(dve.tensor_copy(mixT[:], tiny_ps[:, 0:KD * B].rearrange("p (k b) -> p k b", k=KD)))
                spread(v, dve)
                dve.sem_inc(spread_done, 1)
                dve.wait_ge(probe2_done, 1)
                v(dve.tensor_copy(value_probe[:], wide_ps[:]))
                first = v.n
                with dve.Fori(0, B) as b:
                    v = Steps(dve, own, b * 3 + first)
                    v(dve.tensor_tensor(prod[:], h[:, bass.ds(b * TB, TB), :],
                                        value_probe[:, bass.ds(b, 1), :].to_broadcast([P, TB, D]), ALU.mult))
                    v(dve.tensor_reduce(score[:, bass.ds(b * TB, TB)], prod[:], AX.X, ALU.add))
                    v(dve.tensor_reduce(peak[:, bass.ds(b, 1)], score[:, bass.ds(b * TB, TB)], AX.X, ALU.max))
                v = Steps(dve, own, first + 3 * B)
                dve.sem_inc(score_max, 1)
                dve.wait_ge(row_max, 1)
                v(dve.reduce_max(peak_row[:], tiny_ps[0:B, 128:256], AX.X))
                v(dve.tensor_scalar(peak_diag[:], g.ident[0:B, 0:B], peak_row[:], -1.0, ALU.mult, ALU.mult))
                dve.sem_inc(peak_ready, 1)
                dve.wait_ge(peak_done, 1)
                v(dve.tensor_copy(neg_peak[:], tiny_ps[:, 256:256 + B]))
                v(dve.tensor_tensor(tok[:], agent[:], agent[:], ALU.subtract))
                dve.sem_inc(neg_ready, 1)
                dve.wait_ge(score_exp, 1)
                v(dve.tensor_reduce(part_sum[:], score[:].rearrange("p (b t) -> p b t", b=B), AX.X, ALU.add))
                for b in range(B):
                    v.mark(dve.memset(mix[:], 0.0)) if b == 0 else None
                v.sync()
                dve.sem_inc(sums_done, 1)
                first = v.n + first + 3 * B
                with dve.Fori(0, B) as b:
                    v = Steps(dve, own, b * 1 + first)
                    dve.tensor_tensor(masked[:, 0], score[:, bass.ds(b * TB, TB)].unsqueeze(2).to_broadcast([P, TB, B]),
                                      g.eye_b[:, bass.ds(b, 1), :].to_broadcast([P, TB, B]), ALU.mult).then_inc(masked2, 1)
                    dve.wait_ge(mix2, b + 1)
                    v(dve.tensor_tensor(mix[:], mix[:], mix_ps[0:B, 0:D], ALU.add))
                v = Steps(dve, own, first + B)
                dve.sem_inc(sums_done, 1)
                dve.wait_ge(mixT2_done, 1)
                v(dve.tensor_copy(mixT[:], tiny_ps[:, 0:KD * B].rearrange("p (k b) -> p k b", k=KD)))
                v(dve.reciprocal(inv_sum[:], tiny_ps[:, 260:260 + B]))
                spread(v, dve)
                dve.sem_inc(spread2_done, 1)
                dve.wait_ge(tok_exp, 1)
                v(dve.reciprocal(score[:], tok[:]))
                v(dve.tensor_tensor(tok[:], tok[:], score[:], ALU.mult))
                dve.wait_ge(value_done, 1)
                for b in range(B):
                    v.mark(dve.scalar_tensor_tensor(gated[:, b, :], wide_ps[:, b, :], inv_sum[:, b:b + 1],
                                                    mod[:, b, GA, :], ALU.mult, ALU.mult))
                v.sync()
                with dve.Fori(0, B) as b:
                    for j in range(TB):
                        rows = g.x[:, bass.ds(b * TB + j, 1), :]
                        dve.scalar_tensor_tensor(rows, gated[:, bass.ds(b, 1), :], tok[:, bass.ds(b * TB + j, 1)], rows,
                                                 ALU.mult, ALU.add)

            @block.scalar
            def _(act):
                act.wait_ge(attn_done, 1)
                act.activation(keys[:], wide_ps[0:B, 0, :], ACT.Exp, bias=small[0:B, 1:2],
                               accum_out=small[0:B, 2:3]).then_inc(exp_done, 1)
                act.wait_ge(neg_ready, 1)
                for b in range(B):
                    last = act.activation(score[:, b * TB:(b + 1) * TB], score[:, b * TB:(b + 1) * TB], ACT.Exp,
                                          bias=neg_peak[:, b:b + 1])
                last.then_inc(score_exp, 1)
                act.activation(tok[:], tok[:], ACT.Exp).then_inc(tok_exp, 1)

            @block.tensor
            def _(pe):
                def mixT_of(rows, done):
                    for k in range(KD):
                        last = pe.transpose(tiny_ps[:, k * B:(k + 1) * B], rows[:, k * P:(k + 1) * P], g.ident[0:B, 0:B])
                    last.then_inc(done, 1)

                mixT_of(mix, tp_done)
                pe.wait_ge(tp_copied, 1)
                for k in range(KD):
                    last = pe.matmul(wide_ps[0:B, 0, :], mixT[:, k, :], wkT[:, k, :], start=(k == 0), stop=(k == KD - 1))
                last.then_inc(keys_done, 1)
                pe.wait_ge(attn_done, 2)
                mixT_of(keys, attnT_done)
                pe.wait_ge(spread_done, 1)
                for b in range(B):
                    for k in range(KD):
                        last = pe.matmul(wide_ps[:, b, :], mixT_b[:, k, b, :], g.wqkv[:, 4 + k, :],
                                         start=(k == 0), stop=(k == KD - 1))
                last.then_inc(probe2_done, 1)
                pe.wait_ge(score_max, 1)
                pe.transpose(tiny_ps[0:B, 128:256], peak[:], g.ident[:]).then_inc(row_max, 1)
                pe.wait_ge(peak_ready, 1)
                pe.matmul(tiny_ps[:, 256:256 + B], g.ones[0:B, :], peak_diag[:], start=True, stop=True).then_inc(peak_done, 1)
                pe.wait_ge(neg_ready, 1)
                pe.wait_ge(sums_done, 1)
                pe.matmul(tiny_ps[:, 260:260 + B], g.ones[:], part_sum[:], start=True, stop=True)
                with pe.Fori(0, B) as b:
                    pe.wait_ge(masked2, b + 1)
                    for j in range(TB):
                        last = pe.matmul(mix_ps[0:B, 0:D], masked[:, 0, j, :], h[:, bass.ds(b * TB + j, 1), :],
                                         start=(j == 0), stop=(j == TB - 1))
                    last.then_inc(mix2, 1)
                pe.wait_ge(sums_done, 2)
                mixT_of(mix, mixT2_done)
                pe.wait_ge(spread2_done, 1)
                for b in range(B):
                    for k in range(KD):
                        last = pe.matmul(wide_ps[:, b, :], mixT_b[:, k, b, :], wvT[:, k, :],
                                         start=(k == 0), stop=(k == KD - 1))
                last.then_inc(value_done, 1)


RING = 8
TOP = 8


def expert_choice(nc, mk, g, a):
    HALF = T // 2
    LOW = 64
    ROWS = LOW + E
    with ExitStack() as ctx:
        t = Maker(nc, ctx)
        w1 = t.sb("w1", [P, RING, S, KD, M])
        w2 = t.sb("w2", [P, RING, S, KD, KS])
        b2_row = t.sb("b2_row", [1, RING, D])
        b1T = t.sb("b1T", [P, E * S, KD])
        index = t.sb("index", [P, E], U32)
        weight = t.sb("weight", [P, E])
        h_dram = nc.dram_tensor("h_dram", (T, D), F32, kind="Internal").ap()
        sum_dram = nc.dram_tensor("sum_dram", (T, D), F32, kind="Internal").ap()
        w_in = [mk.sem(f"w_in{q}") for q in range(RING)]
        mod = g.modb[:].rearrange("p b (s d) -> p b s d", s=6)

        def load_expert(eng, e, q):
            eng.dma_start(w1[:, q], a["L0_ffn_W1"][bass.ds(e, 1)].rearrange("a s (p k) m -> p (a s) k m", k=KD)).then_inc(w_in[q], 16)
            eng.dma_start(w2[:, q], a["L0_ffn_W2"][bass.ds(e, 1)].rearrange("a s (p k) n -> p (a s) k n", k=KD)).then_inc(w_in[q], 16)
            eng.dma_start(b2_row[:, q, :], a["L0_ffn_b2"][bass.ds(e, 1)].rearrange("a s n -> a (s n)")).then_inc(w_in[q], 16)

        with ExitStack() as c2:
            r = Maker(nc, c2)
            logits = r.sb("logits", [ROWS, HALF])
            with ExitStack() as c3:
                t = Maker(nc, c3)
                hg = t.sb("hg", [P, 2, G, D])
                hT = t.sb("hT", [P, 2, KD, GT])
                wr = t.sb("wr", [E, D])
                wrT = t.sb("wrT", [P, KD, E])
                b1_rows = t.sb("b1_rows", [2 * E, 2, M])
                zero = t.sb("zero", [P, 2048])
                st, mv, var, rstd = (t.sb("st1", [P, G, 6]), t.sb("mv1", [P, G, 2]), t.sb("var1", [P, G]),
                                     t.sb("rstd1", [P, G]))
                tp = t.ps("tp1", [P, 2, KD, GT])
                lp = t.ps("lp1", [P, 2, GT])
                own, var_ready, rstd_ready, h_ready = (mk.sem("ec_dve"), mk.sem("ec_var"), mk.sem("ec_rstd"),
                                                       mk.sem("ec_h"))
                turned, hT_ready, logits_done, logits_out = (mk.sem("ec_turned"), mk.sem("ec_hT"), mk.sem("ec_logits"),
                                                             mk.sem("ec_logits_out"))
                h_out = [mk.sem("ec_h_out0"), mk.sem("ec_h_out1")]
                small_in, zeroed, zero_out, wrT_done, wrT_copied = (mk.sem("ec_small_in"), mk.sem("ec_zeroed"),
                                                                    mk.sem("ec_zero_out"), mk.sem("ec_wrT"),
                                                                    mk.sem("ec_wrT_copied"))
                with nc.Block() as block:
                    @block.sync
                    def _(sp):
                        with sp.Fori(0, B) as b:
                            for k in range(2):
                                sp.wait_ge(h_ready, 2 * b + k + 1)
                                sp.dma_start(h_dram[bass.ds((2 * b + k) * GT, GT), :].rearrange("(t p) d -> p t d", p=P),
                                             hg[:, k]).then_inc(h_out[k], 16)
                        for k in range(2):
                            sp.wait_ge(h_out[k], 16 * (B + 1))

                    @block.scalar
                    def _(act):
                        act.dma_start(wr[:], a["L0_ffn_Wr"]).then_inc(small_in, 16)
                        act.dma_start(b1_rows[:], a["L0_ffn_b1"].rearrange("e s m -> (e s) m").rearrange("(i r) m -> r i m", i=2)).then_inc(small_in, 16)
                        act.wait_ge(zeroed, 2)
                        for i in range(4):
                            act.dma_start(sum_dram.rearrange("(i p r) d -> i p (r d)", i=4, p=P)[i], zero[:]).then_inc(zero_out, 16)
                        for e in range(RING):
                            load_expert(act, e, e)
                        act.wait_ge(wrT_done, 1)
                        act.activation(wrT[:], lp[:, 0, 0:KD * E].rearrange("p (k e) -> p k e", k=KD), ACT.Copy).then_inc(wrT_copied, 1)
                        act.activation(b1T[:].rearrange("p (i r) k -> p k i r", i=2),
                                       tp[:, 1, 0, 0:2 * 2 * 2 * E].rearrange("p (k i r) -> p k i r", k=KD, i=2),
                                       ACT.Copy).then_inc(wrT_copied, 1)
                        for half in range(2):
                            with act.Fori(0, B // 2) as i:
                                for k in range(2):
                                    n = 2 * i + k + half * NG // 2
                                    act.wait_ge(turned, n + 1 + 2)
                                    act.activation(hT[:, k], tp[:, k], ACT.Copy).then_inc(hT_ready, 1)
                                    act.wait_ge(logits_done, n + 1)
                                    rows = slice(LOW * half, LOW * half + E)
                                    act.activation(logits[rows, bass.ds((2 * i + k) * GT, GT)], lp[rows, k, :],
                                                   ACT.Copy).then_inc(logits_out, 1)
                        act.wait_ge(zero_out, 64)

                    @block.gpsimd
                    def _(pool):
                        pool.memset(zero[:], 0.0).then_inc(zeroed, 1)
                        with pool.Fori(0, NG) as n:
                            pool.wait_ge(var_ready, n + 1)
                            rsqrt_rows(pool, rstd, var, g.minus_half, G, rstd_ready)

                    @block.vector
                    def _(dve):
                        dve.memset(logits[32:64, :], LOWEST).then_inc(zeroed, 1)
                        dve.sem_inc(turned, 2)
                        dve.sem_inc(h_out[0], 16)
                        dve.sem_inc(h_out[1], 16)
                        per = 3 * G + 1
                        with dve.Fori(0, B) as b:
                            for k in range(2):
                                v = Steps(dve, own, (2 * b + k) * per)
                                tile = lambda j: g.x[:, bass.ds(b * TB + k * G + j, 1), :]
                                layer_norm_stats(v, g.spare, st, mv, var, G, tile, LN_EPS, var_ready)
                                dve.wait_ge(rstd_ready, 2 * b + k + 1)
                                dve.wait_ge(h_out[k], 16 * (b + 1))
                                dve.wait_ge(turned, 2 * b + k + 1)
                                for j in range(G):
                                    v.mark(dve.tensor_scalar(hg[:, k, j:j + 1, :], tile(j), mv[:, j, 0:1], rstd[:, j:j + 1],
                                                             ALU.subtract, ALU.mult))
                                v.sync()
                                v(dve.tensor_tensor(hg[:, k], hg[:, k], mod[:, bass.ds(b, 1), CB, :].to_broadcast([P, G, D]), ALU.mult))
                                dve.tensor_tensor(hg[:, k], hg[:, k], mod[:, bass.ds(b, 1), SB, :].to_broadcast([P, G, D]),
                                                  ALU.add).then_inc(h_ready, 1)
                                assert v.n == per

                    @block.tensor
                    def _(pe):
                        pe.wait_ge(small_in, 32)
                        for k in range(KD):
                            pe.transpose(lp[:, 0, k * E:(k + 1) * E], wr[:, k * P:(k + 1) * P], g.ident[0:E, 0:E])
                            for i in range(2):
                                last = pe.transpose(tp[:, 1, 0, (2 * k + i) * 2 * E:(2 * k + i + 1) * 2 * E],
                                                    b1_rows[:, i, k::KD], g.ident[0:2 * E, 0:2 * E])
                        last.then_inc(wrT_done, 1)
                        pe.wait_ge(wrT_copied, 2)
                        for half in range(2):
                            with pe.Fori(0, B // 2) as i:
                                for k in range(2):
                                    n = 2 * i + k + half * NG // 2
                                    pe.wait_ge(h_ready, n + 1)
                                    for j in range(G):
                                        for c in range(KD):
                                            last = pe.transpose(tp[:, k, c, j * P:(j + 1) * P], hg[:, k, j, c * P:(c + 1) * P],
                                                                g.ident[:])
                                    last.then_inc(turned, 1)
                                    pe.wait_ge(hT_ready, n + 1)
                                    for c in range(KD):
                                        last = pe.matmul(lp[LOW * half:LOW * half + E, k, :], wrT[:, c, :], hT[:, k, c, :],
                                                         start=(c == 0), stop=(c == KD - 1))
                                    last.then_inc(logits_done, 1)

            with ExitStack() as c3:
                t = Maker(nc, c3)
                top = t.sb("top", [ROWS, CAP])
                at = t.sb("at", [ROWS, CAP], U32)
                at_f = t.sb("at_f", [ROWS, CAP])
                both = t.sb("both", [P, 2, ROWS])
                rank0 = t.sb("rank0", [P, P])
                low = t.sb("low", [P, 2, E])
                take, best, chosen = t.sb("take", [P, E]), t.sb("best", [P, E]), t.sb("chosen", [P, E])
                rank_ps, low_ps, peak_ps, sum_ps = (t.ps("rank_ps", [P, 512]), t.ps("low_ps", [P, 512]),
                                                    t.ps("peak_ps", [P, 512]), t.ps("sum_ps", [P, 512]))
                own, found, ranked, copied, lowered, expd, expd_done, summed, row0 = (
                    mk.sem("top_dve"), mk.sem("top_found"), mk.sem("top_ranked"), mk.sem("top_copied"), mk.sem("top_lowered"),
                    mk.sem("top_shifted"), mk.sem("top_exp"), mk.sem("top_sum"), mk.sem("top_rank0"))
                with nc.Block() as block:
                    @block.gpsimd
                    def _(pool):
                        pool.memset(rank0[:], 0.0).then_inc(row0, 1)
                        pool.wait_ge(row0, 1)
                        pool.memset(rank0[0:1, :], 1.0).then_inc(row0, 1)

                    @block.vector
                    def _(dve):
                        v = Steps(dve, own)
                        for n in range(CAP // TOP):
                            cols = slice(n * TOP, (n + 1) * TOP)
                            v(dve.max(top[:, cols], logits[:]))
                            v(dve.max_index(at[:, cols], top[:, cols], logits[:]))
                            if n < CAP // TOP - 1:
                                v(dve.match_replace(logits[:], top[:, cols], logits[:], LOWEST))
                        v(dve.tensor_copy(at_f[:], at[:]))
                        v(dve.tensor_scalar(at_f[LOW:ROWS, :], at_f[LOW:ROWS, :], float(HALF), None, ALU.add))
                        dve.sem_inc(found, 1)
                        dve.wait_ge(ranked, 1)
                        v(dve.tensor_copy(both[:], rank_ps[:, 0:2 * ROWS].rearrange("p (i r) -> p i r", i=2)))
                        dve.sem_inc(copied, 1)
                        dve.wait_ge(lowered, 1)
                        v(dve.tensor_copy(low[:], low_ps[:, 0:2 * E].rearrange("p (i e) -> p i e", i=2)))
                        v(dve.tensor_tensor(take[:], both[:, 0, 0:E], low[:, 0, :], ALU.is_ge))
                        v(dve.tensor_tensor(best[:], both[:, 0, 0:E], low[:, 0, :], ALU.max))
                        v(dve.tensor_tensor(chosen[:], both[:, 1, 0:E], low[:, 1, :], ALU.subtract))
                        v(dve.tensor_tensor(chosen[:], chosen[:], take[:], ALU.mult))
                        v(dve.tensor_tensor(chosen[:], chosen[:], low[:, 1, :], ALU.add))
                        v(dve.tensor_copy(index[:], chosen[:]))
                        v(dve.tensor_copy(take[:], peak_ps[:, 0:E]))
                        v(dve.tensor_tensor(take[:], take[:], peak_ps[:, E:2 * E], ALU.max))
                        v(dve.tensor_tensor(best[:], best[:], take[:], ALU.subtract))
                        dve.sem_inc(expd, 1)
                        dve.wait_ge(summed, 1)
                        v(dve.reciprocal(take[:], sum_ps[:, 0:E]))
                        v(dve.tensor_tensor(weight[:], best[:], take[:], ALU.mult))

                    @block.scalar
                    def _(act):
                        act.wait_ge(expd, 1)
                        act.activation(best[:], best[:], ACT.Exp).then_inc(expd_done, 1)

                    @block.tensor
                    def _(pe):
                        pe.wait_ge(found, 1)
                        pe.transpose(rank_ps[:, 0:ROWS], top[:], g.ident[0:ROWS, 0:ROWS])
                        pe.transpose(rank_ps[:, ROWS:2 * ROWS], at_f[:], g.ident[0:ROWS, 0:ROWS]).then_inc(ranked, 1)
                        pe.wait_ge(copied, 1)
                        pe.wait_ge(row0, 2)
                        pe.matmul(peak_ps[:, 0:E], rank0[:], both[:, 0, 0:E], start=True, stop=True)
                        pe.matmul(peak_ps[:, E:2 * E], rank0[:], both[:, 0, LOW:ROWS], start=True, stop=True)
                        pe.matmul(low_ps[:, 0:E], g.flip[:], both[:, 0, LOW:ROWS], start=True, stop=True)
                        pe.matmul(low_ps[:, E:2 * E], g.flip[:], both[:, 1, LOW:ROWS], start=True, stop=True).then_inc(lowered, 1)
                        pe.wait_ge(expd_done, 1)
                        pe.matmul(sum_ps[:, 0:E], g.ones[:], best[:], start=True, stop=True).then_inc(summed, 1)

        with ExitStack() as c2:
            t = Maker(nc, c2)
            XG = 4
            slot = t.sb("slot", [P, XG, 1], U32)
            xg = t.sb("xg", [P, XG, D])
            xT = t.sb("xT", [P, 2, KD, P])
            pre = t.sb("pre", [P, 2, S * KD, P])
            act_h = t.sb("act_h", [P, 2, S * KD, P])
            y = t.sb("y", [P, 2, D])
            x_ps = t.ps("x_ps", [P, 2, 512])
            h_ps = t.ps("h_ps", [P, 2, S * KD, P])
            y_ps = t.ps("y_ps", [P, 2, 512])
            xg_in = [mk.sem(f"xg_in{q}") for q in range(XG)]
            slot_set, turned, xT_ready, up_done, biased, gelu_done, down_done, y_ready, added = (
                mk.sem("slot_set"), mk.sem("xg_turned"), mk.sem("xT_ready"), mk.sem("up_done"), mk.sem("biased"),
                mk.sem("gelu_done"), mk.sem("down_done"), mk.sem("y_ready"), mk.sem("added"))
            carried, y_free = mk.sem("pool_carried"), mk.sem("y_free")
            LAST = E // RING - 1

            def bodies(eng, body):
                with eng.Fori(0, LAST) as i:
                    for q in range(RING):
                        body(i * RING + q, q, False)
                for q in range(RING):
                    body(LAST * RING + q, q, True)

            with nc.Block() as block:
                @block.sync
                def _(sp):
                    with sp.Fori(0, LAST) as i:
                        for q in range(RING):
                            e = i * RING + q
                            sp.wait_ge(down_done, e + 1)
                            load_expert(sp, e + RING, q)

                @block.gpsimd
                def _(pool):
                    def carry_wait(n):
                        pool.wait_ge(carried, n + 1)
                        pool.tensor_tensor(g.pool_spare[:], g.minus_half[:, 0:1], g.minus_half[:, 0:1],
                                           ALU.add).then_inc(carried, 1)

                    def gather(e, q, n):
                        pool.tensor_copy(slot[:, q], index[:, bass.ds(e, 1)]).then_inc(slot_set, 1)
                        pool.wait_ge(slot_set, e + 1)
                        carry_wait(n)
                        pool.indirect_dma_start(out=xg[:, q, :], out_offset=None, in_=h_dram,
                                                in_offset=bass.IndirectOffsetOnAxis(ap=slot[:, q], axis=0)).then_inc(xg_in[q], 16)

                    pool.sem_inc(carried, 1)
                    pool.sem_inc(y_free, 2)
                    pool.sem_inc(turned, 1)
                    for e in range(XG - 1):
                        gather(e, e, e)

                    def body(e, q, last):
                        if not last or q + XG - 1 < RING:
                            pool.wait_ge(turned, e + 1)
                            gather(e + XG - 1, (q + XG - 1) % XG, XG - 1 + 2 * e)
                        pool.wait_ge(y_ready, e + 1)
                        carry_wait(XG + 2 * e - max(0, q + XG - RING) if last else XG + 2 * e)
                        pool.indirect_dma_start(out=sum_dram, out_offset=bass.IndirectOffsetOnAxis(ap=slot[:, q % XG], axis=0),
                                                in_=y[:, q % 2, :], in_offset=None, compute_op=ALU.add).then_inc(added, 16)
                        pool.wait_ge(added, 16 * (e + 1))
                        pool.sem_inc(y_free, 1)

                    bodies(pool, body)
                    pool.wait_ge(added, 16 * E)

                @block.scalar
                def _(act):
                    def x_copy(e, q):
                        act.wait_ge(turned, e + 2)
                        act.activation(xT[:, q % 2], x_ps[:, q % 2, 0:D].rearrange("p (k n) -> p k n", k=KD), ACT.Copy).then_inc(xT_ready, 1)

                    x_copy(0, 0)

                    def body(e, q, last):
                        if not last or q + 1 < RING:
                            x_copy(e + 1, q + 1)
                        act.wait_ge(biased, e + 1)
                        act.activation(act_h[:, q % 2], pre[:, q % 2], ACT.Gelu).then_inc(gelu_done, 1)

                    bodies(act, body)

                @block.vector
                def _(dve):
                    def bias(e, q):
                        dve.wait_ge(up_done, e + 1)
                        dve.tensor_tensor(pre[:, q % 2], h_ps[:, q % 2],
                                          b1T[:, bass.ds(e * S, S), :].rearrange("p s k -> p (s k)").unsqueeze(2)
                                          .to_broadcast([P, S * KD, P]), ALU.add).then_inc(biased, 1)

                    bias(0, 0)

                    def body(e, q, last):
                        if not last or q + 1 < RING:
                            bias(e + 1, q + 1)
                        dve.wait_ge(down_done, e + 1)
                        dve.wait_ge(y_free, e + 1)
                        dve.tensor_scalar(y[:, q % 2, :], y_ps[:, q % 2, 0:D], weight[:, bass.ds(e, 1)], None,
                                          ALU.mult).then_inc(y_ready, 1)

                    bodies(dve, body)

                @block.tensor
                def _(pe):
                    def turn(e, q):
                        pe.wait_ge(xg_in[q % XG], 16 * (q // XG + 1) + (e - q) * (16 // XG))
                        for k in range(KD):
                            last = pe.transpose(x_ps[:, q % 2, k * P:(k + 1) * P], xg[:, q % XG, k::KD], g.ident[:])
                        last.then_inc(turned, 1)

                    def up(e, q):
                        pe.wait_ge(w_in[q], 48 + (e - q) * (48 // RING))
                        pe.wait_ge(xT_ready, e + 1)
                        for s in range(S):
                            for c in range(KD):
                                for k in range(KD):
                                    last = pe.matmul(h_ps[:, q % 2, s * KD + c, :], w1[:, q, s, k, c::KD], xT[:, q % 2, k, :],
                                                     start=(k == 0), stop=(k == KD - 1))
                        last.then_inc(up_done, 1)

                    def down(e, q):
                        pe.wait_ge(gelu_done, e + 1)
                        for s in range(S):
                            cols = slice(s * KS, (s + 1) * KS)
                            for c in range(KD):
                                pe.matmul(y_ps[:, q % 2, cols], act_h[:, q % 2, s * KD + c, :], w2[:, q, s, c, :],
                                          start=(c == 0), stop=False)
                            last = pe.matmul(y_ps[:, q % 2, cols], g.ones[0:1, :], b2_row[:, q, cols], start=False, stop=True)
                        last.then_inc(down_done, 1)

                    turn(0, 0)
                    up(0, 0)
                    turn(1, 1)

                    def body(e, q, last):
                        if not last or q + 1 < RING:
                            up(e + 1, (q + 1) % RING)
                        if not last or q + 2 < RING:
                            turn(e + 2, (q + 2) % RING)
                        down(e, q)

                    bodies(pe, body)

        with ExitStack() as c2:
            t = Maker(nc, c2)
            part = t.sb("part", [P, 2, G, D])
            part_in = [mk.sem("part_in0"), mk.sem("part_in1")]
            used, own = mk.sem("part_used"), mk.sem("part_dve")
            with nc.Block() as block:
                @block.sync
                def _(sp):
                    sp.sem_inc(used, 2)
                    with sp.Fori(0, B) as b:
                        for k in range(2):
                            sp.wait_ge(used, 2 * b + k + 1)
                            sp.dma_start(part[:, k], sum_dram[bass.ds((2 * b + k) * GT, GT), :]
                                         .rearrange("(t p) d -> p t d", p=P)).then_inc(part_in[k], 16)

                @block.vector
                def _(dve):
                    with dve.Fori(0, B) as b:
                        for k in range(2):
                            v = Steps(dve, own, 2 * b + k)
                            dve.wait_ge(part_in[k], 16 * (b + 1))
                            v(dve.tensor_tensor(part[:, k], part[:, k], mod[:, bass.ds(b, 1), GB, :].to_broadcast([P, G, D]), ALU.mult))
                            rows = g.x[:, bass.ds(b * TB + k * G, G), :]
                            dve.tensor_tensor(rows, rows, part[:, k], ALU.add).then_inc(used, 1)
        mk.clear_signals()


def project_heads(pe, ring, rows, wide, ident, w, full, free, uses):
    def take(n):
        pe.wait_ge(free, uses + n + 1)

    for c in range(KD):
        take(c)
        for j in range(G):
            last = pe.transpose(ring[:, c, j * P:(j + 1) * P], rows[:, j, c * P:(c + 1) * P], ident)
        last.then_inc(full, 1)
    pe.wait_ge(free, uses + KD + 2)
    for c in range(CH):
        take(KD + c)
        for k in range(KD):
            last = pe.matmul(ring[:, c % 2, :], w[:, k, c * P:(c + 1) * P], wide[:, k, :], start=(k == 0), stop=(k == KD - 1))
        last.then_inc(full, 1)


def copy_heads(act, ring, turned, scaled, squares, full, free, uses):
    for c in range(KD):
        act.wait_ge(full, uses + c + 1)
        act.activation(turned[:, c, :], ring[:, c, :], ACT.Copy).then_inc(free, 1)
    for c in range(CH):
        act.wait_ge(full, uses + KD + c + 1)
        act.activation(scaled[:, c, :], ring[:, c % 2, :], ACT.Copy, scale=DN)
        act.activation(squares[:, c, :], ring[:, c % 2, :], ACT.Square, scale=DN).then_inc(free, 1)


def random_features(pe, dash, diag, scaled, squares, j, features, half_heads):
    for c in range(CH):
        pe.matmul(dash[:, c * P:(c + 1) * P], scaled[:, c, j * P:(j + 1) * P], features, start=True, stop=True)
    for c in range(CH):
        last = pe.matmul(diag[:, 2 * c:2 * c + 2], squares[:, c, j * P:(j + 1) * P], half_heads, start=True, stop=True)
    return last


def performer(nc, mk, g, a):
    USES = KD + CH
    with ExitStack() as ctx:
        t = Maker(nc, ctx)
        h_dram = nc.dram_tensor("h1_dram", (T, D), F32, kind="Internal").ap()
        y_dram = nc.dram_tensor("y1_dram", (T, D), F32, kind="Internal").ap()
        kv_out = t.sb("kv_out", [P, B, CH, D])
        wide = t.sb("wide", [P, TB, HD])
        k_dash, ksum, q_dash, qn = wide, wide[:, 0:B, :], wide[:, B:B + 2, :], wide[:, B + 2:B + 4, :]
        features = t.sb("features", [P, P])
        half_heads = t.sb("half_heads", [P, 2])
        mod = g.modb[:].rearrange("p b (s d) -> p b s d", s=6)
        wide_in = mk.sem("pf_weights_in")

        with ExitStack() as c1:
            r = Maker(nc, c1)
            wo, wv = r.sb("wo", [P, CH, D]), r.sb("wv", [P, KD, HD])
            a_sum = kv_out
            k_sum = r.sb("k_sum", [P, B, CH])
            h_sum = r.sb("h_sum", [P, B, D + 1])
            peak = r.sb("key_peak", [P, B])
            with ExitStack() as c2:
                t = Maker(nc, c2)
                hk = t.sb("hk", [P, 2, G, D + 1])
                hT = t.sb("hkT", [P, KD, GT])
                kT, k2 = t.sb("kT", [P, CH, GT]), t.sb("k2", [P, CH, GT])
                dash = k_dash
                wk = t.sb("wk", [P, KD, HD])
                proj2 = t.sb("proj2", [MF, 2, DH])
                half_diag = t.sb("k_half_diag", [P, 2, H])
                row_peak, tile_peak, neg_peak = t.sb("row_peak", [P, TB]), t.sb("tile_peak", [P, 1]), t.sb("neg_peak1", [P, 1])
                st, mv, var, rstd = (t.sb("st2", [P, G, 6]), t.sb("mv2", [P, G, 2]), t.sb("var2", [P, G]),
                                     t.sb("rstd2", [P, G]))
                ring = t.ps("k_ring", [P, 2, 512])
                dash_ps = t.ps("k_dash_ps", [P, 2, HD])
                diag_ps = t.ps("k_diag_ps", [P, 512])
                h_sum_ps = t.ps("h_sum_ps", [P, 512])
                own, var_ready, rstd_ready, h_ready = mk.sem("pk_dve"), mk.sem("pk_var"), mk.sem("pk_rstd"), mk.sem("pk_h")
                full, free, dash_done, dash_used, diag_copied = (mk.sem("k_full"), mk.sem("k_free"), mk.sem("k_dash_done"),
                                                                 mk.sem("k_dash_used"), mk.sem("k_diag_copied"))
                h_out = [mk.sem("h1_out0"), mk.sem("h1_out1")]
                mod_in, wk_in, proj_done, const_done = mk.sem("mod1_in"), mk.sem("wk_in"), mk.sem("proj_turned"), mk.sem("pk_const")
                carried = mk.sem("pk_carried")
                peak_part, peak_all, neg_ready, exp_done, h_sum_done = (
                    mk.sem("peak_part"), mk.sem("peak_all"), mk.sem("neg_peak_ready"), mk.sem("k_exp"), mk.sem("h_sum_done"))
                PER = 2 * USES + CH
                with nc.Block() as block:
                    @block.sync
                    def _(sp):
                        sp.dma_start(g.modb[:], g.mod_dram[1].partition_broadcast(P)).then_inc(mod_in, 16)
                        for k in range(2):
                            sp.dma_start(proj2[:, k, :], a["L1_attn_proj"]).then_inc(wk_in, 16)
                        for dst, name in ((wk, "Wk"), (wv, "Wv")):
                            sp.dma_start(dst[:], a[f"L1_attn_{name}"].rearrange("(k p) h d -> p k (h d)", p=P)
                                         ).then_inc(wk_in if name == "Wk" else wide_in, 16)
                        sp.dma_start(wo[:], a["L1_attn_Wo"].rearrange("h d o -> (h d) o").rearrange("(c p) o -> p c o", p=P)).then_inc(wide_in, 16)
                        with sp.Fori(0, B) as b:
                            for k in range(2):
                                sp.wait_ge(h_ready, 2 * b + k + 1)
                                sp.dma_start(h_dram[bass.ds((2 * b + k) * GT, GT), :].rearrange("(t p) d -> p t d", p=P),
                                             hk[:, k, :, 0:D]).then_inc(h_out[k], 16)
                        for k in range(2):
                            sp.wait_ge(h_out[k], 16 * (B + 1))
                        sp.wait_ge(wide_in, 32)

                    @block.gpsimd
                    def _(pool):
                        pool.sem_inc(carried, 1)
                        with pool.Fori(0, B) as b:
                            for k in range(2):
                                pool.wait_ge(var_ready, 2 * b + k + 1)
                                rsqrt_rows(pool, rstd, var, g.minus_half, G, rstd_ready)
                            pool.wait_ge(carried, b + 1)
                            pool.wait_ge(peak_part, b + 1)
                            pool.tensor_tensor(g.pool_spare[:], tile_peak[:], tile_peak[:], ALU.add).then_inc(carried, 1)
                            pool.partition_all_reduce(g.pool_max[:], tile_peak[:], P, bass.bass_isa.ReduceOp.max).then_inc(peak_all, 1)

                    @block.vector
                    def _(dve):
                        v = Steps(dve, own)
                        dve.sem_inc(h_sum_done, 1)
                        dve.sem_inc(dash_used, 2)
                        for k in range(2):
                            dve.sem_inc(h_out[k], 16)
                        v.mark(dve.memset(features[:], 0.0))
                        v.mark(dve.memset(half_heads[:], 0.0))
                        v.mark(dve.memset(hk[:].rearrange("p i t d -> p (i t) d")[:, :, D:D + 1], 1.0))
                        v.sync()
                        v.mark(dve.memset(half_heads[0:DH, 0:1], 0.5))
                        v.mark(dve.memset(half_heads[DH:P, 1:2], 0.5))
                        dve.wait_ge(proj_done, 1)
                        for i in range(2):
                            at = slice(i * DH, (i + 1) * DH)
                            v.mark(dve.tensor_copy(features[at, i * MF:(i + 1) * MF], ring[at, 0, 0:MF]))
                        v.sync()
                        dve.sem_inc(const_done, 1)
                        dve.wait_ge(mod_in, 16)
                        first = v.n
                        ln = 3 * G + 1
                        per = 2 * ln + 2 * TB + 2
                        with dve.Fori(0, B) as b:
                            v = Steps(dve, own, b * per + first)
                            for k in range(2):
                                tile = lambda j: g.x[:, bass.ds(b * TB + k * G + j, 1), :]
                                layer_norm_stats(v, g.spare, st, mv, var, G, tile, LN_EPS, var_ready)
                                dve.wait_ge(rstd_ready, 2 * b + k + 1)
                                dve.wait_ge(h_out[k], 16 * (b + 1))
                                dve.wait_ge(h_sum_done, b + 1)
                                for j in range(G):
                                    v.mark(dve.tensor_scalar(hk[:, k, j:j + 1, 0:D], tile(j), mv[:, j, 0:1], rstd[:, j:j + 1],
                                                             ALU.subtract, ALU.mult))
                                v.sync()
                                rows = hk[:, k, :, 0:D]
                                v(dve.tensor_tensor(rows, rows, mod[:, bass.ds(b, 1), CA, :].to_broadcast([P, G, D]), ALU.mult))
                                dve.tensor_tensor(rows, rows, mod[:, bass.ds(b, 1), SA, :].to_broadcast([P, G, D]),
                                                  ALU.add).then_inc(h_ready, 1)
                            for j in range(TB):
                                n = b * TB + j
                                dve.wait_ge(diag_copied, n + 2)
                                v.mark(dve.reduce_max(row_peak[:, j:j + 1], dash_ps[:, j % 2, :], AX.X))
                                v.mark(dve.tensor_tensor(dash[:, j, :].rearrange("p (h m) -> p h m", h=H),
                                                         dash_ps[:, j % 2, :].rearrange("p (h m) -> p h m", h=H),
                                                         half_diag[:, j % 2, :].unsqueeze(2).to_broadcast([P, H, MF]), ALU.subtract))
                                v.sync()
                                dve.sem_inc(dash_used, 1)
                            v(dve.reduce_max(tile_peak[:], row_peak[:], AX.X))
                            dve.sem_inc(peak_part, 1)
                            dve.wait_ge(peak_all, b + 1)
                            v.mark(dve.tensor_copy(peak[:, bass.ds(b, 1)], g.pool_max[:]))
                            dve.tensor_scalar(neg_peak[:], g.pool_max[:], -1.0, None, ALU.mult).then_inc(neg_ready, 1)
                            assert v.n == per, (v.n, per)

                    @block.scalar
                    def _(act):
                        act.sem_inc(free, 2)
                        act.sem_inc(diag_copied, 1)
                        with act.Fori(0, B) as b:
                            for k in range(2):
                                if k == 0:
                                    act.wait_ge(dash_done, b * TB + 1)
                                else:
                                    act.wait_ge(dash_done, b * TB + G + 1)
                                copy_heads(act, ring, hT, kT, k2, full, free, b * PER + k * USES)
                                for j in range(k * G, k * G + G):
                                    act.wait_ge(dash_done, b * TB + j + 2)
                                    act.activation(half_diag[:, j % 2, :], diag_ps[:, 0:H], ACT.Copy).then_inc(diag_copied, 1)
                            act.wait_ge(neg_ready, b + 1)
                            for j in range(TB):
                                last = act.activation(dash[:, j, :], dash[:, j, :], ACT.Exp, bias=neg_peak[:])
                            last.then_inc(exp_done, 1)
                            for c in range(CH):
                                act.wait_ge(full, b * PER + 2 * USES + c + 1)
                                act.activation(a_sum[:, bass.ds(b, 1), c, :], ring[:, c % 2, 0:D], ACT.Copy)
                                act.activation(k_sum[:, bass.ds(b, 1), c:c + 1], ring[:, c % 2, D:D + 1], ACT.Copy).then_inc(free, 1)
                            act.wait_ge(h_sum_done, b + 2)
                            act.activation(h_sum[:, bass.ds(b, 1), :], h_sum_ps[:, 0:D + 1], ACT.Copy)

                    @block.tensor
                    def _(pe):
                        pe.sem_inc(dash_done, 1)
                        pe.wait_ge(wk_in, 48)
                        pe.transpose(ring[:, 0, 0:MF], proj2[:].rearrange("m i d -> m (i d)"), g.ident[0:MF, 0:MF]).then_inc(proj_done, 1)
                        pe.wait_ge(const_done, 1)
                        with pe.Fori(0, B) as b:
                            for k in range(2):
                                pe.wait_ge(h_ready, 2 * b + k + 1)
                                project_heads(pe, ring, hk[:, k], hT, g.ident[:], wk, full, free, b * PER + k * USES)
                                pe.wait_ge(free, b * PER + (k + 1) * USES + 2)
                                for j in range(k * G, k * G + G):
                                    n = b * TB + j
                                    pe.wait_ge(dash_used, n + 1)
                                    pe.wait_ge(diag_copied, n + 1)
                                    random_features(pe, dash_ps[:, j % 2], diag_ps, kT, k2, j % G, features[:],
                                                    half_heads[:]).then_inc(dash_done, 1)
                            pe.wait_ge(exp_done, b + 1)
                            for c in range(CH):
                                pe.wait_ge(free, b * PER + 2 * USES + c + 1)
                                for j in range(TB):
                                    last = pe.matmul(ring[:, c % 2, 0:D + 1], dash[:, j, c * P:(c + 1) * P], hk[:, j // G, j % G, :],
                                                     start=(j == 0), stop=(j == TB - 1))
                                last.then_inc(full, 1)
                            for j in range(TB):
                                last = pe.matmul(h_sum_ps[:, 0:D + 1], g.ones[:], hk[:, j // G, j % G, :],
                                                 start=(j == 0), stop=(j == TB - 1))
                            last.then_inc(h_sum_done, 1)

            with ExitStack() as c2:
                t = Maker(nc, c2)
                sums = t.sb("sums", [P, CH, D])
                sumsT = t.sb("sumsT", [P, CH, KD, P])
                h_eps, k_col, k_diag = t.sb("h_eps", [P, D + 1]), t.sb("k_col", [P, CH]), t.sb("k_diag", [P, CH, P])
                kv = t.sb("kv", [P, CH, P])
                common, alpha = t.sb("common", [P, 1]), t.sb("alpha", [P, B])
                big_ps = t.ps("big_ps", [P, CH, KD, P])
                kv_ps = t.ps("kv_ps", [P, CH, P])
                ks_ps = t.ps("ks_ps", [P, CH, P])
                own, alpha_in, alpha_done, sums_ready, turned, turned_out, kv_done, kv_ready, out_done, out_copied = (
                    mk.sem("kc_dve"), mk.sem("alpha_in"), mk.sem("alpha_done"), mk.sem("kc_sums"), mk.sem("kc_turned"),
                    mk.sem("kc_turned_out"), mk.sem("kc_kv_done"), mk.sem("kc_kv_ready"), mk.sem("kc_out_done"),
                    mk.sem("kc_out_copied"))
                diag_ready, ks_done, ks_copied = mk.sem("kc_diag"), mk.sem("kc_ks_done"), mk.sem("kc_ks_copied")
                with nc.Block() as block:
                    @block.vector
                    def _(dve):
                        v = Steps(dve, own)
                        v.mark(dve.memset(kv[:], 0.0))
                        v(dve.reduce_max(common[:], peak[:], AX.X))
                        v(dve.tensor_scalar(alpha[:], peak[:], common[:], None, ALU.subtract))
                        dve.sem_inc(alpha_in, 1)
                        dve.wait_ge(alpha_done, 1)
                        first, per = v.n, 7
                        with dve.Fori(0, B) as b:
                            v = Steps(dve, own, b * per + first)
                            scale = alpha[:, bass.ds(b, 1)]
                            v.mark(dve.tensor_scalar(h_eps[:], h_sum[:, bass.ds(b, 1), :].rearrange("p a d -> p (a d)"), KERN_EPS,
                                                     None, ALU.mult))
                            v.mark(dve.tensor_scalar(sums[:], a_sum[:, bass.ds(b, 1)].rearrange("p a c d -> p (a c) d"), scale, None, ALU.mult))
                            v.mark(dve.tensor_scalar(k_col[:], k_sum[:, bass.ds(b, 1), :].rearrange("p a c -> p (a c)"), scale, None, ALU.mult))
                            v.sync()
                            v.mark(dve.tensor_tensor(sums[:], sums[:], h_eps[:, 0:D].unsqueeze(1).to_broadcast([P, CH, D]), ALU.add))
                            v.mark(dve.tensor_scalar(k_col[:], k_col[:], h_eps[:, D:D + 1], None, ALU.add))
                            v.sync()
                            dve.sem_inc(sums_ready, 1)
                            v(dve.tensor_tensor(k_diag[:], g.ident[:].unsqueeze(1).to_broadcast([P, CH, P]),
                                                k_col[:].unsqueeze(2).to_broadcast([P, CH, P]), ALU.mult))
                            dve.sem_inc(diag_ready, 1)
                            dve.wait_ge(turned, b + 1)
                            dve.tensor_copy(sumsT[:, CH // 2:], big_ps[:, CH // 2:]).then_inc(turned_out, 1)
                            dve.wait_ge(kv_done, b + 1)
                            dve.tensor_copy(kv[DH:P, :, MF:P], kv_ps[DH:P, :, MF:P]).then_inc(kv_ready, 1)
                            dve.wait_ge(ks_done, b + 1)
                            v(dve.tensor_copy(ksum[:, bass.ds(b, 1), :].rearrange("p a n -> p (a n)"), ks_ps[:].rearrange("p c n -> p (c n)")))
                            dve.wait_ge(out_done, b + 1)
                            dve.tensor_copy(kv_out[:, bass.ds(b, 1), CH // 2:, :].rearrange("p a c n -> p (a c n)"),
                                            big_ps[:, CH // 2:].rearrange("p c k n -> p (c k n)")).then_inc(out_copied, 1)
                            assert v.n == per, v.n

                    @block.scalar
                    def _(act):
                        act.wait_ge(alpha_in, 1)
                        act.activation(alpha[:], alpha[:], ACT.Exp).then_inc(alpha_done, 1)
                        with act.Fori(0, B) as b:
                            act.wait_ge(turned, b + 1)
                            act.activation(sumsT[:, 0:CH // 2], big_ps[:, 0:CH // 2], ACT.Copy).then_inc(turned_out, 1)
                            act.wait_ge(kv_done, b + 1)
                            act.activation(kv[0:DH, :, 0:MF], kv_ps[0:DH, :, 0:MF], ACT.Copy).then_inc(kv_ready, 1)
                            act.wait_ge(out_done, b + 1)
                            act.activation(kv_out[:, bass.ds(b, 1), 0:CH // 2, :].rearrange("p a c n -> p (a c n)"),
                                           big_ps[:, 0:CH // 2].rearrange("p c k n -> p (c k n)"), ACT.Copy).then_inc(out_copied, 1)

                    @block.tensor
                    def _(pe):
                        pe.sem_inc(out_copied, 2)
                        with pe.Fori(0, B) as b:
                            pe.wait_ge(sums_ready, b + 1)
                            pe.wait_ge(out_copied, 2 * b + 2)
                            for c in range(CH):
                                for k in range(KD):
                                    last = pe.transpose(big_ps[:, c, k, :], sums[:, c, k * P:(k + 1) * P], g.ident[:])
                            last.then_inc(turned, 1)
                            pe.wait_ge(diag_ready, b + 1)
                            for c in range(CH):
                                last = pe.matmul(ks_ps[:, c, :], g.ones[:], k_diag[:, c, :], start=True, stop=True)
                            last.then_inc(ks_done, 1)
                            pe.wait_ge(turned_out, 2 * b + 2)
                            for c in range(CH):
                                for k in range(KD):
                                    last = pe.matmul(kv_ps[:, c, :], wv[:, k, c * P:(c + 1) * P], sumsT[:, c, k, :],
                                                     start=(k == 0), stop=(k == KD - 1))
                            last.then_inc(kv_done, 1)
                            pe.wait_ge(kv_ready, 2 * b + 2)
                            for c in range(CH):
                                last = pe.matmul(big_ps[:, c].rearrange("p k n -> p (k n)"), kv[:, c, :], wo[:, c, :],
                                                 start=True, stop=True)
                            last.then_inc(out_done, 1)

        with ExitStack() as c2:
            t = Maker(nc, c2)
            hq = t.sb("hq", [P, 2, G, D])
            hT = t.sb("hqT", [P, KD, GT])
            qT, q2 = t.sb("qT", [P, CH, GT]), t.sb("q2", [P, CH, GT])
            wq = t.sb("wq", [P, KD, HD])
            dash = q_dash
            prod = t.sb("q_prod", [P, HD])
            qnT = t.sb("qnT", [P, 2, CH, P])
            y = t.sb("y1", [P, 2, G, D])
            half_diag, top, shift, inv = (t.sb("q_half_diag", [P, 2, H]), t.sb("q_top", [P, H]), t.sb("q_shift", [P, H]),
                                          t.sb("q_inv", [P, H]))
            ring = t.ps("q_ring", [P, 2, 512])
            dash_ps = t.ps("q_dash_ps", [P, HD])
            diag_ps = t.ps("q_diag_ps", [P, 512])
            turn_ps = t.ps("q_turn_ps", [P, CH, P])
            out_ps = t.ps("q_out_ps", [P, 512])
            own, full, free, dash_done, dash_used, diag_copied, shifted, exp_done = (
                mk.sem("pq_dve"), mk.sem("q_full"), mk.sem("q_free"), mk.sem("q_dash_done"), mk.sem("q_dash_used"),
                mk.sem("q_diag_copied"), mk.sem("q_shifted"), mk.sem("q_exp"))
            qn_ready, turned, turned_out, out_done, out_copied, y_ready = (
                mk.sem("qn_ready"), mk.sem("qn_turned"), mk.sem("qnT_ready"), mk.sem("q_out_done"), mk.sem("q_out_copied"),
                mk.sem("y1_ready"))
            wq_in = mk.sem("wq_in")
            h_in = [mk.sem("hq_in0"), mk.sem("hq_in1")]
            y_out = [mk.sem("y1_out0"), mk.sem("y1_out1")]

            with nc.Block() as block:
                @block.sync
                def _(sp):
                    def load(n, k):
                        sp.dma_start(hq[:, k], h_dram[bass.ds(n * GT, GT), :].rearrange("(t p) d -> p t d", p=P)).then_inc(h_in[k], 16)

                    load(0, 0)
                    sp.dma_start(wq[:], a["L1_attn_Wq"].rearrange("(k p) h d -> p k (h d)", p=P)).then_inc(wq_in, 16)
                    load(1, 1)

                    def body(b, last):
                        for k in range(2):
                            n = 2 * b + k
                            sp.wait_ge(y_ready, n + 1)
                            sp.dma_start(y_dram[bass.ds(n * GT, GT), :].rearrange("(t p) d -> p t d", p=P), y[:, k]).then_inc(y_out[k], 16)
                            if not last:
                                load(n + 2, k)

                    batches(sp, body)
                    for k in range(2):
                        sp.wait_ge(y_out[k], 16 * (B + 1))

                @block.gpsimd
                def _(pool):
                    for k in range(2):
                        pool.sem_inc(y_out[k], 16)
                    with pool.Fori(0, B) as b:
                        for k in range(2):
                            pool.wait_ge(out_copied, (2 * b + k + 1) * G + 1)
                            pool.tensor_tensor(y[:, k], y[:, k], hq[:, k], ALU.add).then_inc(y_ready, 1)

                @block.vector
                def _(dve):
                    dve.sem_inc(dash_used, 1)
                    per = 6
                    with dve.Fori(0, B) as b:
                        for j in range(TB):
                            n = b * TB + j
                            v = Steps(dve, own, n * per)
                            heads = lambda ap: ap.rearrange("p (h m) -> p h m", h=H)
                            dve.wait_ge(diag_copied, n + 2)
                            v(dve.tensor_reduce(top[:], heads(dash_ps[:]), AX.X, ALU.max))
                            v(dve.tensor_tensor(shift[:], top[:], half_diag[:, j % 2, :], ALU.add))
                            v(dve.tensor_tensor(heads(dash[:, j % 2, :]), heads(dash_ps[:]),
                                                shift[:].unsqueeze(2).to_broadcast([P, H, MF]), ALU.subtract))
                            dve.sem_inc(dash_used, 1)
                            dve.sem_inc(shifted, 1)
                            dve.wait_ge(exp_done, n + 1)
                            v(dve.scalar_tensor_tensor(prod[:], dash[:, j % 2, :], KERN_EPS,
                                                       ksum[:, bass.ds(b, 1), :].rearrange("p a n -> p (a n)"), ALU.add, ALU.mult))
                            v(dve.tensor_reduce(top[:], heads(prod[:]), AX.X, ALU.add))
                            v(dve.reciprocal(inv[:], top[:]))
                            dve.scalar_tensor_tensor(heads(qn[:, j % 2, :]), heads(dash[:, j % 2, :]), KERN_EPS,
                                                     inv[:].unsqueeze(2).to_broadcast([P, H, MF]), ALU.add, ALU.mult).then_inc(qn_ready, 1)
                            assert v.n == per

                @block.scalar
                def _(act):
                    act.sem_inc(free, 2)
                    act.sem_inc(diag_copied, 1)
                    act.sem_inc(out_copied, 1)
                    act.sem_inc(turned_out, 1)
                    copy_heads(act, ring, hT, qT, q2, full, free, 0)

                    def finish(b, k, j):
                        n = b * TB + k * G + j
                        act.wait_ge(out_done, n + 1)
                        if j == 0:
                            act.wait_ge(y_out[k], 16 * (b + 1))
                        act.activation(y[:, k, j, :], out_ps[:, 0:D], ACT.Copy).then_inc(out_copied, 1)

                    def turn(n, j):
                        act.wait_ge(turned, n + 1)
                        act.activation(qnT[:, j % 2], turn_ps[:], ACT.Copy).then_inc(turned_out, 1)

                    def body(b, last):
                        for k in range(2):
                            for j in range(G):
                                n = b * TB + k * G + j
                                act.wait_ge(dash_done, n + 1)
                                act.activation(half_diag[:, j % 2, :], diag_ps[:, 0:H], ACT.Copy).then_inc(diag_copied, 1)
                                if j:
                                    turn(n - 1, j - 1)
                                act.wait_ge(shifted, n + 1)
                                act.activation(dash[:, j % 2, :], dash[:, j % 2, :], ACT.Exp).then_inc(exp_done, 1)
                                if j:
                                    finish(b, k, j - 1)
                            if k == 0 or not last:
                                copy_heads(act, ring, hT, qT, q2, full, free, (2 * b + k + 1) * USES)
                            turn(b * TB + k * G + G - 1, G - 1)
                            finish(b, k, G - 1)

                    batches(act, body)

                @block.tensor
                def _(pe):
                    def project(n, k, uses):
                        pe.wait_ge(h_in[k], uses)
                        project_heads(pe, ring, hq[:, k], hT, g.ident[:], wq, full, free, n * USES)

                    def attend(n, j):
                        pe.wait_ge(qn_ready, n + 1)
                        pe.wait_ge(turned_out, n + 1)
                        for c in range(CH):
                            last = pe.transpose(turn_ps[:, c, :], qn[:, j % 2, c * P:(c + 1) * P], g.ident[:])
                        last.then_inc(turned, 1)
                        pe.wait_ge(turned_out, n + 2)
                        pe.wait_ge(out_copied, n + 1)

                    def outputs(b, n, j):
                        attend(n, j)
                        for c in range(CH):
                            last = pe.matmul(out_ps[:, 0:D], qnT[:, j % 2, c, :],
                                             kv_out[:, bass.ds(b, 1), c, :].rearrange("p a n -> p (a n)"),
                                             start=(c == 0), stop=(c == CH - 1))
                        last.then_inc(out_done, 1)

                    pe.wait_ge(wq_in, 16)
                    project(0, 0, 16)

                    def body(b, last):
                        for k in range(2):
                            pe.wait_ge(free, (2 * b + k + 1) * USES + 2)
                            for j in range(G):
                                n = b * TB + k * G + j
                                pe.wait_ge(dash_used, n + 1)
                                pe.wait_ge(diag_copied, n + 1)
                                random_features(pe, dash_ps, diag_ps, qT, q2, j, features[:], half_heads[:]).then_inc(dash_done, 1)
                                if j:
                                    outputs(b, n - 1, j - 1)
                            if k == 0:
                                project(2 * b + 1, 1, 16 * (b + 1))
                            elif not last:
                                project(2 * b + 2, 0, 16 * (b + 2))
                            outputs(b, b * TB + k * G + G - 1, G - 1)

                    batches(pe, body)

    mk.clear_signals()
    elu_ffn(nc, mk, g, a, y_dram)


RINGS = 4
PLACES = KD + CF


class Ffn:

    HID_CREDIT = 2

    def __init__(self, nc, mk, t, tag):
        sb, ps, sem = (lambda n, *s: t.sb(f"{tag}_{n}", *s)), (lambda n, *s: t.ps(f"{tag}_{n}", *s)), (lambda n: mk.sem(f"{tag}_{n}"))
        self.rows = sb("rows", [P, 2, G, D])
        self.rowsT = sb("rowsT", [P, KD, GT])
        self.hid = sb("hid", [P, 2, CF, GT])
        self.w1, self.w2 = sb("w1", [P, KD, DFF]), sb("w2", [P, CF, D])
        self.back = sb("back", [P, G, D])
        self.st, self.mv, self.var, self.rstd = sb("st", [P, G, 6]), sb("mv", [P, G, 2]), sb("var", [P, G]), sb("rstd", [P, G])
        self.ring = ps("ring", [P, RINGS, GT])
        self.down = ps("down", [P, G, 512])
        self.own, self.var_ready, self.rstd_ready = sem("dve"), sem("var"), sem("rstd_ready")
        self.weights_in, self.rows_ready, self.full = sem("weights_in"), sem("rows_ready"), sem("full")
        self.act_free, self.dve_free, self.hid_ready = sem("act_free"), sem("dve_free"), sem("hid_ready")
        self.down_done, self.down_used = sem("down_done"), sem("down_used")

    def place(self, k, i):
        return (k * PLACES + i) % RINGS

    def up(self, pe, n, k, ident):
        pe.wait_ge(self.rows_ready, n + 1)
        for i in range(PLACES):
            pe.wait_ge(self.act_free, n * PLACES + i + 1)
            pe.wait_ge(self.dve_free, n * PLACES + i + 1)
            out = self.ring[:, self.place(k, i), :]
            if i < KD:
                for j in range(G):
                    last = pe.transpose(out[:, j * P:(j + 1) * P], self.rows[:, k, j, i * P:(i + 1) * P], ident)
            else:
                if i == KD:
                    pe.wait_ge(self.act_free, n * PLACES + KD + RINGS)
                c = i - KD
                for d in range(KD):
                    last = pe.matmul(out, self.w1[:, d, c * P:(c + 1) * P], self.rowsT[:, d, :], start=(d == 0), stop=(d == KD - 1))
            last.then_inc(self.full, 1)

    def back_down(self, pe, n, k):
        pe.wait_ge(self.hid_ready, (n + 1) * CF + self.HID_CREDIT)
        for j in range(G):
            pe.wait_ge(self.down_used, n * G + j + 1)
            for c in range(CF):
                last = pe.matmul(self.down[:, j, 0:D], self.hid[:, k, c, j * P:(j + 1) * P], self.w2[:, c, :],
                                 start=(c == 0), stop=(c == CF - 1))
            last.then_inc(self.down_done, 1)

    def tensor_program(self, pe, ident, b_loop):
        pe.wait_ge(self.weights_in, 32)
        self.up(pe, 0, 0, ident)

        def body(b, last):
            for k in range(2):
                n = 2 * b + k
                if k == 0 or not last:
                    self.up(pe, n + 1, 1 - k, ident)
                self.back_down(pe, n, k)

        b_loop(pe, body)

    def copy_turned(self, act, n, k):
        for i in range(KD):
            act.wait_ge(self.full, n * PLACES + i + 1)
            act.activation(self.rowsT[:, i, :], self.ring[:, self.place(k, i), :], ACT.Copy).then_inc(self.act_free, 1)


def columns(ap):
    return ap.rearrange("(c p) -> p c", p=P)


def elu_ffn(nc, mk, g, a, y_dram):
    with ExitStack() as ctx:
        t = Maker(nc, ctx)
        f = Ffn(nc, mk, t, "elu")
        y = t.sb("elu_y", [P, 2, G, D])
        base = t.sb("elu_base", [P, 2, G, D])
        e, r = t.sb("elu_e", [P, 2, GT]), t.sb("elu_r", [P, 2, GT])
        b1, b1_less = t.sb("elu_b1", [P, CF]), t.sb("elu_b1_less", [P, CF])
        vec = t.sb("elu_vec", [P, 5, D])
        LN1_G, LN1_B, B2, LN2_G, LN2_B = range(5)
        gate_g, gate_b = t.sb("elu_gate_g", [P, B, D]), t.sb("elu_gate_b", [P, B, D])
        y_in = [mk.sem("elu_y_in0"), mk.sem("elu_y_in1")]
        small_in, base_ready, base_used = mk.sem("elu_small_in"), mk.sem("elu_base_ready"), mk.sem("elu_base_used")
        mod = g.modb[:].rearrange("p b (s d) -> p b s d", s=6)
        spread = lambda i: vec[:, i:i + 1, :].to_broadcast([P, G, D])

        with nc.Block() as block:
            @block.sync
            def _(sp):
                def load(n, k):
                    sp.dma_start(y[:, k], y_dram[bass.ds(n * GT, GT), :].rearrange("(t p) d -> p t d", p=P)).then_inc(y_in[k], 16)

                load(0, 0)
                for i, name in enumerate(("ln1_g", "ln1_b", "b2", "ln2_g", "ln2_b")):
                    sp.dma_start(vec[:, i, :], a[f"L1_attn_{name}"].partition_broadcast(P)).then_inc(small_in, 16)
                sp.dma_start(b1[:], columns(a["L1_attn_b1"]), allow_slow_non_contiguous=True).then_inc(small_in, 16)
                load(1, 1)
                sp.dma_start(f.w1[:], a["L1_attn_W1"].rearrange("(k p) n -> p k n", p=P)).then_inc(f.weights_in, 16)
                sp.dma_start(f.w2[:], a["L1_attn_W2"].rearrange("(c p) n -> p c n", p=P)).then_inc(f.weights_in, 16)
                with sp.Fori(0, B - 1) as b:
                    for k in range(2):
                        sp.wait_ge(f.rows_ready, 2 * b + k + 1)
                        load(2 * b + k + 2, k)

            @block.gpsimd
            def _(pool):
                pool.wait_ge(small_in, 96)

                def power(norms):
                    pool.wait_ge(f.var_ready, norms + 1)
                    rsqrt_rows(pool, f.rstd, f.var, g.minus_half, G, f.rstd_ready)

                def add_bias(n, k):
                    pool.wait_ge(f.rows_ready, n + 1)
                    pool.tensor_tensor(base[:, k], f.rows[:, k], spread(B2), ALU.add).then_inc(base_ready, 1)

                power(0)
                power(1)
                add_bias(0, 0)
                add_bias(1, 1)

                def body(b, last):
                    for k in range(2):
                        n = 2 * b + k
                        power(2 + 2 * n - (k if last else 0))
                        if not last:
                            power(3 + 2 * n)
                            pool.wait_ge(base_used, n + 1)
                            add_bias(n + 2, k)

                batches(pool, body)

            @block.scalar
            def _(act):
                act.wait_ge(small_in, 96)
                act.sem_inc(f.act_free, RINGS)

                def up(n, k):
                    f.copy_turned(act, n, k)
                    for c in range(CF):
                        act.wait_ge(f.dve_free, n * PLACES + KD + c + 1 + RINGS)
                        act.wait_ge(f.hid_ready, n * CF + c + 1)
                        act.activation(e[:, c % 2, :], f.ring[:, f.place(k, KD + c), :], ACT.Exp,
                                       bias=b1[:, c:c + 1]).then_inc(f.act_free, 1)

                up(0, 0)

                def body(b, last):
                    up(2 * b + 1, 1)
                    if not last:
                        up(2 * b + 2, 0)

                batches(act, body)

            @block.vector
            def _(dve):
                v = Steps(dve, f.own)
                dve.sem_inc(f.dve_free, RINGS)
                dve.sem_inc(f.down_used, G)
                dve.sem_inc(f.hid_ready, f.HID_CREDIT)
                dve.wait_ge(small_in, 96)
                v.mark(dve.tensor_scalar(b1_less[:], b1[:], -1.0, None, ALU.add))
                v.mark(dve.tensor_tensor(gate_g[:], mod[:, :, GA, :], vec[:, LN2_G:LN2_G + 1, :].to_broadcast([P, B, D]), ALU.mult))
                v.mark(dve.tensor_tensor(gate_b[:], mod[:, :, GA, :], vec[:, LN2_B:LN2_B + 1, :].to_broadcast([P, B, D]), ALU.mult))
                v.sync()

                def prepare(v, n, k, b, norms, based=None):
                    dve.wait_ge(y_in[k], 16 * (b + 1))
                    if based is not None:
                        dve.wait_ge(base_ready, based)
                    layer_norm_stats(v, g.spare, f.st, f.mv, f.var, G, lambda j: y[:, k, j, :], ENC_EPS, f.var_ready)
                    dve.wait_ge(f.rstd_ready, norms + 1)
                    for j in range(G):
                        v.mark(dve.tensor_scalar(f.rows[:, k, j, :], y[:, k, j, :], f.mv[:, j, 0:1], f.rstd[:, j:j + 1],
                                                 ALU.subtract, ALU.mult))
                    v.sync()
                    v(dve.tensor_tensor(f.rows[:, k], f.rows[:, k], spread(LN1_G), ALU.mult))
                    dve.tensor_tensor(f.rows[:, k], f.rows[:, k], spread(LN1_B), ALU.add).then_inc(f.rows_ready, 1)

                def hidden(v, n, k):
                    dve.sem_inc(f.dve_free, KD)
                    for c in range(CF):
                        dve.wait_ge(f.full, n * PLACES + KD + c + 1)
                        v(dve.tensor_scalar(r[:, c % 2, :], f.ring[:, f.place(k, KD + c), :], b1_less[:, c:c + 1], -1.0,
                                            ALU.add, ALU.max))
                        dve.sem_inc(f.dve_free, 1)
                        dve.wait_ge(f.act_free, n * PLACES + KD + c + 1 + RINGS)
                        dve.scalar_tensor_tensor(f.hid[:, k, c, :], e[:, c % 2, :], 1.0, r[:, c % 2, :], ALU.min,
                                                 ALU.add).then_inc(f.hid_ready, 1)

                def result(v, n, k, b, norms):
                    v.sync()
                    dve.wait_ge(base_ready, n + 1)
                    for j in range(G):
                        dve.wait_ge(f.down_done, n * G + j + 1)
                        v.mark(dve.tensor_tensor(f.back[:, j, :], f.down[:, j, 0:D], base[:, k, j, :], ALU.add))
                    v.sync()
                    dve.sem_inc(f.down_used, G)
                    dve.sem_inc(base_used, 1)
                    layer_norm_stats(v, g.spare, f.st, f.mv, f.var, G, lambda j: f.back[:, j, :], ENC_EPS, f.var_ready)
                    dve.wait_ge(f.rstd_ready, norms + 1)
                    for j in range(G):
                        v.mark(dve.tensor_scalar(f.back[:, j, :], f.back[:, j, :], f.mv[:, j, 0:1], f.rstd[:, j:j + 1],
                                                 ALU.subtract, ALU.mult))
                    v.sync()
                    v(dve.tensor_tensor(f.back[:], f.back[:], gate_g[:, bass.ds(b, 1), :].to_broadcast([P, G, D]), ALU.mult))
                    v(dve.tensor_tensor(f.back[:], f.back[:], gate_b[:, bass.ds(b, 1), :].to_broadcast([P, G, D]), ALU.add))
                    x = g.x[:, bass.ds(b * TB + k * G, G), :]
                    v.mark(dve.tensor_tensor(x, x, f.back[:], ALU.add))

                prepare(v, 0, 0, 0, 0)
                prepare(v, 1, 1, 0, 1)
                hidden(v, 0, 0)
                first = v.n
                PREP, HID, RES = 3 * G + 1, CF, 4 * G + 3
                per = 2 * (PREP + HID + RES)

                def body(b, last):
                    v = Steps(dve, f.own, b * per + first)
                    for k in range(2):
                        n = 2 * b + k
                        if k == 0 or not last:
                            hidden(v, n + 1, 1 - k)
                        if not last:
                            prepare(v, n + 2, k, b + 1, 2 + 2 * n, n + 1)
                        result(v, n, k, b, 2 + 2 * n - k if last else 3 + 2 * n)
                    assert last or v.n == per, (v.n, per)

                batches(dve, body)

            @block.tensor
            def _(pe):
                f.tensor_program(pe, g.ident[:], batches)
        mk.clear_signals()


def wave_ffn(nc, mk, g, a, out):
    TURN = 1.0 / (2.0 * 3.141592653589793)
    FULL = 6.283185
    with ExitStack() as ctx:
        t = Maker(nc, ctx)
        f = Ffn(nc, mk, t, "wave")
        whole, turns, wave, u = (t.sb("wave_whole", [P, 2, GT]), t.sb("wave_turns", [P, 2, GT]), t.sb("wave_sine", [P, 2, GT]),
                                 t.sb("wave_u", [P, 2, GT]))
        vec = t.sb("wave_vec", [P, 8, CF])
        B1, THETA, W_RE, W_IM, OFFSET, AMP, SINE, COSINE = range(8)
        part = t.sb("wave_part", [P, 2, CF])
        b2 = t.sb("wave_b2", [P, D])
        small_in, consts, angles, sines = mk.sem("wave_small_in"), mk.sem("wave_consts"), mk.sem("wave_angles"), mk.sem("wave_sines")
        turns_ready, sine_ready, u_ready, x_ready, x_out = (mk.sem("wave_turns_ready"), mk.sem("wave_sine_ready"),
                                                            mk.sem("wave_u_ready"), mk.sem("wave_x_ready"), mk.sem("x_out"))
        mod = g.modb[:].rearrange("p b (s d) -> p b s d", s=6)

        with nc.Block() as block:
            @block.sync
            def _(sp):
                for i, name in ((B1, "b1"), (THETA, "quantum_phases"), (W_RE, "quantum_weights_real"), (W_IM, "quantum_weights_imag")):
                    sp.dma_start(vec[:, i, :], columns(a[f"L1_ffn_{name}"]), allow_slow_non_contiguous=True).then_inc(small_in, 16)
                sp.dma_start(b2[:], a["L1_ffn_b2"].partition_broadcast(P)).then_inc(small_in, 16)
                sp.dma_start(f.w1[:], a["L1_ffn_W1"].rearrange("(k p) n -> p k n", p=P)).then_inc(f.weights_in, 16)
                sp.dma_start(f.w2[:], a["L1_ffn_W2"].rearrange("(c p) n -> p c n", p=P)).then_inc(f.weights_in, 16)
                rows = out.rearrange("b (t p) d -> p (b t) d", p=P)
                with sp.Fori(0, NG) as n:
                    sp.wait_ge(x_ready, n + 1)
                    sp.dma_start(rows[:, bass.ds(n * G, G), :], g.x[:, bass.ds(n * G, G), :]).then_inc(x_out, 16)
                sp.wait_ge(x_out, 16 * NG)

            @block.gpsimd
            def _(pool):
                with pool.Fori(0, NG) as n:
                    pool.wait_ge(f.var_ready, n + 1)
                    rsqrt_rows(pool, f.rstd, f.var, g.minus_half, G, f.rstd_ready)

            @block.scalar
            def _(act):
                act.sem_inc(f.act_free, RINGS)
                act.wait_ge(angles, 1)
                act.activation(vec[:, SINE, :], part[:, 0, :], ACT.Sin, scale=FULL)
                act.activation(vec[:, COSINE, :], part[:, 1, :], ACT.Sin, scale=FULL).then_inc(sines, 1)

                def up(n, k):
                    f.copy_turned(act, n, k)
                    act.wait_ge(f.act_free, n * PLACES + KD + RINGS)
                    act.sem_inc(f.act_free, CF)
                    for c in range(CF + 1):
                        if c < CF:
                            act.wait_ge(turns_ready, n * CF + c + 1)
                            if c >= 2:
                                act.wait_ge(u_ready, n * CF + c - 1)
                            else:
                                act.wait_ge(u_ready, n * CF)
                            act.activation(wave[:, c % 2, :], turns[:, c % 2, :], ACT.Sin, scale=FULL).then_inc(sine_ready, 1)
                        if c:
                            act.wait_ge(u_ready, n * CF + c)
                            act.activation(f.hid[:, k, c - 1, :], u[:, (c - 1) % 2, :], ACT.Relu,
                                           bias=vec[:, B1, c - 1:c]).then_inc(f.hid_ready, 1)

                up(0, 0)

                def body(b, last):
                    up(2 * b + 1, 1)
                    if not last:
                        up(2 * b + 2, 0)

                batches(act, body)

            @block.vector
            def _(dve):
                v = Steps(dve, f.own)
                dve.sem_inc(f.dve_free, RINGS)
                dve.sem_inc(f.down_used, G)
                dve.sem_inc(f.hid_ready, f.HID_CREDIT)
                dve.wait_ge(small_in, 80)
                v(dve.tensor_scalar(part[:, 0, :], vec[:, THETA, :], TURN, None, ALU.mult))
                v(dve.tensor_scalar(part[:, 0, :], part[:, 0, :], ROUND, ROUND, ALU.add, ALU.subtract))
                v(dve.scalar_tensor_tensor(vec[:, THETA, :], part[:, 0, :], -PI2_HI, vec[:, THETA, :], ALU.mult, ALU.add))
                v(dve.scalar_tensor_tensor(vec[:, THETA, :], part[:, 0, :], -PI2_LO, vec[:, THETA, :], ALU.mult, ALU.add))
                v(dve.tensor_scalar(vec[:, THETA, :], vec[:, THETA, :], TURN, None, ALU.mult))
                for i, ahead in ((0, 0.0), (1, 0.25)):
                    v(dve.tensor_scalar(part[:, i, :], vec[:, THETA, :], ahead, ROUND, ALU.add, ALU.add))
                    v(dve.tensor_scalar(part[:, i, :], part[:, i, :], ROUND, ahead, ALU.subtract, ALU.subtract))
                    v(dve.tensor_tensor(part[:, i, :], vec[:, THETA, :], part[:, i, :], ALU.subtract))
                dve.sem_inc(angles, 1)
                v(dve.scalar_tensor_tensor(vec[:, OFFSET, :], vec[:, B1, :], 0.1 * TURN, vec[:, THETA, :], ALU.mult, ALU.add))
                dve.wait_ge(sines, 1)
                v.mark(dve.tensor_tensor(vec[:, COSINE, :], vec[:, COSINE, :], vec[:, W_RE, :], ALU.mult))
                v.mark(dve.tensor_tensor(vec[:, SINE, :], vec[:, SINE, :], vec[:, W_IM, :], ALU.mult))
                v.sync()
                v(dve.tensor_tensor(vec[:, AMP, :], vec[:, COSINE, :], vec[:, SINE, :], ALU.add))
                v(dve.scalar_tensor_tensor(vec[:, AMP, :], vec[:, AMP, :], 0.1, vec[:, W_IM, :], ALU.mult, ALU.mult))

                def prepare(v, n, k, b):
                    tile = lambda j: g.x[:, bass.ds(b * TB + k * G + j, 1), :]
                    layer_norm_stats(v, g.spare, f.st, f.mv, f.var, G, tile, LN_EPS, f.var_ready)
                    dve.wait_ge(f.rstd_ready, n + 1)
                    for j in range(G):
                        v.mark(dve.tensor_scalar(f.rows[:, k, j:j + 1, :], tile(j), f.mv[:, j, 0:1], f.rstd[:, j:j + 1],
                                                 ALU.subtract, ALU.mult))
                    v.sync()
                    v(dve.tensor_tensor(f.rows[:, k], f.rows[:, k], mod[:, bass.ds(b, 1), CB, :].to_broadcast([P, G, D]), ALU.mult))
                    dve.tensor_tensor(f.rows[:, k], f.rows[:, k], mod[:, bass.ds(b, 1), SB, :].to_broadcast([P, G, D]),
                                      ALU.add).then_inc(f.rows_ready, 1)

                def hidden(v, n, k):
                    dve.sem_inc(f.dve_free, KD)
                    for c in range(CF + 1):
                        if c < CF:
                            z, i = f.ring[:, f.place(k, KD + c), :], c % 2
                            dve.wait_ge(f.full, n * PLACES + KD + c + 1)
                            if c >= 2:
                                dve.wait_ge(sine_ready, n * CF + c - 1)
                            v(dve.tensor_scalar(turns[:, i, :], z, 0.1 * TURN, vec[:, OFFSET, c:c + 1], ALU.mult, ALU.add))
                            v(dve.tensor_scalar(whole[:, i, :], turns[:, i, :], ROUND, ROUND, ALU.add, ALU.subtract))
                            dve.tensor_tensor(turns[:, i, :], turns[:, i, :], whole[:, i, :], ALU.subtract).then_inc(turns_ready, 1)
                        if c:
                            z, i = f.ring[:, f.place(k, KD + c - 1), :], (c - 1) % 2
                            dve.wait_ge(sine_ready, n * CF + c)
                            dve.wait_ge(f.hid_ready, n * CF + max(c - 2, 0) + f.HID_CREDIT)
                            dve.scalar_tensor_tensor(u[:, i, :], wave[:, i, :], vec[:, AMP, c - 1:c], z, ALU.mult,
                                                     ALU.add).then_inc(u_ready, 1)
                            dve.wait_ge(u_ready, n * CF + c)
                            dve.sem_inc(f.dve_free, 1)

                def result(v, n, k, b):
                    if k:
                        dve.wait_ge(x_ready, n)
                    for j in range(G):
                        dve.wait_ge(f.down_done, n * G + j + 1)
                        v.mark(dve.tensor_tensor(f.back[:, j, :], f.down[:, j, 0:D], b2[:], ALU.add))
                    v.sync()
                    dve.sem_inc(f.down_used, G)
                    v(dve.tensor_tensor(f.back[:], f.back[:], mod[:, bass.ds(b, 1), GB, :].to_broadcast([P, G, D]), ALU.mult))
                    x = g.x[:, bass.ds(b * TB + k * G, G), :]
                    dve.tensor_tensor(x, x, f.back[:], ALU.add).then_inc(x_ready, 1)

                prepare(v, 0, 0, 0)
                prepare(v, 1, 1, 0)
                hidden(v, 0, 0)
                first = v.n
                per = 2 * (3 * G + 1 + 2 * CF + G + 1)

                def body(b, last):
                    v = Steps(dve, f.own, b * per + first)
                    for k in range(2):
                        n = 2 * b + k
                        if k == 0 or not last:
                            hidden(v, n + 1, 1 - k)
                        if not last:
                            prepare(v, n + 2, k, b + 1)
                        result(v, n, k, b)
                    assert last or v.n == per, (v.n, per)

                batches(dve, body)

            @block.tensor
            def _(pe):
                f.tensor_program(pe, g.ident[:], batches)
        mk.clear_signals()


class Chip:
    pass


def program(nc, a, out):
    with ExitStack() as ctx:
        mk = Maker(nc, ctx)
        g = Chip()
        g.x = mk.sb("x", [P, NT, D])
        g.modb = mk.sb("modb", [P, B, 6 * D])
        g.ident, g.flip, g.ones = mk.sb("ident", [P, P]), mk.sb("flip", [P, P]), mk.sb("ones", [P, P])
        g.minus_half, g.eye_b = mk.sb("minus_half", [P, TB]), mk.sb("eye_b", [P, B, B])
        g.spare, g.pool_spare, g.pool_max = mk.sb("spare", [P, 1]), mk.sb("pool_spare", [P, 1]), mk.sb("pool_max", [P, 1])
        g.mod_dram = nc.dram_tensor("mod_dram", (2, B, 6 * D), F32, kind="Internal").ap()
        with ExitStack() as c:
            w = Maker(nc, c)
            g.wqkv, g.wconv = w.sb("wqkv", [P, 6, D]), w.sb("wconv", [P, KD])
            setup(nc, mk, g, a)
            agent_attention(nc, mk, g)
            mk.clear_signals()
        expert_choice(nc, mk, g, a)
        performer(nc, mk, g, a)
        wave_ffn(nc, mk, g, a, out)


_INS = ["L0_attn_x", "L0_attn_w_qkv", "L0_attn_w_conv1", "L0_ffn_Wr", "L0_ffn_W1", "L0_ffn_b1", "L0_ffn_W2", "L0_ffn_b2",
        "L0_c", "L0_wmod", "L1_attn_Wq", "L1_attn_Wk", "L1_attn_Wv", "L1_attn_Wo", "L1_attn_proj", "L1_attn_W1",
        "L1_attn_b1", "L1_attn_W2", "L1_attn_b2", "L1_attn_ln1_g", "L1_attn_ln1_b", "L1_attn_ln2_g", "L1_attn_ln2_b",
        "L1_ffn_W1", "L1_ffn_b1", "L1_ffn_quantum_phases", "L1_ffn_quantum_weights_real", "L1_ffn_quantum_weights_imag",
        "L1_ffn_W2", "L1_ffn_b2", "L1_c", "L1_wmod"]


def kernel(**inputs):
    import numpy as _np
    import concourse.bacc as _bacc
    from concourse import mybir as _mybir
    from concourse.bass_utils import run_bass_kernel_spmd as _run

    nc = _bacc.Bacc("TRN2", target_bir_lowering=False, num_devices=1)
    arrays, args = {}, {}
    for name in _INS:
        a = _np.ascontiguousarray(inputs[name])
        arrays[f"in_{name}_dram"] = a
        args[name] = nc.dram_tensor(f"in_{name}_dram", a.shape, _mybir.dt.from_np(a.dtype), kind="ExternalInput").ap()
    out = nc.dram_tensor("out_0_dram", (B, N, D), F32, kind="ExternalOutput").ap()
    program(nc, args, out)
    r = _run(nc, [arrays], core_ids=[0])
    return r.results[0]["out_0_dram"]
```

```python
from contextlib import ExitStack

import concourse.bass as bass
from concourse import mybir

ALU = mybir.AluOpType
ACT = mybir.ActivationFunctionType
AX = mybir.AxisListType
F32 = mybir.dt.float32
F32R = mybir.dt.float32r
U32 = mybir.dt.uint32

P = 128
B, N, D = 4, 1024, 256
T = B * N
NT = T // P
TB = N // P
KD = D // P
G = 4
GT = G * P
NG = NT // G
E, S, M = 48, 4, 256
KS = D // S
CAP = int(1.5 * T / E)
H, DH, MF = 16, 64, 64
HD = H * DH
CH = HD // P
DFF = 1024
CF = DFF // P
LN_EPS = 1e-5
ENC_EPS = 1e-6
KERN_EPS = 1e-6
DN = float(DH) ** -0.25
GATE_MIN = 0.25
SA, CA, GA, SB, CB, GB = range(6)
PI2_HI, PI2_LO = 6.28125, 0.0019353071795864769
ROUND = 12582912.0
LOWEST = -3.0e38


class Steps:

    def __init__(self, eng, sem, base=0):
        self.eng, self.sem, self.base, self.n = eng, sem, base, 0

    def start(self, base):
        self.base, self.n = base, 0

    def mark(self, ins):
        self.n += 1
        ins.then_inc(self.sem, 1)

    def sync(self):
        self.eng.wait_ge(self.sem, self.base + self.n)

    def __call__(self, ins):
        self.mark(ins)
        self.sync()


def batches(eng, body):
    with eng.Fori(0, B - 1) as b:
        body(b, False)
    body(B - 1, True)


def wait_apart(eng, sem, value, passed):
    eng.wait_ge(sem, value)
    eng.sem_inc(passed, 1)


class Maker:

    def __init__(self, nc, ctx):
        self.nc, self.ctx, self.signals = nc, ctx, []

    def sb(self, name, shape, dt=F32):
        return self.ctx.enter_context(self.nc.sbuf_tensor(name, shape, dt))

    def ps(self, name, shape, dt=F32):
        return self.ctx.enter_context(self.nc.psum_tensor(name, shape, dt))

    def sem(self, name):
        handle = self.nc.alloc_semaphore(name=name)
        self.signals.append(handle)
        return handle

    def clear_signals(self):
        self.nc.clear_and_free_semaphores(self.signals)
        self.signals = []
        self.nc.all_engine_barrier()


def layer_norm_stats(v, mv_spare, st, mv, var, tiles, x_tile, eps, var_ready):
    for j in range(tiles):
        v.mark(v.eng.bn_stats(st[:, j, :], x_tile(j)))
    v.sync()
    v.eng.memset(mv_spare[:], 0.0)
    for j in range(tiles):
        v.mark(v.eng.bn_aggr(mv[:, j, :], st[:, j, :]))
    v.sync()
    v.eng.tensor_scalar(var[:, 0:tiles], mv[:, 0:tiles, 1], eps, None, ALU.add).then_inc(var_ready, 1)


def rsqrt_rows(pool, rstd, var, minus_half, tiles, rstd_ready):
    pool.tensor_tensor(rstd[:, 0:tiles], var[:, 0:tiles], minus_half[:, 0:tiles], ALU.pow).then_inc(rstd_ready, 1)


def setup(nc, mk, g, a):
    with ExitStack() as ctx:
        t = Maker(nc, ctx)
        c_rows = t.sb("c_rows", [B, 2, D])
        c_exp = t.sb("c_exp", [B, 2, D])
        c_silu = t.sb("c_silu", [B, 2, D])
        cT = t.sb("cT", [P, 2, KD, B])
        wmod = t.sb("wmod", [P, 2, KD, 6 * D])
        rows = t.sb("rows", [B, 2, 6, D])
        size = t.sb("size", [B, 2, 2, D])
        sign = t.sb("sign", [B, 2, 2, D])
        cT_ps = t.ps("cT_ps", [P, 2, KD, B])
        mod_ps = t.ps("mod_ps", [P, 2, 6 * D])

        c_in, x_in, w_in = mk.sem("c_in"), mk.sem("x_in"), mk.sem("w_in")
        wmod_in = [mk.sem("wmod_in0"), mk.sem("wmod_in1")]
        zeroed, ident_done, exp_done = mk.sem("zeroed"), mk.sem("ident_done"), mk.sem("exp_done")
        silu_done, cT_done, cT_copied = mk.sem("silu_done"), mk.sem("cT_done"), mk.sem("cT_copied")
        mod_done, rows_done, rows_out = mk.sem("mod_done"), mk.sem("rows_done"), mk.sem("rows_out")
        g.modb_in = mk.sem("modb_in")
        own = mk.sem("setup_dve")

        with nc.Block() as block:
            @block.sync
            def _(sp):
                sp.dma_start(c_rows[:, 0, :], a["L0_c"]).then_inc(c_in, 16)
                sp.dma_start(c_rows[:, 1, :], a["L1_c"]).then_inc(c_in, 16)
                sp.dma_start(wmod[:, 0], a["L0_wmod"].rearrange("(k p) n -> p k n", p=P)).then_inc(wmod_in[0], 16)
                sp.dma_start(wmod[:, 1], a["L1_wmod"].rearrange("(k p) n -> p k n", p=P)).then_inc(wmod_in[1], 16)
                sp.dma_start(g.x[:], a["L0_attn_x"].rearrange("b (t p) d -> p (b t) d", p=P)).then_inc(x_in, 16)
                for l in range(2):
                    sp.wait_ge(rows_done, l + 1)
                    sp.dma_start(g.mod_dram[l], rows[:, l].rearrange("b s d -> b (s d)")).then_inc(rows_out, 16)
                    if l == 0:
                        sp.wait_ge(rows_out, 16)
                        sp.dma_start(g.modb[:], g.mod_dram[0].partition_broadcast(P)).then_inc(g.modb_in, 16)
                sp.wait_ge(rows_out, 32)
                sp.wait_ge(x_in, 16)

            @block.scalar
            def _(act):
                act.dma_start(g.wqkv[:], a["L0_attn_w_qkv"].rearrange("(j p) c -> p j c", p=P)).then_inc(w_in, 16)
                act.dma_start(g.wconv[:], a["L0_attn_w_conv1"].rearrange("(j p) -> p j", p=P),
                              allow_slow_non_contiguous=True).then_inc(w_in, 16)
                act.wait_ge(c_in, 32)
                act.activation(c_exp[:], c_rows[:], ACT.Exp, scale=-1.0).then_inc(exp_done, 1)
                act.wait_ge(w_in, 32)

            @block.gpsimd
            def _(pool):
                pool.memset(g.ident[:], 0.0).then_inc(zeroed, 1)
                pool.memset(g.flip[:], 0.0).then_inc(zeroed, 1)
                pool.memset(g.ones[:], 1.0)
                pool.memset(g.minus_half[:], -0.5)
                pool.memset(g.eye_b[:], 0.0).then_inc(zeroed, 1)
                pool.wait_ge(zeroed, 3)
                pool.affine_select(out=g.ident[:], in_=g.ident[:], compare_op=ALU.not_equal, fill=1.0, base=0,
                                   pattern=[[-1, P]], channel_multiplier=1).then_inc(ident_done, 1)
                pool.affine_select(out=g.flip[:], in_=g.flip[:], compare_op=ALU.not_equal, fill=1.0, base=1 - P,
                                   pattern=[[1, P]], channel_multiplier=1).then_inc(ident_done, 1)
                pool.affine_select(out=g.eye_b[:], in_=g.eye_b[:], compare_op=ALU.not_equal, fill=1.0, base=0,
                                   pattern=[[1, B], [-1, B]], channel_multiplier=0).then_inc(ident_done, 1)
                pool.wait_ge(ident_done, 3)

            @block.vector
            def _(dve):
                v = Steps(dve, own)
                dve.wait_ge(exp_done, 1)
                v(dve.tensor_scalar(c_exp[:], c_exp[:], 1.0, None, ALU.add))
                v(dve.reciprocal(c_exp[:], c_exp[:]))
                dve.tensor_tensor(c_silu[:], c_rows[:], c_exp[:], ALU.mult).then_inc(silu_done, 1)
                dve.wait_ge(cT_done, 1)
                dve.tensor_copy(cT[:], cT_ps[:]).then_inc(cT_copied, 1)
                gates, shifts = rows[:, :, GA::3, :], rows[:, :, CA::3, :]
                for l in range(2):
                    dve.wait_ge(mod_done, l + 1)
                    v(dve.tensor_copy(rows[:, l].rearrange("b s d -> b (s d)"), mod_ps[0:B, l]))
                    v.mark(dve.tensor_scalar(shifts[:, l], shifts[:, l], 1.0, None, ALU.add))
                    v.mark(dve.scalar_tensor_tensor(size[:, l], gates[:, l], -1.0, gates[:, l], ALU.mult, ALU.max))
                    v.mark(dve.tensor_scalar(sign[:, l], gates[:, l], 0.0, 2.0, ALU.is_ge, ALU.mult))
                    v.sync()
                    v(dve.tensor_scalar(size[:, l], size[:, l], GATE_MIN, None, ALU.max))
                    v(dve.scalar_tensor_tensor(gates[:, l], sign[:, l], -1.0, size[:, l], ALU.add, ALU.mult))
                    dve.sem_inc(rows_done, 1)

            @block.tensor
            def _(pe):
                pe.wait_ge(ident_done, 1)
                pe.wait_ge(silu_done, 1)
                for l in range(2):
                    for k in range(KD):
                        last = pe.transpose(cT_ps[:, l, k, :], c_silu[:, l, k * P:(k + 1) * P], g.ident[0:B, 0:B])
                last.then_inc(cT_done, 1)
                pe.wait_ge(cT_copied, 1)
                for l in range(2):
                    pe.wait_ge(wmod_in[l], 16)
                    for n in range(3):
                        cols = slice(n * 512, (n + 1) * 512)
                        for k in range(KD):
                            last = pe.matmul(mod_ps[0:B, l, cols], cT[:, l, k, :], wmod[:, l, k, cols],
                                             start=(k == 0), stop=(k == KD - 1))
                    last.then_inc(mod_done, 1)


def agent_attention(nc, mk, g):
    with ExitStack() as ctx:
        t = Maker(nc, ctx)
        h = t.sb("h0", [P, NT, D])
        prod = t.sb("prod", [P, TB, D])
        st, mv, var, rstd = (t.sb("st0", [P, TB, 6]), t.sb("mv0", [P, TB, 2]), t.sb("var0", [P, TB]),
                             t.sb("rstd0", [P, TB]))
        wconv_b = t.sb("wconv_b", [P, KD, P])
        wkT, wvT = t.sb("wkT", [P, KD, D]), t.sb("wvT", [P, KD, D])
        probe = t.sb("probe", [P, D])
        agent = t.sb("agent", [P, NT])
        score = t.sb("score", [P, NT])
        tok = t.sb("tok", [P, NT])
        masked = t.sb("masked", [P, 2, TB, B])
        mix = t.sb("mix", [B, D])
        mixT = t.sb("mixT", [P, KD, B])
        mixT_b = t.sb("mixT_b", [P, KD, B, P])
        keys = t.sb("keys", [B, D])
        small = t.sb("small", [P, 8])
        value_probe = t.sb("value_probe", [P, B, D])
        peak, peak_diag, neg_peak = t.sb("peak", [P, B]), t.sb("peak_diag", [B, B]), t.sb("neg_peak", [P, B])
        peak_row = t.sb("peak_row", [B, 1])
        part_sum, inv_sum = t.sb("part_sum", [P, B]), t.sb("inv_sum", [P, B])
        gated = t.sb("gated", [P, B, D])
        w_ps = t.ps("w_ps", [P, 2, 512])
        probe_ps = t.ps("probe_ps", [P, 512])
        mix_ps = t.ps("mix_ps", [P, B, D])
        wide_ps = t.ps("wide_ps", [P, B, D])
        tiny_ps = t.ps("tiny_ps", [P, 512])

        own, wb = mk.sem("aa_dve"), mk.sem("wconv_b_done")
        w_done, w_copied, probe_done = mk.sem("wT_done"), mk.sem("wT_copied"), mk.sem("probe_done")
        var_ready, rstd_ready, masked_ready, mix_done = (mk.sem("aa_var"), mk.sem("aa_rstd"), mk.sem("aa_masked"),
                                                         mk.sem("aa_mix"))
        normalised, scaled, rows_ready = mk.sem("aa_normalised"), mk.sem("aa_scaled"), mk.sem("aa_rows")
        mod = g.modb[:].rearrange("p b (s d) -> p b s d", s=6)

        with nc.Block() as block:
            @block.vector
            def _(dve):
                v = Steps(dve, own)
                for k in range(KD):
                    v.mark(dve.tensor_scalar(wconv_b[:, k, :], g.ones[:], g.wconv[:, k:k + 1], None, ALU.mult))
                v.sync()
                dve.sem_inc(wb, 1)
                dve.wait_ge(probe_done, 1)
                v(dve.tensor_copy(probe[:], probe_ps[:, 0:D]))

                def normalise(v, b):
                    layer_norm_stats(v, g.spare, st, mv, var, TB, lambda j: g.x[:, bass.ds(b * TB + j, 1), :], LN_EPS, var_ready)
                    dve.wait_ge(rstd_ready, b + 1)
                    for j in range(TB):
                        v.mark(dve.tensor_scalar(h[:, bass.ds(b * TB + j, 1), :], g.x[:, bass.ds(b * TB + j, 1), :],
                                                 mv[:, j, 0:1], rstd[:, j:j + 1], ALU.subtract, ALU.mult))
                    v.sync()
                    dve.sem_inc(normalised, 1)

                normalise(v, 0)
                per = 3 * TB + 3
                first = v.n

                def body(b, last):
                    v.start(b * per + first)
                    if not last:
                        normalise(v, b + 1)
                    rows = h[:, bass.ds(b * TB, TB), :]
                    dve.wait_ge(rows_ready, b + 1)
                    v(dve.tensor_tensor(prod[:], rows, probe[:].unsqueeze(1).to_broadcast([P, TB, D]), ALU.mult))
                    v(dve.tensor_reduce(agent[:, bass.ds(b * TB, TB)], prod[:], AX.X, ALU.add))
                    v(dve.tensor_tensor(masked[:, 0], agent[:, bass.ds(b * TB, TB)].unsqueeze(2).to_broadcast([P, TB, B]),
                                        g.eye_b[:, bass.ds(b, 1), :].to_broadcast([P, TB, B]), ALU.mult))
                    dve.wait_ge(mix_done, b + 1)
                    dve.tensor_scalar(masked[:, 1], masked[:, 0], float(D) ** -0.5, None, ALU.mult).then_inc(masked_ready, 1)
                    assert last or v.n == per, v.n

                dve.sem_inc(mix_done, 1)
                batches(dve, body)
                dve.wait_ge(mix_done, B + 1)
                dve.tensor_reduce(mix[:], mix_ps[0:B].rearrange("p b d -> p d b"), AX.X, ALU.add)

            @block.gpsimd
            def _(pool):
                pool.wait_ge(g.modb_in, 16)
                with pool.Fori(0, B) as b:
                    pool.wait_ge(var_ready, b + 1)
                    rsqrt_rows(pool, rstd, var, g.minus_half, TB, rstd_ready)
                    rows = h[:, bass.ds(b * TB, TB), :]
                    pool.wait_ge(normalised, b + 1)
                    pool.tensor_tensor(rows, rows, mod[:, bass.ds(b, 1), CA, :].to_broadcast([P, TB, D]), ALU.mult).then_inc(scaled, 1)
                    pool.wait_ge(scaled, b + 1)
                    pool.tensor_tensor(rows, rows, mod[:, bass.ds(b, 1), SA, :].to_broadcast([P, TB, D]), ALU.add).then_inc(rows_ready, 1)

            @block.scalar
            def _(act):
                act.wait_ge(w_done, 1)
                act.activation(wkT[:], w_ps[:, 0, :].rearrange("p (k d) -> p k d", k=KD), ACT.Copy).then_inc(w_copied, 1)
                act.activation(wvT[:], w_ps[:, 1, :].rearrange("p (k d) -> p k d", k=KD), ACT.Copy).then_inc(w_copied, 1)

            @block.tensor
            def _(pe):
                for half in range(2):
                    for k in range(KD):
                        for j in range(KD):
                            last = pe.transpose(w_ps[:, half, k * D + j * P:k * D + (j + 1) * P],
                                                g.wqkv[:, 2 + 2 * half + j, k * P:(k + 1) * P], g.ident[:])
                last.then_inc(w_done, 1)
                pe.wait_ge(wb, 1)
                for k in range(KD):
                    last = pe.matmul(probe_ps[:, 0:D], wconv_b[:, k, :], g.wqkv[:, k, :], start=(k == 0), stop=(k == KD - 1))
                last.then_inc(probe_done, 1)
                with pe.Fori(0, B) as b:
                    pe.wait_ge(masked_ready, b + 1)
                    for j in range(TB):
                        last = pe.matmul(mix_ps[0:B, bass.ds(b, 1), :], masked[:, 1, j, :], h[:, bass.ds(b * TB + j, 1), :],
                                         start=(j == 0), stop=(j == TB - 1))
                    last.then_inc(mix_done, 1)

        own = mk.sem("ab_dve")
        tp_done, tp_copied, keys_done, exp_done, attn_done, attnT_done = (
            mk.sem("mixT_done"), mk.sem("mixT_copied"), mk.sem("keys_done"), mk.sem("keys_exp"), mk.sem("attn_done"),
            mk.sem("attnT_done"))
        spread_done, probe2_done = mk.sem("spread_done"), mk.sem("value_probe_done")
        score_max, row_max, peak_ready, peak_done, neg_ready, score_exp, sums_done, masked2, mix2 = (
            mk.sem("score_max"), mk.sem("row_max"), mk.sem("peak_ready"), mk.sem("peak_done"), mk.sem("neg_ready"),
            mk.sem("score_exp"), mk.sem("sums_done"), mk.sem("masked2"), mk.sem("mix2"))
        mixT2_done, spread2_done, value_done, tok_exp, tok_diff = (
            mk.sem("mixT2_done"), mk.sem("spread2_done"), mk.sem("value_done"), mk.sem("tok_exp"), mk.sem("tok_diff"))

        def spread(v, dve):
            for k in range(KD):
                v.mark(dve.tensor_copy(mixT_b[:, k], mixT[:, k, :].unsqueeze(2).to_broadcast([P, B, P])))
            v.sync()

        with nc.Block() as block:
            @block.vector
            def _(dve):
                v = Steps(dve, own)
                dve.sem_inc(mix2, 1)
                dve.wait_ge(tp_done, 1)
                dve.tensor_copy(mixT[:], tiny_ps[:, 0:KD * B].rearrange("p (k b) -> p k b", k=KD)).then_inc(tp_copied, 1)
                dve.wait_ge(keys_done, 1)
                v(dve.reduce_max(small[0:B, 0:1], wide_ps[0:B, 0, :], AX.X))
                v(dve.tensor_scalar(small[0:B, 1:2], small[0:B, 0:1], -1.0, None, ALU.mult))
                dve.sem_inc(attn_done, 1)
                dve.wait_ge(exp_done, 1)
                v(dve.reciprocal(small[0:B, 3:4], small[0:B, 2:3]))
                v(dve.tensor_scalar(keys[:], keys[:], small[0:B, 3:4], None, ALU.mult))
                dve.sem_inc(attn_done, 1)
                dve.wait_ge(attnT_done, 1)
                v(dve.tensor_copy(mixT[:], tiny_ps[:, 0:KD * B].rearrange("p (k b) -> p k b", k=KD)))
                spread(v, dve)
                dve.sem_inc(spread_done, 1)
                dve.wait_ge(probe2_done, 1)
                v(dve.tensor_copy(value_probe[:], wide_ps[:]))
                first = v.n
                with dve.Fori(0, B) as b:
                    v = Steps(dve, own, b * 3 + first)
                    v(dve.tensor_tensor(prod[:], h[:, bass.ds(b * TB, TB), :],
                                        value_probe[:, bass.ds(b, 1), :].to_broadcast([P, TB, D]), ALU.mult))
                    v(dve.tensor_reduce(score[:, bass.ds(b * TB, TB)], prod[:], AX.X, ALU.add))
                    v(dve.tensor_reduce(peak[:, bass.ds(b, 1)], score[:, bass.ds(b * TB, TB)], AX.X, ALU.max))
                v = Steps(dve, own, first + 3 * B)
                dve.sem_inc(score_max, 1)
                dve.wait_ge(row_max, 1)
                v(dve.reduce_max(peak_row[:], tiny_ps[0:B, 128:256], AX.X))
                v(dve.tensor_scalar(peak_diag[:], g.ident[0:B, 0:B], peak_row[:], -1.0, ALU.mult, ALU.mult))
                dve.sem_inc(peak_ready, 1)
                dve.wait_ge(peak_done, 1)
                v(dve.tensor_copy(neg_peak[:], tiny_ps[:, 256:256 + B]))
                v(dve.tensor_tensor(tok[:], agent[:], agent[:], ALU.subtract))
                dve.sem_inc(neg_ready, 1)
                dve.wait_ge(score_exp, 1)
                v(dve.tensor_reduce(part_sum[:], score[:].rearrange("p (b t) -> p b t", b=B), AX.X, ALU.add))
                dve.sem_inc(sums_done, 1)
                with dve.Fori(0, B) as b:
                    dve.wait_ge(mix2, b + 1)
                    dve.tensor_tensor(masked[:, 0], score[:, bass.ds(b * TB, TB)].unsqueeze(2).to_broadcast([P, TB, B]),
                                      g.eye_b[:, bass.ds(b, 1), :].to_broadcast([P, TB, B]), ALU.mult).then_inc(masked2, 1)
                dve.wait_ge(mix2, B + 1)
                v(dve.tensor_reduce(mix[:], mix_ps[0:B].rearrange("p b d -> p d b"), AX.X, ALU.add))
                dve.sem_inc(sums_done, 1)
                dve.wait_ge(mixT2_done, 1)
                v(dve.tensor_copy(mixT[:], tiny_ps[:, 0:KD * B].rearrange("p (k b) -> p k b", k=KD)))
                v(dve.reciprocal(inv_sum[:], tiny_ps[:, 260:260 + B]))
                spread(v, dve)
                dve.sem_inc(spread2_done, 1)
                dve.wait_ge(tok_exp, 1)
                v(dve.reciprocal(score[:], tok[:]))
                v(dve.tensor_tensor(tok[:], tok[:], score[:], ALU.mult))
                dve.wait_ge(value_done, 1)
                for b in range(B):
                    v.mark(dve.scalar_tensor_tensor(gated[:, b, :], wide_ps[:, b, :], inv_sum[:, b:b + 1],
                                                    mod[:, b, GA, :], ALU.mult, ALU.mult))
                v.sync()
                with dve.Fori(0, B) as b:
                    for j in range(TB):
                        rows = g.x[:, bass.ds(b * TB + j, 1), :]
                        dve.scalar_tensor_tensor(rows, gated[:, bass.ds(b, 1), :], tok[:, bass.ds(b * TB + j, 1)], rows,
                                                 ALU.mult, ALU.add)

            @block.scalar
            def _(act):
                act.wait_ge(attn_done, 1)
                act.activation(keys[:], wide_ps[0:B, 0, :], ACT.Exp, bias=small[0:B, 1:2],
                               accum_out=small[0:B, 2:3]).then_inc(exp_done, 1)
                act.wait_ge(neg_ready, 1)
                for b in range(B):
                    last = act.activation(score[:, b * TB:(b + 1) * TB], score[:, b * TB:(b + 1) * TB], ACT.Exp,
                                          bias=neg_peak[:, b:b + 1])
                last.then_inc(score_exp, 1)
                act.activation(tok[:], tok[:], ACT.Exp).then_inc(tok_exp, 1)

            @block.tensor
            def _(pe):
                def mixT_of(rows, done):
                    for k in range(KD):
                        last = pe.transpose(tiny_ps[:, k * B:(k + 1) * B], rows[:, k * P:(k + 1) * P], g.ident[0:B, 0:B])
                    last.then_inc(done, 1)

                mixT_of(mix, tp_done)
                pe.wait_ge(tp_copied, 1)
                for k in range(KD):
                    last = pe.matmul(wide_ps[0:B, 0, :], mixT[:, k, :], wkT[:, k, :], start=(k == 0), stop=(k == KD - 1))
                last.then_inc(keys_done, 1)
                pe.wait_ge(attn_done, 2)
                mixT_of(keys, attnT_done)
                pe.wait_ge(spread_done, 1)
                for b in range(B):
                    for k in range(KD):
                        last = pe.matmul(wide_ps[:, b, :], mixT_b[:, k, b, :], g.wqkv[:, 4 + k, :],
                                         start=(k == 0), stop=(k == KD - 1))
                last.then_inc(probe2_done, 1)
                pe.wait_ge(score_max, 1)
                pe.transpose(tiny_ps[0:B, 128:256], peak[:], g.ident[:]).then_inc(row_max, 1)
                pe.wait_ge(peak_ready, 1)
                pe.matmul(tiny_ps[:, 256:256 + B], g.ones[0:B, :], peak_diag[:], start=True, stop=True).then_inc(peak_done, 1)
                pe.wait_ge(neg_ready, 1)
                pe.wait_ge(sums_done, 1)
                pe.matmul(tiny_ps[:, 260:260 + B], g.ones[:], part_sum[:], start=True, stop=True)
                with pe.Fori(0, B) as b:
                    pe.wait_ge(masked2, b + 1)
                    for j in range(TB):
                        last = pe.matmul(mix_ps[0:B, bass.ds(b, 1), :], masked[:, 0, j, :], h[:, bass.ds(b * TB + j, 1), :],
                                         start=(j == 0), stop=(j == TB - 1))
                    last.then_inc(mix2, 1)
                pe.wait_ge(sums_done, 2)
                mixT_of(mix, mixT2_done)
                pe.wait_ge(spread2_done, 1)
                for b in range(B):
                    for k in range(KD):
                        last = pe.matmul(wide_ps[:, b, :], mixT_b[:, k, b, :], wvT[:, k, :],
                                         start=(k == 0), stop=(k == KD - 1))
                last.then_inc(value_done, 1)


RING = 8
TOP = 8


def expert_choice(nc, mk, g, a):
    HALF = T // 2
    LOW = 64
    ROWS = LOW + E
    with ExitStack() as ctx:
        t = Maker(nc, ctx)
        w1 = t.sb("w1", [P, RING, S, KD, M])
        w2 = t.sb("w2", [P, RING, S, KD, KS])
        b2_row = t.sb("b2_row", [1, RING, D])
        b1T = t.sb("b1T", [P, E * S, KD])
        index = t.sb("index", [P, E], U32)
        weight = t.sb("weight", [P, E])
        h_dram = nc.dram_tensor("h_dram", (T, D), F32, kind="Internal").ap()
        sum_dram = nc.dram_tensor("sum_dram", (T, D), F32, kind="Internal").ap()
        w_in = [mk.sem(f"w_in{q}") for q in range(RING)]
        mod = g.modb[:].rearrange("p b (s d) -> p b s d", s=6)

        def load_expert(eng, e, q):
            eng.dma_start(w1[:, q], a["L0_ffn_W1"][bass.ds(e, 1)].rearrange("a s (p k) m -> p (a s) k m", k=KD)).then_inc(w_in[q], 16)
            eng.dma_start(w2[:, q], a["L0_ffn_W2"][bass.ds(e, 1)].rearrange("a s (p k) n -> p (a s) k n", k=KD)).then_inc(w_in[q], 16)
            eng.dma_start(b2_row[:, q, :], a["L0_ffn_b2"][bass.ds(e, 1)].rearrange("a s n -> a (s n)")).then_inc(w_in[q], 16)

        with ExitStack() as c2:
            r = Maker(nc, c2)
            logits = r.sb("logits", [ROWS, HALF])
            with ExitStack() as c3:
                t = Maker(nc, c3)
                hg = t.sb("hg", [P, 2, G, D])
                hT = t.sb("hT", [P, 2, KD, GT])
                wr = t.sb("wr", [E, D])
                wrT = t.sb("wrT", [P, KD, E])
                b1_rows = t.sb("b1_rows", [2 * E, 2, M])
                zero = t.sb("zero", [P, 2048])
                st, mv, var, rstd = (t.sb("st1", [P, G, 6]), t.sb("mv1", [P, G, 2]), t.sb("var1", [P, G]),
                                     t.sb("rstd1", [P, G]))
                tp = t.ps("tp1", [P, 2, KD, GT])
                lp = t.ps("lp1", [P, 2, GT])
                own, var_ready, rstd_ready, h_ready = (mk.sem("ec_dve"), mk.sem("ec_var"), mk.sem("ec_rstd"),
                                                       mk.sem("ec_h"))
                turned, hT_ready, logits_done, logits_out = (mk.sem("ec_turned"), mk.sem("ec_hT"), mk.sem("ec_logits"),
                                                             mk.sem("ec_logits_out"))
                normalised, scaled = mk.sem("ec_normalised"), mk.sem("ec_scaled")
                h_out = [mk.sem("ec_h_out0"), mk.sem("ec_h_out1")]
                small_in, zeroed, zero_out, wrT_done, wrT_copied = (mk.sem("ec_small_in"), mk.sem("ec_zeroed"),
                                                                    mk.sem("ec_zero_out"), mk.sem("ec_wrT"),
                                                                    mk.sem("ec_wrT_copied"))
                with nc.Block() as block:
                    @block.sync
                    def _(sp):
                        with sp.Fori(0, B) as b:
                            for k in range(2):
                                sp.wait_ge(h_ready, 2 * b + k + 1)
                                sp.dma_start(h_dram[bass.ds((2 * b + k) * GT, GT), :].rearrange("(t p) d -> p t d", p=P),
                                             hg[:, k]).then_inc(h_out[k], 16)
                        for k in range(2):
                            sp.wait_ge(h_out[k], 16 * (B + 1))

                    @block.scalar
                    def _(act):
                        act.dma_start(wr[:], a["L0_ffn_Wr"]).then_inc(small_in, 16)
                        act.dma_start(b1_rows[:], a["L0_ffn_b1"].rearrange("e s m -> (e s) m").rearrange("(i r) m -> r i m", i=2)).then_inc(small_in, 16)
                        act.wait_ge(zeroed, 2)
                        for i in range(4):
                            act.dma_start(sum_dram.rearrange("(i p r) d -> i p (r d)", i=4, p=P)[i], zero[:]).then_inc(zero_out, 16)
                        act.wait_ge(wrT_done, 1)
                        act.activation(wrT[:], lp[:, 0, 0:KD * E].rearrange("p (k e) -> p k e", k=KD), ACT.Copy).then_inc(wrT_copied, 1)
                        act.activation(b1T[:].rearrange("p (i r) k -> p k i r", i=2),
                                       tp[:, 1, 0, 0:2 * 2 * 2 * E].rearrange("p (k i r) -> p k i r", k=KD, i=2),
                                       ACT.Copy).then_inc(wrT_copied, 1)
                        for half in range(2):
                            with act.Fori(0, B // 2) as i:
                                for k in range(2):
                                    n = 2 * i + k + half * NG // 2
                                    act.wait_ge(turned, n + 1 + 2)
                                    act.activation(hT[:, k], tp[:, k], ACT.Copy).then_inc(hT_ready, 1)
                                    act.wait_ge(logits_done, n + 1)
                                    rows = slice(LOW * half, LOW * half + E)
                                    act.activation(logits[rows, bass.ds((2 * i + k) * GT, GT)], lp[rows, k, :],
                                                   ACT.Copy).then_inc(logits_out, 1)
                        act.wait_ge(zero_out, 64)

                    @block.gpsimd
                    def _(pool):
                        pool.memset(zero[:], 0.0).then_inc(zeroed, 1)
                        with pool.Fori(0, NG) as n:
                            pool.wait_ge(var_ready, n + 1)
                            rsqrt_rows(pool, rstd, var, g.minus_half, G, rstd_ready)
                            b = n // (NG // B)
                            rows = hg[:, bass.ds(n % 2, 1)].rearrange("p a t d -> p (a t) d")
                            pool.wait_ge(normalised, n + 1)
                            pool.tensor_tensor(rows, rows, mod[:, bass.ds(b, 1), CB, :].to_broadcast([P, G, D]), ALU.mult).then_inc(scaled, 1)
                            pool.wait_ge(scaled, n + 1)
                            pool.tensor_tensor(rows, rows, mod[:, bass.ds(b, 1), SB, :].to_broadcast([P, G, D]), ALU.add).then_inc(h_ready, 1)

                    @block.vector
                    def _(dve):
                        dve.memset(logits[32:64, :], LOWEST).then_inc(zeroed, 1)
                        dve.sem_inc(turned, 2)
                        dve.sem_inc(h_out[0], 16)
                        dve.sem_inc(h_out[1], 16)
                        per = 3 * G
                        with dve.Fori(0, B) as b:
                            for k in range(2):
                                v = Steps(dve, own, (2 * b + k) * per)
                                tile = lambda j: g.x[:, bass.ds(b * TB + k * G + j, 1), :]
                                layer_norm_stats(v, g.spare, st, mv, var, G, tile, LN_EPS, var_ready)
                                dve.wait_ge(rstd_ready, 2 * b + k + 1)
                                dve.wait_ge(h_out[k], 16 * (b + 1))
                                dve.wait_ge(turned, 2 * b + k + 1)
                                for j in range(G):
                                    v.mark(dve.tensor_scalar(hg[:, k, j:j + 1, :], tile(j), mv[:, j, 0:1], rstd[:, j:j + 1],
                                                             ALU.subtract, ALU.mult))
                                v.sync()
                                dve.sem_inc(normalised, 1)
                                assert v.n == per

                    @block.tensor
                    def _(pe):
                        pe.wait_ge(small_in, 32)
                        for k in range(KD):
                            pe.transpose(lp[:, 0, k * E:(k + 1) * E], wr[:, k * P:(k + 1) * P], g.ident[0:E, 0:E])
                            for i in range(2):
                                last = pe.transpose(tp[:, 1, 0, (2 * k + i) * 2 * E:(2 * k + i + 1) * 2 * E],
                                                    b1_rows[:, i, k::KD], g.ident[0:2 * E, 0:2 * E])
                        last.then_inc(wrT_done, 1)
                        pe.wait_ge(wrT_copied, 2)
                        for half in range(2):
                            with pe.Fori(0, B // 2) as i:
                                for k in range(2):
                                    n = 2 * i + k + half * NG // 2
                                    pe.wait_ge(h_ready, n + 1)
                                    for j in range(G):
                                        for c in range(KD):
                                            last = pe.transpose(tp[:, k, c, j * P:(j + 1) * P], hg[:, k, j, c * P:(c + 1) * P],
                                                                g.ident[:])
                                    last.then_inc(turned, 1)
                                    pe.wait_ge(hT_ready, n + 1)
                                    for c in range(KD):
                                        last = pe.matmul(lp[LOW * half:LOW * half + E, k, :], wrT[:, c, :], hT[:, k, c, :],
                                                         start=(c == 0), stop=(c == KD - 1))
                                    last.then_inc(logits_done, 1)

            with ExitStack() as c3:
                t = Maker(nc, c3)
                top = t.sb("top", [ROWS, CAP])
                at = t.sb("at", [ROWS, CAP], U32)
                at_f = t.sb("at_f", [ROWS, CAP])
                both = t.sb("both", [P, 2, ROWS])
                rank0 = t.sb("rank0", [P, P])
                low = t.sb("low", [P, 2, E])
                take, best, chosen = t.sb("take", [P, E]), t.sb("best", [P, E]), t.sb("chosen", [P, E])
                rank_ps, low_ps, peak_ps, sum_ps = (t.ps("rank_ps", [P, 512]), t.ps("low_ps", [P, 512]),
                                                    t.ps("peak_ps", [P, 512]), t.ps("sum_ps", [P, 512]))
                own, found, ranked, copied, lowered, expd, expd_done, summed, row0 = (
                    mk.sem("top_dve"), mk.sem("top_found"), mk.sem("top_ranked"), mk.sem("top_copied"), mk.sem("top_lowered"),
                    mk.sem("top_shifted"), mk.sem("top_exp"), mk.sem("top_sum"), mk.sem("top_rank0"))
                with nc.Block() as block:
                    @block.sync
                    def _(sp):
                        for e in range(RING):
                            load_expert(sp, e, e)

                    @block.gpsimd
                    def _(pool):
                        pool.memset(rank0[:], 0.0).then_inc(row0, 1)
                        pool.wait_ge(row0, 1)
                        pool.memset(rank0[0:1, :], 1.0).then_inc(row0, 1)

                    @block.vector
                    def _(dve):
                        v = Steps(dve, own)
                        for n in range(CAP // TOP):
                            cols = slice(n * TOP, (n + 1) * TOP)
                            v(dve.max(top[:, cols], logits[:]))
                            v(dve.max_index(at[:, cols], top[:, cols], logits[:]))
                            if n < CAP // TOP - 1:
                                v(dve.match_replace(logits[:], top[:, cols], logits[:], LOWEST))
                        v(dve.tensor_copy(at_f[:], at[:]))
                        v(dve.tensor_scalar(at_f[LOW:ROWS, :], at_f[LOW:ROWS, :], float(HALF), None, ALU.add))
                        dve.sem_inc(found, 1)
                        dve.wait_ge(ranked, 1)
                        v(dve.tensor_copy(both[:], rank_ps[:, 0:2 * ROWS].rearrange("p (i r) -> p i r", i=2)))
                        dve.sem_inc(copied, 1)
                        dve.wait_ge(lowered, 1)
                        v(dve.tensor_copy(low[:], low_ps[:, 0:2 * E].rearrange("p (i e) -> p i e", i=2)))
                        v(dve.tensor_tensor(take[:], both[:, 0, 0:E], low[:, 0, :], ALU.is_ge))
                        v(dve.tensor_tensor(best[:], both[:, 0, 0:E], low[:, 0, :], ALU.max))
                        v(dve.tensor_tensor(chosen[:], both[:, 1, 0:E], low[:, 1, :], ALU.subtract))
                        v(dve.tensor_tensor(chosen[:], chosen[:], take[:], ALU.mult))
                        v(dve.tensor_tensor(chosen[:], chosen[:], low[:, 1, :], ALU.add))
                        v(dve.tensor_copy(index[:], chosen[:]))
                        v(dve.tensor_copy(take[:], peak_ps[:, 0:E]))
                        v(dve.tensor_tensor(take[:], take[:], peak_ps[:, E:2 * E], ALU.max))
                        v(dve.tensor_tensor(best[:], best[:], take[:], ALU.subtract))
                        dve.sem_inc(expd, 1)
                        dve.wait_ge(summed, 1)
                        v(dve.reciprocal(take[:], sum_ps[:, 0:E]))
                        v(dve.tensor_tensor(weight[:], best[:], take[:], ALU.mult))

                    @block.scalar
                    def _(act):
                        act.wait_ge(expd, 1)
                        act.activation(best[:], best[:], ACT.Exp).then_inc(expd_done, 1)

                    @block.tensor
                    def _(pe):
                        pe.wait_ge(found, 1)
                        pe.transpose(rank_ps[:, 0:ROWS], top[:], g.ident[0:ROWS, 0:ROWS])
                        pe.transpose(rank_ps[:, ROWS:2 * ROWS], at_f[:], g.ident[0:ROWS, 0:ROWS]).then_inc(ranked, 1)
                        pe.wait_ge(copied, 1)
                        pe.wait_ge(row0, 2)
                        pe.matmul(peak_ps[:, 0:E], rank0[:], both[:, 0, 0:E], start=True, stop=True)
                        pe.matmul(peak_ps[:, E:2 * E], rank0[:], both[:, 0, LOW:ROWS], start=True, stop=True)
                        pe.matmul(low_ps[:, 0:E], g.flip[:], both[:, 0, LOW:ROWS], start=True, stop=True)
                        pe.matmul(low_ps[:, E:2 * E], g.flip[:], both[:, 1, LOW:ROWS], start=True, stop=True).then_inc(lowered, 1)
                        pe.wait_ge(expd_done, 1)
                        pe.matmul(sum_ps[:, 0:E], g.ones[:], best[:], start=True, stop=True).then_inc(summed, 1)

        with ExitStack() as c2:
            t = Maker(nc, c2)
            XG = 8
            slot = t.sb("slot", [P, XG, 1], U32)
            xg = t.sb("xg", [P, XG, D])
            xT = t.sb("xT", [P, 2, KD, P])
            pre = t.sb("pre", [P, 2, S * KD, P])
            act_h = t.sb("act_h", [P, 2, S * KD, P])
            y = t.sb("y", [P, 2, D])
            x_ps = t.ps("x_ps", [P, 2, 512])
            h_ps = t.ps("h_ps", [P, 2, S * KD, P])
            y_ps = t.ps("y_ps", [P, 2, 512])
            xg_in = [mk.sem(f"xg_in{q}") for q in range(XG)]
            slot_set, turned, xT_ready, up_done, biased, gelu_done, down_done, y_ready, added = (
                mk.sem("slot_set"), mk.sem("xg_turned"), mk.sem("xT_ready"), mk.sem("up_done"), mk.sem("biased"),
                mk.sem("gelu_done"), mk.sem("down_done"), mk.sem("y_ready"), mk.sem("added"))
            carried, y_free = mk.sem("pool_carried"), mk.sem("y_free")
            LAST = E // RING - 1

            def bodies(eng, body):
                with eng.Fori(0, LAST) as i:
                    for q in range(RING):
                        body(i * RING + q, q, False)
                for q in range(RING):
                    body(LAST * RING + q, q, True)

            with nc.Block() as block:
                @block.sync
                def _(sp):
                    with sp.Fori(0, LAST) as i:
                        for q in range(RING):
                            e = i * RING + q
                            sp.wait_ge(down_done, e + 1)
                            load_expert(sp, e + RING, q)

                @block.gpsimd
                def _(pool):
                    def carry_wait(n):
                        pool.wait_ge(carried, n + 1)
                        pool.tensor_tensor(g.pool_spare[:], g.minus_half[:, 0:1], g.minus_half[:, 0:1],
                                           ALU.add).then_inc(carried, 1)

                    def gather(e, q, n):
                        pool.tensor_copy(slot[:, q], index[:, bass.ds(e, 1)]).then_inc(slot_set, 1)
                        pool.wait_ge(slot_set, e + 1)
                        carry_wait(n)
                        pool.indirect_dma_start(out=xg[:, q, :], out_offset=None, in_=h_dram,
                                                in_offset=bass.IndirectOffsetOnAxis(ap=slot[:, q], axis=0)).then_inc(xg_in[q], 16)

                    pool.sem_inc(carried, 1)
                    pool.sem_inc(y_free, 2)
                    pool.sem_inc(turned, 1)
                    for e in range(XG - 1):
                        gather(e, e, e)

                    def body(e, q, last):
                        pool.wait_ge(y_ready, e + 1)
                        carry_wait(XG - 1 + 2 * e - (max(0, q + XG - 1 - RING) if last else 0))
                        pool.indirect_dma_start(out=sum_dram, out_offset=bass.IndirectOffsetOnAxis(ap=slot[:, q % XG], axis=0),
                                                in_=y[:, q % 2, :], in_offset=None, compute_op=ALU.add).then_inc(added, 16)
                        if not last or q + XG - 1 < RING:
                            pool.wait_ge(turned, e + 1)
                            gather(e + XG - 1, (q + XG - 1) % XG, XG + 2 * e)
                        pool.wait_ge(added, 16 * (e + 1))
                        pool.sem_inc(y_free, 1)

                    bodies(pool, body)
                    pool.wait_ge(added, 16 * E)

                @block.scalar
                def _(act):
                    def x_copy(e, q):
                        act.wait_ge(turned, e + 2)
                        act.activation(xT[:, q % 2], x_ps[:, q % 2, 0:D].rearrange("p (k n) -> p k n", k=KD), ACT.Copy).then_inc(xT_ready, 1)

                    x_copy(0, 0)

                    def body(e, q, last):
                        if not last or q + 1 < RING:
                            x_copy(e + 1, q + 1)
                        act.wait_ge(biased, e + 1)
                        act.activation(act_h[:, q % 2], pre[:, q % 2], ACT.Gelu).then_inc(gelu_done, 1)

                    bodies(act, body)

                @block.vector
                def _(dve):
                    def bias(e, q):
                        dve.wait_ge(up_done, e + 1)
                        dve.tensor_tensor(pre[:, q % 2], h_ps[:, q % 2],
                                          b1T[:, bass.ds(e * S, S), :].rearrange("p s k -> p (s k)").unsqueeze(2)
                                          .to_broadcast([P, S * KD, P]), ALU.add).then_inc(biased, 1)

                    bias(0, 0)

                    def body(e, q, last):
                        if not last or q + 1 < RING:
                            bias(e + 1, q + 1)
                        dve.wait_ge(down_done, e + 1)
                        dve.wait_ge(y_free, e + 1)
                        dve.tensor_scalar(y[:, q % 2, :], y_ps[:, q % 2, 0:D], weight[:, bass.ds(e, 1)], None,
                                          ALU.mult).then_inc(y_ready, 1)

                    bodies(dve, body)

                @block.tensor
                def _(pe):
                    def turn(e, q):
                        pe.wait_ge(xg_in[q % XG], 16 * (q // XG + 1) + (e - q) * (16 // XG))
                        for k in range(KD):
                            last = pe.transpose(x_ps[:, q % 2, k * P:(k + 1) * P], xg[:, q % XG, k::KD], g.ident[:])
                        last.then_inc(turned, 1)

                    def up(e, q):
                        pe.wait_ge(w_in[q], 48 + (e - q) * (48 // RING))
                        pe.wait_ge(xT_ready, e + 1)
                        for s in range(S):
                            for c in range(KD):
                                for k in range(KD):
                                    last = pe.matmul(h_ps[:, q % 2, s * KD + c, :], w1[:, q, s, k, c::KD], xT[:, q % 2, k, :],
                                                     start=(k == 0), stop=(k == KD - 1))
                        last.then_inc(up_done, 1)

                    def down(e, q):
                        pe.wait_ge(gelu_done, e + 1)
                        for s in range(S):
                            cols = slice(s * KS, (s + 1) * KS)
                            for c in range(KD):
                                pe.matmul(y_ps[:, q % 2, cols], act_h[:, q % 2, s * KD + c, :], w2[:, q, s, c, :],
                                          start=(c == 0), stop=False)
                            last = pe.matmul(y_ps[:, q % 2, cols], g.ones[0:1, :], b2_row[:, q, cols], start=False, stop=True)
                        last.then_inc(down_done, 1)

                    turn(0, 0)
                    up(0, 0)
                    turn(1, 1)

                    def body(e, q, last):
                        if not last or q + 1 < RING:
                            up(e + 1, (q + 1) % RING)
                        if not last or q + 2 < RING:
                            turn(e + 2, (q + 2) % RING)
                        down(e, q)

                    bodies(pe, body)

        with ExitStack() as c2:
            t = Maker(nc, c2)
            part = t.sb("part", [P, 2, G, D])
            part_in = [mk.sem("part_in0"), mk.sem("part_in1")]
            used, own = mk.sem("part_used"), mk.sem("part_dve")
            with nc.Block() as block:
                @block.sync
                def _(sp):
                    sp.sem_inc(used, 2)
                    with sp.Fori(0, B) as b:
                        for k in range(2):
                            sp.wait_ge(used, 2 * b + k + 1)
                            sp.dma_start(part[:, k], sum_dram[bass.ds((2 * b + k) * GT, GT), :]
                                         .rearrange("(t p) d -> p t d", p=P)).then_inc(part_in[k], 16)

                @block.vector
                def _(dve):
                    with dve.Fori(0, B) as b:
                        for k in range(2):
                            v = Steps(dve, own, 2 * b + k)
                            dve.wait_ge(part_in[k], 16 * (b + 1))
                            v(dve.tensor_tensor(part[:, k], part[:, k], mod[:, bass.ds(b, 1), GB, :].to_broadcast([P, G, D]), ALU.mult))
                            rows = g.x[:, bass.ds(b * TB + k * G, G), :]
                            dve.tensor_tensor(rows, rows, part[:, k], ALU.add).then_inc(used, 1)
        mk.clear_signals()


def project_heads(pe, ring, rows, wide, ident, w, full, free, uses, before=None):
    def take(i):
        if i < 2 and before:
            before(i)
        pe.wait_ge(free, uses + i + 1)

    for c in range(KD):
        take(c)
        for j in range(G):
            last = pe.transpose(ring[:, c, j * P:(j + 1) * P], rows[:, j, c * P:(c + 1) * P], ident)
        last.then_inc(full, 1)
    pe.wait_ge(free, uses + KD + 2)
    for c in range(CH):
        take(KD + c)
        for k in range(KD):
            last = pe.matmul(ring[:, c % 2, :], w[:, k, c * P:(c + 1) * P], wide[:, k, :], start=(k == 0), stop=(k == KD - 1))
        last.then_inc(full, 1)


def copy_heads(act, ring, turned, scaled, full, full_uses, free):
    for c in range(KD):
        act.wait_ge(full, full_uses + c + 1)
        act.activation(turned[:, c, :], ring[:, c, :], ACT.Copy).then_inc(free, 1)
    for c in range(CH):
        act.wait_ge(full, full_uses + KD + c + 1)
        act.activation(scaled[:, c, :], ring[:, c % 2, :], ACT.Copy, scale=DN).then_inc(free, 1)


def square_heads(pool, scaled, squares, free, uses, squared):
    for c in range(CH):
        pool.wait_ge(free, uses + KD + c + 1 + 2)
        pool.tensor_tensor(squares[:, c, :], scaled[:, c, :], scaled[:, c, :], ALU.mult).then_inc(squared, 1)


def random_features(pe, dash, diag, scaled, squares, j, features, half_heads):
    for c in range(CH):
        pe.matmul(dash[:, c * P:(c + 1) * P], scaled[:, c, j * P:(j + 1) * P], features, start=True, stop=True)
    for c in range(CH):
        last = pe.matmul(diag[:, 2 * c:2 * c + 2], squares[:, c, j * P:(j + 1) * P], half_heads, start=True, stop=True)
    return last


def performer(nc, mk, g, a):
    USES = KD + CH
    with ExitStack() as ctx:
        t = Maker(nc, ctx)
        h_dram = nc.dram_tensor("h1_dram", (T, D), F32, kind="Internal").ap()
        y_dram = nc.dram_tensor("y1_dram", (T, D), F32, kind="Internal").ap()
        kv_out = t.sb("kv_out", [P, B, CH, D])
        wide = t.sb("wide", [P, TB, HD])
        k_dash, ksum, q_dash, qn = wide, wide[:, 0:B, :], wide[:, B:B + 2, :], wide[:, B + 2:B + 4, :]
        features = t.sb("features", [P, P])
        half_heads = t.sb("half_heads", [P, 2])
        mod = g.modb[:].rearrange("p b (s d) -> p b s d", s=6)
        wide_in = mk.sem("pf_weights_in")

        with ExitStack() as c1:
            r = Maker(nc, c1)
            wo, wv = r.sb("wo", [P, CH, D]), r.sb("wv", [P, KD, HD])
            a_sum = kv_out
            k_sum = r.sb("k_sum", [P, B, CH])
            h_sum = r.sb("h_sum", [P, B, D + 1])
            peak = r.sb("key_peak", [P, B])
            with ExitStack() as c2:
                t = Maker(nc, c2)
                RING = 4
                hk = t.sb("hk", [P, RING, G, D + 1])
                hT = t.sb("hkT", [P, KD, GT])
                kT, k2 = t.sb("kT", [P, CH, GT]), t.sb("k2", [P, CH, GT])
                dash = k_dash
                wk = t.sb("wk", [P, KD, HD])
                proj2 = t.sb("proj2", [MF, 2, DH])
                half_diag = t.sb("k_half_diag", [P, 2, H])
                row_peak, tile_peak = t.sb("row_peak", [P, G]), t.sb("tile_peak", [P, 1])
                neg_peak, ratio = t.sb("neg_peak1", [P, 1]), t.sb("ratio", [P, 1])
                st, mv, var, rstd = (t.sb("st2", [P, G, 6]), t.sb("mv2", [P, G, 2]), t.sb("var2", [P, G]),
                                     t.sb("rstd2", [P, G]))
                ring = t.ps("k_ring", [P, 2, 512])
                dash_ps = t.ps("k_dash_ps", [P, 2, HD])
                diag_ps = t.ps("k_diag_ps", [P, 512])
                h_sum_ps = t.ps("h_sum_ps", [P, 512])
                own, var_ready, rstd_ready, h_ready = mk.sem("pk_dve"), mk.sem("pk_var"), mk.sem("pk_rstd"), mk.sem("pk_h")
                full, free, dash_done, dash_used, diag_copied = (mk.sem("k_full"), mk.sem("k_free"), mk.sem("k_dash_done"),
                                                                 mk.sem("k_dash_used"), mk.sem("k_diag_copied"))
                h_out = [mk.sem(f"h1_out{i}") for i in range(RING)]
                mod_in, wk_in, proj_done, const_done = mk.sem("mod1_in"), mk.sem("wk_in"), mk.sem("proj_turned"), mk.sem("pk_const")
                squared, carried, sums_done, sums_used = (mk.sem("k_squared"), mk.sem("pk_carried"), mk.sem("k_sums_done"),
                                                          mk.sem("k_sums_used"))
                peak_part, peak_all, neg_ready, exp_done, h_sum_done, h_sum_used = (
                    mk.sem("peak_part"), mk.sem("peak_all"), mk.sem("neg_peak_ready"), mk.sem("k_exp"), mk.sem("h_sum_done"),
                    mk.sem("h_sum_used"))
                TURNS = NG // RING

                def groups(eng, body):
                    with eng.Fori(0, TURNS - 1) as r:
                        for i in range(RING):
                            body(r * RING + i, i, r, False)
                    for i in range(RING):
                        body((TURNS - 1) * RING + i, i, TURNS - 1, True)

                with nc.Block() as block:
                    @block.sync
                    def _(sp):
                        sp.dma_start(g.modb[:], g.mod_dram[1].partition_broadcast(P)).then_inc(mod_in, 16)
                        for k in range(2):
                            sp.dma_start(proj2[:, k, :], a["L1_attn_proj"]).then_inc(wk_in, 16)
                        for dst, name in ((wk, "Wk"), (wv, "Wv")):
                            sp.dma_start(dst[:], a[f"L1_attn_{name}"].rearrange("(k p) h d -> p k (h d)", p=P)
                                         ).then_inc(wk_in if name == "Wk" else wide_in, 16)
                        sp.dma_start(wo[:], a["L1_attn_Wo"].rearrange("h d o -> (h d) o").rearrange("(c p) o -> p c o", p=P)).then_inc(wide_in, 16)
                        with sp.Fori(0, TURNS) as r:
                            for i in range(RING):
                                n = r * RING + i
                                sp.wait_ge(h_ready, n + 1)
                                sp.dma_start(h_dram[bass.ds(n * GT, GT), :].rearrange("(t p) d -> p t d", p=P),
                                             hk[:, i, :, 0:D]).then_inc(h_out[i], 16)
                        for i in range(RING):
                            sp.wait_ge(h_out[i], 16 * (TURNS + 1))
                        sp.wait_ge(wide_in, 32)

                    @block.gpsimd
                    def _(pool):
                        def power(n):
                            pool.wait_ge(var_ready, n + 1)
                            rsqrt_rows(pool, rstd, var, g.minus_half, G, rstd_ready)

                        def keys(n):
                            square_heads(pool, kT, k2, free, n * USES, squared)
                            pool.wait_ge(carried, n + 1)
                            pool.wait_ge(peak_part, n + 1)
                            pool.tensor_tensor(g.pool_spare[:], tile_peak[:], tile_peak[:], ALU.add).then_inc(carried, 1)
                            pool.partition_all_reduce(g.pool_max[:], tile_peak[:], P, bass.bass_isa.ReduceOp.max).then_inc(peak_all, 1)

                        pool.sem_inc(carried, 1)
                        power(0)
                        power(1)
                        keys(0)

                        def body(n, i, r, last):
                            if not last or i + 2 < RING:
                                power(n + 2)
                            if not last or i + 1 < RING:
                                keys(n + 1)

                        groups(pool, body)

                    @block.vector
                    def _(dve):
                        v = Steps(dve, own)
                        dve.sem_inc(dash_used, 2)
                        dve.sem_inc(sums_used, 2)
                        dve.sem_inc(h_sum_used, 1)
                        for i in range(RING):
                            dve.sem_inc(h_out[i], 16)
                        v.mark(dve.memset(features[:], 0.0))
                        v.mark(dve.memset(half_heads[:], 0.0))
                        v.mark(dve.memset(hk[:].rearrange("p i t d -> p (i t) d")[:, :, D:D + 1], 1.0))
                        v.sync()
                        v.mark(dve.memset(half_heads[0:DH, 0:1], 0.5))
                        v.mark(dve.memset(half_heads[DH:P, 1:2], 0.5))
                        dve.wait_ge(proj_done, 1)
                        for i in range(2):
                            at = slice(i * DH, (i + 1) * DH)
                            v.mark(dve.tensor_copy(features[at, i * MF:(i + 1) * MF], ring[at, 0, 0:MF]))
                        v.sync()
                        dve.sem_inc(const_done, 1)
                        dve.wait_ge(mod_in, 16)

                        def prepare(v, n, i, r, b):
                            tile = lambda j: g.x[:, bass.ds(n * G + j, 1), :]
                            layer_norm_stats(v, g.spare, st, mv, var, G, tile, LN_EPS, var_ready)
                            dve.wait_ge(rstd_ready, n + 1)
                            dve.wait_ge(h_out[i], 16 * (r + 1))
                            for j in range(G):
                                v.mark(dve.tensor_scalar(hk[:, i, j:j + 1, 0:D], tile(j), mv[:, j, 0:1], rstd[:, j:j + 1],
                                                         ALU.subtract, ALU.mult))
                            v.sync()
                            rows = hk[:, i, :, 0:D]
                            v(dve.tensor_tensor(rows, rows, mod[:, bass.ds(b, 1), CA, :].to_broadcast([P, G, D]), ALU.mult))
                            dve.tensor_tensor(rows, rows, mod[:, bass.ds(b, 1), SA, :].to_broadcast([P, G, D]),
                                              ALU.add).then_inc(h_ready, 1)

                        def shift(v, n, k):
                            for j in range(G):
                                dve.wait_ge(diag_copied, n * G + j + 2)
                                v.mark(dve.reduce_max(row_peak[:, j:j + 1], dash_ps[:, j % 2, :], AX.X))
                                v.mark(dve.tensor_tensor(dash[:, k * G + j, :].rearrange("p (h m) -> p h m", h=H),
                                                         dash_ps[:, j % 2, :].rearrange("p (h m) -> p h m", h=H),
                                                         half_diag[:, j % 2, :].unsqueeze(2).to_broadcast([P, H, MF]), ALU.subtract))
                                v.sync()
                                dve.sem_inc(dash_used, 1)
                            v(dve.reduce_max(tile_peak[:], row_peak[:], AX.X))
                            dve.sem_inc(peak_part, 1)

                        def refer(v, n, k, b):
                            so_far = peak[:, bass.ds(b, 1)]
                            dve.wait_ge(peak_all, n + 1)
                            if k == 0:
                                v(dve.tensor_copy(so_far, g.pool_max[:]))
                            else:
                                v(dve.tensor_copy(neg_peak[:], so_far))
                                v(dve.tensor_tensor(so_far, so_far, g.pool_max[:], ALU.max))
                                v(dve.tensor_tensor(ratio[:], neg_peak[:], so_far, ALU.subtract))
                            dve.tensor_scalar(neg_peak[:], so_far, -1.0, None, ALU.mult).then_inc(neg_ready, 1)

                        def add_sums(v, n, k, b, ref=None):
                            for c in range(CH):
                                if c == 2 and ref:
                                    ref()
                                a_out = a_sum[:, bass.ds(b, 1), c, :]
                                k_out = k_sum[:, bass.ds(b, 1), c:c + 1]
                                a_in, k_in = ring[:, c % 2, 0:D].unsqueeze(1), ring[:, c % 2, D:D + 1].unsqueeze(1)
                                dve.wait_ge(sums_done, n * CH + c + 1)
                                if k == 0:
                                    v.mark(dve.tensor_copy(a_out, a_in))
                                    v.mark(dve.tensor_copy(k_out, k_in))
                                else:
                                    v.mark(dve.scalar_tensor_tensor(a_out, a_out, ratio[:], a_in, ALU.mult, ALU.add))
                                    v.mark(dve.scalar_tensor_tensor(k_out, k_out, ratio[:], k_in, ALU.mult, ALU.add))
                                v.sync()
                                dve.sem_inc(sums_used, 1)
                            if k:
                                dve.wait_ge(h_sum_done, b + 1)
                                v(dve.tensor_copy(h_sum[:, bass.ds(b, 1), :], h_sum_ps[:, 0:D + 1].unsqueeze(1)))
                                dve.sem_inc(h_sum_used, 1)

                        prepare(v, 0, 0, 0, 0)
                        prepare(v, 1, 1, 0, 0)
                        shift(v, 0, 0)
                        refer(v, 0, 0, 0)
                        first = v.n
                        PREP, SHIFT, SUMS = 3 * G + 1, 2 * G + 1, 2 * CH
                        per = RING * (PREP + SHIFT + SUMS) + RING // 2 * (1 + 3 + 1)

                        def body(n, i, r, last):
                            b = r * (RING // 2) + i // 2
                            if i == 0:
                                v.start(r * per + first)
                            if not last or i + 2 < RING:
                                prepare(v, n + 2, (i + 2) % RING, r + (i + 2) // RING, b + 1)
                            more = not last or i + 1 < RING
                            if more:
                                shift(v, n + 1, (i + 1) % 2)
                            add_sums(v, n, i % 2, b, (lambda: refer(v, n + 1, (i + 1) % 2, b + i % 2)) if more else None)
                            assert last or i < RING - 1 or v.n == per, (v.n, per)

                        groups(dve, body)

                    @block.scalar
                    def _(act):
                        act.sem_inc(free, 2)
                        act.sem_inc(diag_copied, 1)

                        def heads(n):
                            copy_heads(act, ring, hT, kT, full, n * USES, free)
                            for j in range(G):
                                act.wait_ge(dash_done, n * G + j + 1)
                                act.activation(half_diag[:, j % 2, :], diag_ps[:, 0:H], ACT.Copy).then_inc(diag_copied, 1)

                        def exps(n, k):
                            act.wait_ge(neg_ready, n + 1)
                            if k:
                                act.activation(ratio[:], ratio[:], ACT.Exp)
                            for j in range(k * G, k * G + G):
                                last = act.activation(dash[:, j, :], dash[:, j, :], ACT.Exp, bias=neg_peak[:])
                            last.then_inc(exp_done, 1)

                        heads(0)
                        exps(0, 0)

                        def body(n, i, r, last):
                            if not last or i + 1 < RING:
                                heads(n + 1)
                                exps(n + 1, (i + 1) % 2)

                        groups(act, body)

                    @block.tensor
                    def _(pe):
                        pe.wait_ge(wk_in, 48)
                        pe.transpose(ring[:, 0, 0:MF], proj2[:].rearrange("m i d -> m (i d)"), g.ident[0:MF, 0:MF]).then_inc(proj_done, 1)
                        pe.wait_ge(const_done, 1)

                        def keys(n, i, before):
                            pe.wait_ge(h_ready, n + 1)
                            project_heads(pe, ring, hk[:, i], hT, g.ident[:], wk, full, free, n * USES, before)
                            pe.wait_ge(free, (n + 1) * USES + 2)
                            pe.wait_ge(squared, (n + 1) * CH)
                            for j in range(G):
                                pe.wait_ge(dash_used, n * G + j + 1)
                                pe.wait_ge(diag_copied, n * G + j + 1)
                                random_features(pe, dash_ps[:, j % 2], diag_ps, kT, k2, j, features[:],
                                                half_heads[:]).then_inc(dash_done, 1)

                        def sums(n, i, b, alone):
                            k = i % 2
                            pe.wait_ge(exp_done, n + 1)
                            if k == 0:
                                pe.wait_ge(h_sum_used, b + 1)
                            for c in range(CH):
                                if c < 2 and not alone:
                                    pe.wait_ge(free, (n + 1) * USES + CH + c + 1 + 2)
                                else:
                                    pe.wait_ge(sums_used, n * CH + c + 1)
                                for j in range(G):
                                    last = pe.matmul(ring[:, c % 2, 0:D + 1], dash[:, k * G + j, c * P:(c + 1) * P], hk[:, i, j, :],
                                                     start=(j == 0), stop=(j == G - 1))
                                last.then_inc(sums_done, 1)
                            for j in range(G):
                                last = pe.matmul(h_sum_ps[:, 0:D + 1], g.ones[:], hk[:, i, j, :],
                                                 start=(k == 0 and j == 0), stop=(k == 1 and j == G - 1))
                            if k:
                                last.then_inc(h_sum_done, 1)

                        keys(0, 0, None)

                        def body(n, i, r, last):
                            more = not last or i + 1 < RING
                            if more:
                                keys(n + 1, (i + 1) % RING, lambda c: pe.wait_ge(sums_used, n * CH + c + 1))
                            sums(n, i, r * (RING // 2) + i // 2, not more)

                        groups(pe, body)

            with ExitStack() as c2:
                t = Maker(nc, c2)
                sums = t.sb("sums", [P, CH, D])
                sumsT = t.sb("sumsT", [P, CH, KD, P])
                h_eps, k_col, k_diag = t.sb("h_eps", [P, D + 1]), t.sb("k_col", [P, CH]), t.sb("k_diag", [P, CH, P])
                kv = t.sb("kv", [P, CH, P])
                common, alpha = t.sb("common", [P, 1]), t.sb("alpha", [P, B])
                big_ps = t.ps("big_ps", [P, CH, KD, P])
                kv_ps = t.ps("kv_ps", [P, CH, P])
                ks_ps = t.ps("ks_ps", [P, CH, P])
                own, alpha_in, alpha_done, sums_ready, turned, turned_out, kv_done, kv_ready, out_done, out_copied = (
                    mk.sem("kc_dve"), mk.sem("alpha_in"), mk.sem("alpha_done"), mk.sem("kc_sums"), mk.sem("kc_turned"),
                    mk.sem("kc_turned_out"), mk.sem("kc_kv_done"), mk.sem("kc_kv_ready"), mk.sem("kc_out_done"),
                    mk.sem("kc_out_copied"))
                diag_ready, ks_done, ks_copied = mk.sem("kc_diag"), mk.sem("kc_ks_done"), mk.sem("kc_ks_copied")
                with nc.Block() as block:
                    @block.vector
                    def _(dve):
                        v = Steps(dve, own)
                        v.mark(dve.memset(kv[:], 0.0))
                        v(dve.reduce_max(common[:], peak[:], AX.X))
                        v(dve.tensor_scalar(alpha[:], peak[:], common[:], None, ALU.subtract))
                        dve.sem_inc(alpha_in, 1)
                        dve.wait_ge(alpha_done, 1)
                        first, per = v.n, 7
                        with dve.Fori(0, B) as b:
                            v = Steps(dve, own, b * per + first)
                            scale = alpha[:, bass.ds(b, 1)]
                            v.mark(dve.tensor_scalar(h_eps[:], h_sum[:, bass.ds(b, 1), :].rearrange("p a d -> p (a d)"), KERN_EPS,
                                                     None, ALU.mult))
                            v.mark(dve.tensor_scalar(sums[:], a_sum[:, bass.ds(b, 1)].rearrange("p a c d -> p (a c) d"), scale, None, ALU.mult))
                            v.mark(dve.tensor_scalar(k_col[:], k_sum[:, bass.ds(b, 1), :].rearrange("p a c -> p (a c)"), scale, None, ALU.mult))
                            v.sync()
                            v.mark(dve.tensor_tensor(sums[:], sums[:], h_eps[:, 0:D].unsqueeze(1).to_broadcast([P, CH, D]), ALU.add))
                            v.mark(dve.tensor_scalar(k_col[:], k_col[:], h_eps[:, D:D + 1], None, ALU.add))
                            v.sync()
                            dve.sem_inc(sums_ready, 1)
                            v(dve.tensor_tensor(k_diag[:], g.ident[:].unsqueeze(1).to_broadcast([P, CH, P]),
                                                k_col[:].unsqueeze(2).to_broadcast([P, CH, P]), ALU.mult))
                            dve.sem_inc(diag_ready, 1)
                            dve.wait_ge(turned, b + 1)
                            dve.tensor_copy(sumsT[:, CH // 2:], big_ps[:, CH // 2:]).then_inc(turned_out, 1)
                            dve.wait_ge(kv_done, b + 1)
                            dve.tensor_copy(kv[DH:P, :, MF:P], kv_ps[DH:P, :, MF:P]).then_inc(kv_ready, 1)
                            dve.wait_ge(ks_done, b + 1)
                            v(dve.tensor_copy(ksum[:, bass.ds(b, 1), :].rearrange("p a n -> p (a n)"), ks_ps[:].rearrange("p c n -> p (c n)")))
                            dve.wait_ge(out_done, b + 1)
                            dve.tensor_copy(kv_out[:, bass.ds(b, 1), CH // 2:, :].rearrange("p a c n -> p (a c n)"),
                                            big_ps[:, CH // 2:].rearrange("p c k n -> p (c k n)")).then_inc(out_copied, 1)
                            assert v.n == per, v.n

                    @block.scalar
                    def _(act):
                        act.wait_ge(alpha_in, 1)
                        act.activation(alpha[:], alpha[:], ACT.Exp).then_inc(alpha_done, 1)
                        with act.Fori(0, B) as b:
                            act.wait_ge(turned, b + 1)
                            act.activation(sumsT[:, 0:CH // 2], big_ps[:, 0:CH // 2], ACT.Copy).then_inc(turned_out, 1)
                            act.wait_ge(kv_done, b + 1)
                            act.activation(kv[0:DH, :, 0:MF], kv_ps[0:DH, :, 0:MF], ACT.Copy).then_inc(kv_ready, 1)
                            act.wait_ge(out_done, b + 1)
                            act.activation(kv_out[:, bass.ds(b, 1), 0:CH // 2, :].rearrange("p a c n -> p (a c n)"),
                                           big_ps[:, 0:CH // 2].rearrange("p c k n -> p (c k n)"), ACT.Copy).then_inc(out_copied, 1)

                    @block.tensor
                    def _(pe):
                        pe.sem_inc(out_copied, 2)
                        with pe.Fori(0, B) as b:
                            pe.wait_ge(sums_ready, b + 1)
                            pe.wait_ge(out_copied, 2 * b + 2)
                            for c in range(CH):
                                for k in range(KD):
                                    last = pe.transpose(big_ps[:, c, k, :], sums[:, c, k * P:(k + 1) * P], g.ident[:])
                            last.then_inc(turned, 1)
                            pe.wait_ge(diag_ready, b + 1)
                            for c in range(CH):
                                last = pe.matmul(ks_ps[:, c, :], g.ones[:], k_diag[:, c, :], start=True, stop=True)
                            last.then_inc(ks_done, 1)
                            pe.wait_ge(turned_out, 2 * b + 2)
                            for c in range(CH):
                                for k in range(KD):
                                    last = pe.matmul(kv_ps[:, c, :], wv[:, k, c * P:(c + 1) * P], sumsT[:, c, k, :],
                                                     start=(k == 0), stop=(k == KD - 1))
                            last.then_inc(kv_done, 1)
                            pe.wait_ge(kv_ready, 2 * b + 2)
                            for c in range(CH):
                                last = pe.matmul(big_ps[:, c].rearrange("p k n -> p (k n)"), kv[:, c, :], wo[:, c, :],
                                                 start=True, stop=True)
                            last.then_inc(out_done, 1)

        with ExitStack() as c2:
            t = Maker(nc, c2)
            hq = t.sb("hq", [P, 2, G, D])
            hT = t.sb("hqT", [P, KD, GT])
            qT, q2 = t.sb("qT", [P, CH, GT]), t.sb("q2", [P, CH, GT])
            wq = t.sb("wq", [P, KD, HD])
            dash = q_dash
            prod = t.sb("q_prod", [P, HD])
            qnT = t.sb("qnT", [P, 2, CH, P])
            y = t.sb("y1", [P, 2, G, D])
            half_diag, top, shift, inv = (t.sb("q_half_diag", [P, 2, H]), t.sb("q_top", [P, H]), t.sb("q_shift", [P, H]),
                                          t.sb("q_inv", [P, H]))
            ring = t.ps("q_ring", [P, 2, 512])
            dash_ps = t.ps("q_dash_ps", [P, HD])
            diag_ps = t.ps("q_diag_ps", [P, 512])
            turn_ps = t.ps("q_turn_ps", [P, CH, P])
            out_ps = t.ps("q_out_ps", [P, 512])
            own, full, free, dash_done, dash_used, diag_copied, shifted, exp_done = (
                mk.sem("pq_dve"), mk.sem("q_full"), mk.sem("q_free"), mk.sem("q_dash_done"), mk.sem("q_dash_used"),
                mk.sem("q_diag_copied"), mk.sem("q_shifted"), mk.sem("q_exp"))
            squared = mk.sem("q_squared")
            qn_ready, turned, turned_out, out_done, out_copied, y_ready = (
                mk.sem("qn_ready"), mk.sem("qn_turned"), mk.sem("qnT_ready"), mk.sem("q_out_done"), mk.sem("q_out_copied"),
                mk.sem("y1_ready"))
            wq_in = mk.sem("wq_in")
            h_in = [mk.sem("hq_in0"), mk.sem("hq_in1")]
            y_out = [mk.sem("y1_out0"), mk.sem("y1_out1")]

            with nc.Block() as block:
                @block.sync
                def _(sp):
                    def load(n, k):
                        sp.dma_start(hq[:, k], h_dram[bass.ds(n * GT, GT), :].rearrange("(t p) d -> p t d", p=P)).then_inc(h_in[k], 16)

                    load(0, 0)
                    sp.dma_start(wq[:], a["L1_attn_Wq"].rearrange("(k p) h d -> p k (h d)", p=P)).then_inc(wq_in, 16)
                    load(1, 1)

                    def body(b, last):
                        for k in range(2):
                            n = 2 * b + k
                            sp.wait_ge(y_ready, n + 1)
                            sp.dma_start(y_dram[bass.ds(n * GT, GT), :].rearrange("(t p) d -> p t d", p=P), y[:, k]).then_inc(y_out[k], 16)
                            if not last:
                                load(n + 2, k)

                    batches(sp, body)
                    for k in range(2):
                        sp.wait_ge(y_out[k], 16 * (B + 1))

                @block.gpsimd
                def _(pool):
                    for k in range(2):
                        pool.sem_inc(y_out[k], 16)
                    square_heads(pool, qT, q2, free, 0, squared)

                    def body(b, last):
                        for k in range(2):
                            if k == 0 or not last:
                                square_heads(pool, qT, q2, free, (2 * b + k + 1) * USES, squared)
                            pool.wait_ge(out_copied, (2 * b + k + 1) * G + 1)
                            pool.tensor_tensor(y[:, k], y[:, k], hq[:, k], ALU.add).then_inc(y_ready, 1)

                    batches(pool, body)

                @block.vector
                def _(dve):
                    dve.sem_inc(dash_used, 1)
                    per = 6
                    with dve.Fori(0, B) as b:
                        for j in range(TB):
                            n = b * TB + j
                            v = Steps(dve, own, n * per)
                            heads = lambda ap: ap.rearrange("p (h m) -> p h m", h=H)
                            dve.wait_ge(diag_copied, n + 2)
                            v(dve.tensor_reduce(top[:], heads(dash_ps[:]), AX.X, ALU.max))
                            v(dve.tensor_tensor(shift[:], top[:], half_diag[:, j % 2, :], ALU.add))
                            v(dve.tensor_tensor(heads(dash[:, j % 2, :]), heads(dash_ps[:]),
                                                shift[:].unsqueeze(2).to_broadcast([P, H, MF]), ALU.subtract))
                            dve.sem_inc(dash_used, 1)
                            dve.sem_inc(shifted, 1)
                            dve.wait_ge(exp_done, n + 1)
                            v(dve.scalar_tensor_tensor(prod[:], dash[:, j % 2, :], KERN_EPS,
                                                       ksum[:, bass.ds(b, 1), :].rearrange("p a n -> p (a n)"), ALU.add, ALU.mult))
                            v(dve.tensor_reduce(top[:], heads(prod[:]), AX.X, ALU.add))
                            v(dve.reciprocal(inv[:], top[:]))
                            dve.scalar_tensor_tensor(heads(qn[:, j % 2, :]), heads(dash[:, j % 2, :]), KERN_EPS,
                                                     inv[:].unsqueeze(2).to_broadcast([P, H, MF]), ALU.add, ALU.mult).then_inc(qn_ready, 1)
                            assert v.n == per

                @block.scalar
                def _(act):
                    act.sem_inc(free, 2)
                    act.sem_inc(diag_copied, 1)
                    act.sem_inc(out_copied, 1)
                    act.sem_inc(turned_out, 1)

                    def heads(n):
                        copy_heads(act, ring, hT, qT, full, n * USES, free)

                    def diag(n, j):
                        act.wait_ge(dash_done, n + 1)
                        act.activation(half_diag[:, j % 2, :], diag_ps[:, 0:H], ACT.Copy).then_inc(diag_copied, 1)

                    def exp(n, j):
                        act.wait_ge(shifted, n + 1)
                        act.activation(dash[:, j % 2, :], dash[:, j % 2, :], ACT.Exp).then_inc(exp_done, 1)

                    heads(0)
                    for j in range(2):
                        diag(j, j)
                        exp(j, j)

                    def body(b, last):
                        for j in range(TB):
                            n = b * TB + j
                            ahead = not last or j + 2 < TB
                            if j % G == G - 2 and ahead:
                                heads(2 * b + j // G + 1)
                            act.wait_ge(turned, n + 1)
                            act.activation(qnT[:, j % 2], turn_ps[:], ACT.Copy).then_inc(turned_out, 1)
                            if ahead:
                                diag(n + 2, j)
                            act.wait_ge(out_done, n + 1)
                            if j % G == 0:
                                act.wait_ge(y_out[j // G], 16 * (b + 1))
                            act.activation(y[:, j // G, j % G, :], out_ps[:, 0:D], ACT.Copy).then_inc(out_copied, 1)
                            if ahead:
                                exp(n + 2, j)

                    batches(act, body)

                @block.tensor
                def _(pe):
                    def project(n, k, uses):
                        pe.wait_ge(h_in[k], uses)
                        project_heads(pe, ring, hq[:, k], hT, g.ident[:], wq, full, free, n * USES)

                    def products(n, j, group):
                        if j == 0:
                            pe.wait_ge(free, (group + 1) * USES + 2)
                            pe.wait_ge(squared, (group + 1) * CH)
                        pe.wait_ge(dash_used, n + 1)
                        pe.wait_ge(diag_copied, n + 1)
                        random_features(pe, dash_ps, diag_ps, qT, q2, j, features[:], half_heads[:]).then_inc(dash_done, 1)

                    pe.wait_ge(wq_in, 16)
                    project(0, 0, 16)
                    products(0, 0, 0)
                    products(1, 1, 0)

                    def body(b, last):
                        for j in range(TB):
                            n = b * TB + j
                            ahead = not last or j + 2 < TB
                            if j % G == G - 2 and ahead:
                                k = j // G
                                project(2 * b + k + 1, 1 - k, 16 * (b + k + 1))
                            pe.wait_ge(qn_ready, n + 1)
                            pe.wait_ge(turned_out, n + 1)
                            for c in range(CH):
                                last_one = pe.transpose(turn_ps[:, c, :], qn[:, j % 2, c * P:(c + 1) * P], g.ident[:])
                            last_one.then_inc(turned, 1)
                            if ahead:
                                products(n + 2, (j + 2) % G, 2 * b + (j + 2) // G)
                            pe.wait_ge(turned_out, n + 2)
                            pe.wait_ge(out_copied, n + 1)
                            for c in range(CH):
                                last_one = pe.matmul(out_ps[:, 0:D], qnT[:, j % 2, c, :],
                                                     kv_out[:, bass.ds(b, 1), c, :].rearrange("p a n -> p (a n)"),
                                                     start=(c == 0), stop=(c == CH - 1))
                            last_one.then_inc(out_done, 1)

                    batches(pe, body)

    mk.clear_signals()
    elu_ffn(nc, mk, g, a, y_dram)


RINGS = 4
PLACES = KD + CF


class Ffn:

    WORK = 4
    HID_CREDIT = 2

    def __init__(self, nc, mk, t, tag):
        sb, ps, sem = (lambda n, *s: t.sb(f"{tag}_{n}", *s)), (lambda n, *s: t.ps(f"{tag}_{n}", *s)), (lambda n: mk.sem(f"{tag}_{n}"))
        pair = lambda n, shape: (sb(n + "_hi", shape, F32R), sb(n + "_lo", shape, F32R))
        self.rows = sb("rows", [P, 2, G, D])
        self.rowsT, self.hid = pair("rowsT", [P, KD, GT]), pair("hid", [P, 2, CF, GT])
        self.w1, self.w2 = pair("w1", [P, KD, DFF]), pair("w2", [P, CF, D])
        self.work = sb("work", [P, self.WORK, GT])
        self.raw = self.work, sb("raw", [P, 2, G, D])
        self.back = sb("back", [P, G, D])
        self.st, self.mv, self.var, self.rstd = sb("st", [P, G, 6]), sb("mv", [P, G, 2]), sb("var", [P, G]), sb("rstd", [P, G])
        self.ring = ps("ring", [P, RINGS, GT])
        self.down = ps("down", [P, G, 512])
        self.own, self.var_ready, self.rstd_ready = sem("dve"), sem("var"), sem("rstd_ready")
        self.weights_in, self.rows_ready, self.full = sem("weights_in"), sem("rows_ready"), sem("full")
        self.act_free, self.dve_free, self.hid_ready = sem("act_free"), sem("dve_free"), sem("hid_ready")
        self.down_done, self.down_used = sem("down_done"), sem("down_used")
        self.hid_high, self.hid_low = sem("hid_high"), sem("hid_low")
        self.weights_high, self.weights_low = sem("weights_high"), sem("weights_low")
        self.back_ready = sem("back_ready")
        self.normed, self.gated, self.back_used, self.passed = sem("normed"), sem("gated"), sem("back_used"), sem("passed")

    def place(self, k, i):
        return (k * PLACES + i) % RINGS

    def raw_weights(self):
        w1, w2 = self.raw[1][:].rearrange("p a t d -> p (a t d)"), self.work[:].rearrange("p a n -> p (a n)")
        return [(raw, *(x[:].rearrange("p a n -> p (a n)") for x in w)) for raw, w in ((w1, self.w1), (w2, self.w2))]

    def load_weights(self, sp, w1, w2):
        (raw1, *_), (raw2, *_) = self.raw_weights()
        sp.dma_start(raw1.rearrange("p (k n) -> p k n", k=KD), w1.rearrange("(k p) n -> p k n", p=P)).then_inc(self.weights_in, 16)
        sp.dma_start(raw2.rearrange("p (c n) -> p c n", c=CF), w2.rearrange("(c p) n -> p c n", p=P)).then_inc(self.weights_in, 16)

    def weights_high_part(self, act):
        act.wait_ge(self.weights_in, 32)
        for raw, high, _ in self.raw_weights():
            act.activation(high, raw, ACT.Copy).then_inc(self.weights_high, 1)

    def weights_low_part(self, dve):
        for i, (raw, high, low) in enumerate(self.raw_weights()):
            dve.wait_ge(self.weights_high, i + 1)
            dve.tensor_tensor(low, raw, high.bitcast(F32), ALU.subtract).then_inc(self.weights_low, 1)

    def products(self, pe, out, w, x, start, stop):
        pe.matmul(out, w[0], x[0], start=start, stop=False)
        pe.matmul(out, w[0], x[1], start=False, stop=False)
        return pe.matmul(out, w[1], x[0], start=False, stop=stop)

    def take(self, pe, n, i):
        pe.wait_ge(self.act_free, n * PLACES + i + 1)
        pe.wait_ge(self.dve_free, n * PLACES + i + 1)

    def turn(self, pe, n, k, ident):
        pe.wait_ge(self.rows_ready, n + 1)
        for i in range(KD):
            self.take(pe, n, i)
            for j in range(G):
                last = pe.transpose(self.ring[:, self.place(k, i), j * P:(j + 1) * P], self.rows[:, k, j, i * P:(i + 1) * P], ident)
            last.then_inc(self.full, 1)

    def up(self, pe, n, k):
        pe.wait_ge(self.dve_free, n * PLACES + KD + RINGS)
        for c in range(CF):
            self.take(pe, n, KD + c)
            for d in range(KD):
                last = self.products(pe, self.ring[:, self.place(k, KD + c), :], [w[:, d, c * P:(c + 1) * P] for w in self.w1],
                                     [x[:, d, :] for x in self.rowsT], d == 0, d == KD - 1)
            last.then_inc(self.full, 1)

    def back_down(self, pe, n, k, before_last=None):
        pe.wait_ge(self.hid_low, (n + 1) * CF + self.WORK)
        for j in range(G):
            if j == G - 1 and before_last:
                before_last()
            pe.wait_ge(self.down_used, n * G + j + 1)
            for c in range(CF):
                last = self.products(pe, self.down[:, j, 0:D], [h[:, k, c, j * P:(j + 1) * P] for h in self.hid],
                                     [w[:, c, :] for w in self.w2], c == 0, c == CF - 1)
            last.then_inc(self.down_done, 1)

    def tensor_program(self, pe, ident, b_loop):
        pe.wait_ge(self.weights_low, 2)
        self.turn(pe, 0, 0, ident)
        self.up(pe, 0, 0)
        self.turn(pe, 1, 1, ident)

        def body(b, last):
            for k in range(2):
                n = 2 * b + k
                if k == 0 or not last:
                    self.up(pe, n + 1, 1 - k)
                self.back_down(pe, n, k, None if last else lambda: self.turn(pe, n + 2, k, ident))

        b_loop(pe, body)

    def turned_high(self, act, n, k):
        for i in range(KD):
            act.wait_ge(self.full, n * PLACES + i + 1)
            act.activation(self.rowsT[0][:, i, :], self.ring[:, self.place(k, i), :], ACT.Copy).then_inc(self.act_free, 1)

    def turned_low(self, dve, n, k):
        for i in range(KD):
            dve.wait_ge(self.act_free, n * PLACES + i + 1 + RINGS)
            dve.tensor_tensor(self.rowsT[1][:, i, :], self.ring[:, self.place(k, i), :], self.rowsT[0][:, i, :].bitcast(F32),
                              ALU.subtract).then_inc(self.dve_free, 1)

    def hidden_high(self, act, n, k, c):
        act.wait_ge(self.hid_ready, n * CF + c + 1 + self.HID_CREDIT)
        act.activation(self.hid[0][:, k, c, :], self.work[:, c % self.WORK, :], ACT.Copy).then_inc(self.hid_high, 1)

    def hidden_low(self, pool, n, k, meanwhile={}):
        for c in range(CF):
            if c in meanwhile:
                meanwhile[c]()
            pool.wait_ge(self.hid_high, n * CF + c + 1)
            pool.tensor_tensor(self.hid[1][:, k, c, :], self.work[:, c % self.WORK, :], self.hid[0][:, k, c, :].bitcast(F32),
                               ALU.subtract).then_inc(self.hid_low, 1)


def columns(ap):
    return ap.rearrange("(c p) -> p c", p=P)


def elu_ffn(nc, mk, g, a, y_dram):
    with ExitStack() as ctx:
        t = Maker(nc, ctx)
        f = Ffn(nc, mk, t, "elu")
        y = t.sb("elu_y", [P, 2, G, D])
        base = f.raw[1]
        e, r = t.sb("elu_e", [P, 2, GT]), f.work
        b1, b1_less = t.sb("elu_b1", [P, CF]), t.sb("elu_b1_less", [P, CF])
        vec = t.sb("elu_vec", [P, 5, D])
        LN1_G, LN1_B, B2, LN2_G, LN2_B = range(5)
        y_in = [mk.sem("elu_y_in0"), mk.sem("elu_y_in1")]
        small_in, base_ready, base_used = mk.sem("elu_small_in"), mk.sem("elu_base_ready"), mk.sem("elu_base_used")
        mod = g.modb[:].rearrange("p b (s d) -> p b s d", s=6)
        gate_g, gate_b = mod[:, :, CA, :], mod[:, :, SA, :]
        gained, shifted = mk.sem("elu_gained"), mk.sem("elu_shifted")
        spread = lambda i: vec[:, i:i + 1, :].to_broadcast([P, G, D])

        with nc.Block() as block:
            @block.sync
            def _(sp):
                def load(n, k):
                    sp.dma_start(y[:, k], y_dram[bass.ds(n * GT, GT), :].rearrange("(t p) d -> p t d", p=P)).then_inc(y_in[k], 16)

                load(0, 0)
                for i, name in enumerate(("ln1_g", "ln1_b", "b2", "ln2_g", "ln2_b")):
                    sp.dma_start(vec[:, i, :], a[f"L1_attn_{name}"].partition_broadcast(P)).then_inc(small_in, 16)
                sp.dma_start(b1[:], columns(a["L1_attn_b1"]), allow_slow_non_contiguous=True).then_inc(small_in, 16)
                load(1, 1)
                f.load_weights(sp, a["L1_attn_W1"], a["L1_attn_W2"])
                with sp.Fori(0, B - 1) as b:
                    for k in range(2):
                        sp.wait_ge(f.rows_ready, 2 * b + k + 1)
                        load(2 * b + k + 2, k)

            @block.gpsimd
            def _(pool):
                pool.wait_ge(small_in, 96)

                def power(norms):
                    pool.wait_ge(f.var_ready, norms + 1)
                    rsqrt_rows(pool, f.rstd, f.var, g.minus_half, G, f.rstd_ready)

                def gain(n, k):
                    pool.wait_ge(f.normed, n + 1)
                    pool.tensor_tensor(f.rows[:, k], f.rows[:, k], spread(LN1_G), ALU.mult).then_inc(gained, 1)

                def shift(n, k):
                    pool.wait_ge(gained, n + 1)
                    pool.tensor_tensor(f.rows[:, k], f.rows[:, k], spread(LN1_B), ALU.add).then_inc(f.rows_ready, 1)

                def finish(n, k, b):
                    wait_apart(pool, f.gated, n + 1, f.passed)
                    pool.tensor_tensor(f.back[:], f.back[:], gate_b[:, bass.ds(b, 1), :].to_broadcast([P, G, D]), ALU.add).then_inc(shifted, 1)
                    wait_apart(pool, shifted, n + 1, f.passed)
                    x = g.x[:, bass.ds(b * TB + k * G, G), :]
                    pool.tensor_tensor(x, x, f.back[:], ALU.add).then_inc(f.back_used, 1)

                def add_bias(n, k):
                    pool.wait_ge(f.rows_ready, n + 1)
                    pool.tensor_tensor(base[:, k], f.rows[:, k], spread(B2), ALU.add).then_inc(base_ready, 1)

                power(0)
                power(1)
                for k in range(2):
                    gain(k, k)
                    shift(k, k)
                pool.wait_ge(f.weights_low, 2)
                for k in range(2):
                    add_bias(k, k)
                f.hidden_low(pool, 0, 0)

                def body(b, last):
                    for k in range(2):
                        n = 2 * b + k
                        if not last:
                            f.hidden_low(pool, n + 1, 1 - k, {1: lambda: power(2 + 2 * n), 3: lambda: gain(n + 2, k),
                                                              5: lambda: shift(n + 2, k)})
                            power(3 + 2 * n)
                            finish(n, k, b)
                            pool.wait_ge(base_used, n + 1)
                            add_bias(n + 2, k)
                        else:
                            if k == 0:
                                f.hidden_low(pool, n + 1, 1 - k)
                            power(2 + 2 * n - k)
                            finish(n, k, b)

                batches(pool, body)

            @block.scalar
            def _(act):
                act.wait_ge(small_in, 96)
                act.sem_inc(f.act_free, RINGS)
                f.weights_high_part(act)

                def up(n, k):
                    f.turned_high(act, n, k)
                    for c in range(CF):
                        act.wait_ge(f.dve_free, n * PLACES + KD + c + 1 + RINGS)
                        act.wait_ge(f.hid_ready, n * CF + c + 1)
                        act.activation(e[:, c % 2, :], f.ring[:, f.place(k, KD + c), :], ACT.Exp,
                                       bias=b1[:, c:c + 1]).then_inc(f.act_free, 1)
                        if c:
                            f.hidden_high(act, n, k, c - 1)
                    f.hidden_high(act, n, k, CF - 1)

                up(0, 0)

                def body(b, last):
                    up(2 * b + 1, 1)
                    if not last:
                        up(2 * b + 2, 0)

                batches(act, body)

            @block.vector
            def _(dve):
                v = Steps(dve, f.own)
                dve.sem_inc(f.dve_free, RINGS)
                dve.sem_inc(f.down_used, G)
                dve.sem_inc(f.hid_ready, f.HID_CREDIT)
                dve.sem_inc(f.hid_low, f.WORK)
                dve.sem_inc(f.back_used, 1)
                dve.wait_ge(small_in, 96)
                v.mark(dve.tensor_scalar(b1_less[:], b1[:], -1.0, None, ALU.add))
                v.mark(dve.tensor_tensor(gate_g, mod[:, :, GA, :], vec[:, LN2_G:LN2_G + 1, :].to_broadcast([P, B, D]), ALU.mult))
                v.mark(dve.tensor_tensor(gate_b, mod[:, :, GA, :], vec[:, LN2_B:LN2_B + 1, :].to_broadcast([P, B, D]), ALU.mult))
                v.sync()

                def prepare(v, n, k, b, norms, based=None):
                    dve.wait_ge(y_in[k], 16 * (b + 1))
                    if based is not None:
                        dve.wait_ge(base_ready, based)
                    layer_norm_stats(v, g.spare, f.st, f.mv, f.var, G, lambda j: y[:, k, j, :], ENC_EPS, f.var_ready)
                    yield
                    dve.wait_ge(f.rstd_ready, norms + 1)
                    for j in range(G):
                        v.mark(dve.tensor_scalar(f.rows[:, k, j, :], y[:, k, j, :], f.mv[:, j, 0:1], f.rstd[:, j:j + 1],
                                                 ALU.subtract, ALU.mult))
                    v.sync()
                    dve.sem_inc(f.normed, 1)

                def hidden(v, n, k, meanwhile=()):
                    meanwhile = iter(meanwhile)
                    for c in range(CF + 1):
                        if c < CF:
                            dve.wait_ge(f.full, n * PLACES + KD + c + 1)
                            dve.wait_ge(f.hid_low, n * CF + c + 1)
                            dve.tensor_scalar(r[:, c % f.WORK, :], f.ring[:, f.place(k, KD + c), :], b1_less[:, c:c + 1], -1.0,
                                              ALU.add, ALU.max).then_inc(f.dve_free, 1)
                        if c:
                            dve.wait_ge(f.dve_free, n * PLACES + KD + c + RINGS)
                            dve.wait_ge(f.act_free, n * PLACES + KD + c + RINGS)
                            part = r[:, (c - 1) % f.WORK, :]
                            dve.scalar_tensor_tensor(part, e[:, (c - 1) % 2, :], 1.0, part, ALU.min, ALU.add).then_inc(f.hid_ready, 1)
                        if c in (1, 3):
                            next(meanwhile, None)
                    for _ in meanwhile:
                        pass

                def result(v, n, k, b, norms):
                    dve.wait_ge(f.back_used, n + 1)
                    dve.wait_ge(base_ready, n + 1)
                    for j in range(G):
                        dve.wait_ge(f.down_done, n * G + j + 1)
                        v.mark(dve.tensor_tensor(f.back[:, j, :], f.down[:, j, 0:D], base[:, k, j, :], ALU.add))
                    v.sync()
                    dve.sem_inc(f.down_used, G)
                    dve.sem_inc(base_used, 1)
                    layer_norm_stats(v, g.spare, f.st, f.mv, f.var, G, lambda j: f.back[:, j, :], ENC_EPS, f.var_ready)
                    dve.wait_ge(f.rstd_ready, norms + 1)
                    for j in range(G):
                        v.mark(dve.tensor_scalar(f.back[:, j, :], f.back[:, j, :], f.mv[:, j, 0:1], f.rstd[:, j:j + 1],
                                                 ALU.subtract, ALU.mult))
                    v.sync()
                    dve.tensor_tensor(f.back[:], f.back[:], gate_g[:, bass.ds(b, 1), :].to_broadcast([P, G, D]),
                                      ALU.mult).then_inc(f.gated, 1)

                for k in range(2):
                    for _ in prepare(v, k, k, 0, k):
                        pass
                f.weights_low_part(dve)
                f.turned_low(dve, 0, 0)
                hidden(v, 0, 0)
                f.turned_low(dve, 1, 1)
                first = v.n
                PREP, RES = 3 * G, 4 * G
                per = 2 * (PREP + RES)

                def body(b, last):
                    v = Steps(dve, f.own, b * per + first)
                    for k in range(2):
                        n = 2 * b + k
                        if not last:
                            hidden(v, n + 1, 1 - k, prepare(v, n + 2, k, b + 1, 2 + 2 * n, n + 1))
                            f.turned_low(dve, n + 2, k)
                        elif k == 0:
                            hidden(v, n + 1, 1 - k)
                        result(v, n, k, b, 2 + 2 * n - k if last else 3 + 2 * n)
                    assert last or v.n == per, (v.n, per)

                batches(dve, body)

            @block.tensor
            def _(pe):
                f.tensor_program(pe, g.ident[:], batches)
        mk.clear_signals()


def wave_ffn(nc, mk, g, a, out):
    TURN = 1.0 / (2.0 * 3.141592653589793)
    FULL = 6.283185
    with ExitStack() as ctx:
        t = Maker(nc, ctx)
        f = Ffn(nc, mk, t, "wave")
        whole, turns, wave, u = (t.sb("wave_whole", [P, 2, GT]), t.sb("wave_turns", [P, 2, GT]), t.sb("wave_sine", [P, 2, GT]),
                                 t.sb("wave_u", [P, 2, GT]))
        vec = t.sb("wave_vec", [P, 8, CF])
        B1, THETA, W_RE, W_IM, OFFSET, AMP, SINE, COSINE = range(8)
        part = t.sb("wave_part", [P, 2, CF])
        b2 = t.sb("wave_b2", [P, D])
        small_in, consts, angles, sines = mk.sem("wave_small_in"), mk.sem("wave_consts"), mk.sem("wave_angles"), mk.sem("wave_sines")
        turns_ready, sine_ready, gained, x_ready, x_out = (mk.sem("wave_turns_ready"), mk.sem("wave_sine_ready"),
                                                           mk.sem("wave_gained"), mk.sem("wave_x_ready"), mk.sem("x_out"))
        mod = g.modb[:].rearrange("p b (s d) -> p b s d", s=6)

        with nc.Block() as block:
            @block.sync
            def _(sp):
                for i, name in ((B1, "b1"), (THETA, "quantum_phases"), (W_RE, "quantum_weights_real"), (W_IM, "quantum_weights_imag")):
                    sp.dma_start(vec[:, i, :], columns(a[f"L1_ffn_{name}"]), allow_slow_non_contiguous=True).then_inc(small_in, 16)
                sp.dma_start(b2[:], a["L1_ffn_b2"].partition_broadcast(P)).then_inc(small_in, 16)
                f.load_weights(sp, a["L1_ffn_W1"], a["L1_ffn_W2"])
                rows = out.rearrange("b (t p) d -> p (b t) d", p=P)
                with sp.Fori(0, NG) as n:
                    sp.wait_ge(x_ready, n + 2)
                    sp.dma_start(rows[:, bass.ds(n * G, G), :], g.x[:, bass.ds(n * G, G), :]).then_inc(x_out, 16)
                sp.wait_ge(x_out, 16 * NG)

            @block.gpsimd
            def _(pool):
                spread = lambda i, b: mod[:, bass.ds(b, 1), i, :].to_broadcast([P, G, D])

                def power(n):
                    pool.wait_ge(f.var_ready, n + 1)
                    rsqrt_rows(pool, f.rstd, f.var, g.minus_half, G, f.rstd_ready)

                def gain(n, k, b):
                    wait_apart(pool, f.normed, n + 1, f.passed)
                    pool.tensor_tensor(f.rows[:, k], f.rows[:, k], spread(CB, b), ALU.mult).then_inc(gained, 1)

                def shift(n, k, b):
                    wait_apart(pool, gained, n + 1, f.passed)
                    pool.tensor_tensor(f.rows[:, k], f.rows[:, k], spread(SB, b), ALU.add).then_inc(f.rows_ready, 1)

                def finish(n, k, b):
                    wait_apart(pool, f.back_ready, n + 1, f.passed)
                    pool.tensor_tensor(f.back[:], f.back[:], spread(GB, b), ALU.mult).then_inc(f.gated, 1)
                    wait_apart(pool, f.gated, n + 1, f.passed)
                    x = g.x[:, bass.ds(b * TB + k * G, G), :]
                    pool.tensor_tensor(x, x, f.back[:], ALU.add).then_inc(x_ready, 1)

                power(0)
                power(1)
                for k in range(2):
                    gain(k, k, 0)
                    shift(k, k, 0)
                f.hidden_low(pool, 0, 0)

                def body(b, last):
                    for k in range(2):
                        n = 2 * b + k
                        if not last:
                            power(n + 2)
                            gain(n + 2, k, b + 1)
                            f.hidden_low(pool, n + 1, 1 - k, {1: lambda: shift(n + 2, k, b + 1)})
                        elif k == 0:
                            f.hidden_low(pool, n + 1, 1 - k)
                        finish(n, k, b)

                batches(pool, body)

            @block.scalar
            def _(act):
                act.sem_inc(f.act_free, RINGS)
                f.weights_high_part(act)
                act.wait_ge(angles, 1)
                act.activation(vec[:, SINE, :], part[:, 0, :], ACT.Sin, scale=FULL)
                act.activation(vec[:, COSINE, :], part[:, 1, :], ACT.Sin, scale=FULL).then_inc(sines, 1)
                act.wait_ge(consts, 1)

                def up(n, k):
                    f.turned_high(act, n, k)
                    used = lambda c: act.wait_ge(f.dve_free, n * PLACES + KD + c + 1 + RINGS)
                    for c in range(CF + 4):
                        if c < CF:
                            act.wait_ge(f.full, n * PLACES + KD + c + 1)
                            act.wait_ge(sine_ready, n * CF + c + 1)
                            act.activation(turns[:, c % 2, :], f.ring[:, f.place(k, KD + c), :], ACT.Identity, scale=0.1 * TURN,
                                           bias=vec[:, OFFSET, c:c + 1]).then_inc(f.act_free, 1)
                        if 1 <= c <= CF:
                            act.wait_ge(turns_ready, n * CF + c)
                            if c >= 3:
                                used(c - 3)
                            act.activation(wave[:, (c - 1) % 2, :], turns[:, (c - 1) % 2, :], ACT.Sin, scale=FULL).then_inc(sine_ready, 1)
                        if 3 <= c < CF + 3:
                            used(c - 3)
                            act.wait_ge(f.hid_low, n * CF + c - 3 + 1)
                            act.activation(f.work[:, (c - 3) % f.WORK, :], u[:, (c - 3) % 2, :], ACT.Relu,
                                           bias=vec[:, B1, c - 3:c - 2]).then_inc(f.hid_ready, 1)
                        if c >= 4:
                            f.hidden_high(act, n, k, c - 4)

                up(0, 0)

                def body(b, last):
                    up(2 * b + 1, 1)
                    if not last:
                        up(2 * b + 2, 0)

                batches(act, body)

            @block.vector
            def _(dve):
                v = Steps(dve, f.own)
                dve.sem_inc(f.dve_free, RINGS)
                dve.sem_inc(f.down_used, G)
                dve.sem_inc(f.hid_ready, f.HID_CREDIT)
                dve.sem_inc(f.hid_low, f.WORK)
                dve.sem_inc(sine_ready, 2)
                dve.sem_inc(x_ready, 1)
                dve.wait_ge(small_in, 80)
                v(dve.tensor_scalar(part[:, 0, :], vec[:, THETA, :], TURN, None, ALU.mult))
                v(dve.tensor_scalar(part[:, 0, :], part[:, 0, :], ROUND, ROUND, ALU.add, ALU.subtract))
                v(dve.scalar_tensor_tensor(vec[:, THETA, :], part[:, 0, :], -PI2_HI, vec[:, THETA, :], ALU.mult, ALU.add))
                v(dve.scalar_tensor_tensor(vec[:, THETA, :], part[:, 0, :], -PI2_LO, vec[:, THETA, :], ALU.mult, ALU.add))
                v(dve.tensor_scalar(vec[:, THETA, :], vec[:, THETA, :], TURN, None, ALU.mult))
                for i, ahead in ((0, 0.0), (1, 0.25)):
                    v(dve.tensor_scalar(part[:, i, :], vec[:, THETA, :], ahead, ROUND, ALU.add, ALU.add))
                    v(dve.tensor_scalar(part[:, i, :], part[:, i, :], ROUND, ahead, ALU.subtract, ALU.subtract))
                    v(dve.tensor_tensor(part[:, i, :], vec[:, THETA, :], part[:, i, :], ALU.subtract))
                dve.sem_inc(angles, 1)
                v(dve.scalar_tensor_tensor(vec[:, OFFSET, :], vec[:, B1, :], 0.1 * TURN, vec[:, THETA, :], ALU.mult, ALU.add))
                dve.wait_ge(sines, 1)
                v.mark(dve.tensor_tensor(vec[:, COSINE, :], vec[:, COSINE, :], vec[:, W_RE, :], ALU.mult))
                v.mark(dve.tensor_tensor(vec[:, SINE, :], vec[:, SINE, :], vec[:, W_IM, :], ALU.mult))
                v.sync()
                v(dve.tensor_tensor(vec[:, AMP, :], vec[:, COSINE, :], vec[:, SINE, :], ALU.add))
                v(dve.scalar_tensor_tensor(vec[:, AMP, :], vec[:, AMP, :], 0.1, vec[:, W_IM, :], ALU.mult, ALU.mult))
                dve.sem_inc(consts, 1)

                def prepare(v, n, k, b):
                    tile = lambda j: g.x[:, bass.ds(b * TB + k * G + j, 1), :]
                    layer_norm_stats(v, g.spare, f.st, f.mv, f.var, G, tile, LN_EPS, f.var_ready)
                    yield
                    dve.wait_ge(f.rstd_ready, n + 1)
                    for j in range(G):
                        v.mark(dve.tensor_scalar(f.rows[:, k, j:j + 1, :], tile(j), f.mv[:, j, 0:1], f.rstd[:, j:j + 1],
                                                 ALU.subtract, ALU.mult))
                    v.sync()
                    dve.sem_inc(f.normed, 1)

                def hidden(v, n, k, meanwhile=()):
                    meanwhile = iter(meanwhile)
                    for c in range(CF + 2):
                        if c < CF:
                            i = c % 2
                            dve.wait_ge(f.act_free, n * PLACES + KD + c + 1 + RINGS)
                            v(dve.tensor_scalar(whole[:, i, :], turns[:, i, :], ROUND, ROUND, ALU.add, ALU.subtract))
                            dve.tensor_tensor(turns[:, i, :], turns[:, i, :], whole[:, i, :], ALU.subtract).then_inc(turns_ready, 1)
                        if c >= 2:
                            z, i = f.ring[:, f.place(k, KD + c - 2), :], c % 2
                            dve.wait_ge(sine_ready, n * CF + c - 1 + 2)
                            dve.wait_ge(f.hid_ready, n * CF + max(c - 3, 0) + f.HID_CREDIT)
                            dve.scalar_tensor_tensor(u[:, i, :], wave[:, i, :], vec[:, AMP, c - 2:c - 1], z, ALU.mult,
                                                     ALU.add).then_inc(f.dve_free, 1)
                        if c in (0, 2):
                            next(meanwhile, None)
                    for _ in meanwhile:
                        pass

                def result(v, n):
                    dve.wait_ge(x_ready, n + 1)
                    for j in range(G):
                        dve.wait_ge(f.down_done, n * G + j + 1)
                        v.mark(dve.tensor_tensor(f.back[:, j, :], f.down[:, j, 0:D], b2[:], ALU.add))
                    v.sync()
                    dve.sem_inc(f.down_used, G)
                    dve.sem_inc(f.back_ready, 1)

                for k in range(2):
                    for _ in prepare(v, k, k, 0):
                        pass
                f.weights_low_part(dve)
                f.turned_low(dve, 0, 0)
                hidden(v, 0, 0)
                f.turned_low(dve, 1, 1)
                first = v.n
                per = 2 * (3 * G + CF + G)

                def body(b, last):
                    v = Steps(dve, f.own, b * per + first)
                    for k in range(2):
                        n = 2 * b + k
                        if not last:
                            hidden(v, n + 1, 1 - k, prepare(v, n + 2, k, b + 1))
                            f.turned_low(dve, n + 2, k)
                        elif k == 0:
                            hidden(v, n + 1, 1 - k)
                        result(v, n)
                    assert last or v.n == per, (v.n, per)

                batches(dve, body)

            @block.tensor
            def _(pe):
                f.tensor_program(pe, g.ident[:], batches)
        mk.clear_signals()


class Chip:
    pass


def program(nc, a, out):
    with ExitStack() as ctx:
        mk = Maker(nc, ctx)
        g = Chip()
        g.x = mk.sb("x", [P, NT, D])
        g.modb = mk.sb("modb", [P, B, 6 * D])
        g.ident, g.flip, g.ones = mk.sb("ident", [P, P]), mk.sb("flip", [P, P]), mk.sb("ones", [P, P])
        g.minus_half, g.eye_b = mk.sb("minus_half", [P, TB]), mk.sb("eye_b", [P, B, B])
        g.spare, g.pool_spare, g.pool_max = mk.sb("spare", [P, 1]), mk.sb("pool_spare", [P, 1]), mk.sb("pool_max", [P, 1])
        g.mod_dram = nc.dram_tensor("mod_dram", (2, B, 6 * D), F32, kind="Internal").ap()
        with ExitStack() as c:
            w = Maker(nc, c)
            g.wqkv, g.wconv = w.sb("wqkv", [P, 6, D]), w.sb("wconv", [P, KD])
            setup(nc, mk, g, a)
            agent_attention(nc, mk, g)
            mk.clear_signals()
        expert_choice(nc, mk, g, a)
        performer(nc, mk, g, a)
        wave_ffn(nc, mk, g, a, out)


_INS = ["L0_attn_x", "L0_attn_w_qkv", "L0_attn_w_conv1", "L0_ffn_Wr", "L0_ffn_W1", "L0_ffn_b1", "L0_ffn_W2", "L0_ffn_b2",
        "L0_c", "L0_wmod", "L1_attn_Wq", "L1_attn_Wk", "L1_attn_Wv", "L1_attn_Wo", "L1_attn_proj", "L1_attn_W1",
        "L1_attn_b1", "L1_attn_W2", "L1_attn_b2", "L1_attn_ln1_g", "L1_attn_ln1_b", "L1_attn_ln2_g", "L1_attn_ln2_b",
        "L1_ffn_W1", "L1_ffn_b1", "L1_ffn_quantum_phases", "L1_ffn_quantum_weights_real", "L1_ffn_quantum_weights_imag",
        "L1_ffn_W2", "L1_ffn_b2", "L1_c", "L1_wmod"]


def kernel(**inputs):
    import numpy as _np
    import concourse.bacc as _bacc
    from concourse import mybir as _mybir
    from concourse.bass_utils import run_bass_kernel_spmd as _run

    nc = _bacc.Bacc("TRN2", target_bir_lowering=False, num_devices=1)
    arrays, args = {}, {}
    for name in _INS:
        a = _np.ascontiguousarray(inputs[name])
        arrays[f"in_{name}_dram"] = a
        args[name] = nc.dram_tensor(f"in_{name}_dram", a.shape, _mybir.dt.from_np(a.dtype), kind="ExternalInput").ap()
    out = nc.dram_tensor("out_0_dram", (B, N, D), F32, kind="ExternalOutput").ap()
    program(nc, args, out)
    r = _run(nc, [arrays], core_ids=[0])
    return r.results[0]["out_0_dram"]
```

```python
from contextlib import ExitStack

import concourse.bass as bass
from concourse import mybir

ALU = mybir.AluOpType
ACT = mybir.ActivationFunctionType
AX = mybir.AxisListType
F32 = mybir.dt.float32
F32R = mybir.dt.float32r
U32 = mybir.dt.uint32

P = 128
B, N, D = 4, 1024, 256
T = B * N
NT = T // P
TB = N // P
KD = D // P
G = 4
GT = G * P
NG = NT // G
E, S, M = 48, 4, 256
KS = D // S
CAP = int(1.5 * T / E)
H, DH, MF = 16, 64, 64
HD = H * DH
CH = HD // P
DFF = 1024
CF = DFF // P
LN_EPS = 1e-5
ENC_EPS = 1e-6
KERN_EPS = 1e-6
DN = float(DH) ** -0.25
GATE_MIN = 0.25
SA, CA, GA, SB, CB, GB = range(6)
PI2_HI, PI2_LO = 6.28125, 0.0019353071795864769
ROUND = 12582912.0
LOWEST = -3.0e38


class Steps:

    def __init__(self, eng, sem, base=0):
        self.eng, self.sem, self.base, self.n = eng, sem, base, 0

    def start(self, base):
        self.base, self.n = base, 0

    def mark(self, ins):
        self.n += 1
        ins.then_inc(self.sem, 1)

    def sync(self):
        self.eng.wait_ge(self.sem, self.base + self.n)

    def __call__(self, ins):
        self.mark(ins)
        self.sync()


def batches(eng, body):
    with eng.Fori(0, B - 1) as b:
        body(b, False)
    body(B - 1, True)


def wait_apart(eng, sem, value, passed):
    eng.wait_ge(sem, value)
    eng.sem_inc(passed, 1)


class Maker:

    def __init__(self, nc, ctx):
        self.nc, self.ctx, self.signals = nc, ctx, []

    def sb(self, name, shape, dt=F32):
        return self.ctx.enter_context(self.nc.sbuf_tensor(name, shape, dt))

    def ps(self, name, shape, dt=F32):
        return self.ctx.enter_context(self.nc.psum_tensor(name, shape, dt))

    def sem(self, name):
        handle = self.nc.alloc_semaphore(name=name)
        self.signals.append(handle)
        return handle

    def clear_signals(self):
        self.nc.clear_and_free_semaphores(self.signals)
        self.signals = []
        self.nc.all_engine_barrier()


def layer_norm_stats(v, mv_spare, st, mv, var, tiles, x_tile, eps, var_ready):
    for j in range(tiles):
        v.mark(v.eng.bn_stats(st[:, j, :], x_tile(j)))
    v.sync()
    v.eng.memset(mv_spare[:], 0.0)
    for j in range(tiles):
        v.mark(v.eng.bn_aggr(mv[:, j, :], st[:, j, :]))
    v.sync()
    v.eng.tensor_scalar(var[:, 0:tiles], mv[:, 0:tiles, 1], eps, None, ALU.add).then_inc(var_ready, 1)


def rsqrt_rows(pool, rstd, var, minus_half, tiles, rstd_ready):
    pool.tensor_tensor(rstd[:, 0:tiles], var[:, 0:tiles], minus_half[:, 0:tiles], ALU.pow).then_inc(rstd_ready, 1)


def setup(nc, mk, g, a):
    with ExitStack() as ctx:
        t = Maker(nc, ctx)
        c_rows = t.sb("c_rows", [B, 2, D])
        c_exp = t.sb("c_exp", [B, 2, D])
        c_silu = t.sb("c_silu", [B, 2, D])
        cT = t.sb("cT", [P, 2, KD, B])
        wmod = t.sb("wmod", [P, 2, KD, 6 * D])
        rows = t.sb("rows", [B, 2, 6, D])
        size = t.sb("size", [B, 2, 2, D])
        sign = t.sb("sign", [B, 2, 2, D])
        cT_ps = t.ps("cT_ps", [P, 2, KD, B])
        mod_ps = t.ps("mod_ps", [P, 2, 6 * D])

        c_in, x_in, w_in = mk.sem("c_in"), mk.sem("x_in"), mk.sem("w_in")
        wmod_in = [mk.sem("wmod_in0"), mk.sem("wmod_in1")]
        zeroed, ident_done, exp_done = mk.sem("zeroed"), mk.sem("ident_done"), mk.sem("exp_done")
        silu_done, cT_done, cT_copied = mk.sem("silu_done"), mk.sem("cT_done"), mk.sem("cT_copied")
        mod_done, rows_done, rows_out = mk.sem("mod_done"), mk.sem("rows_done"), mk.sem("rows_out")
        g.modb_in = mk.sem("modb_in")
        own = mk.sem("setup_dve")

        with nc.Block() as block:
            @block.sync
            def _(sp):
                sp.dma_start(c_rows[:, 0, :], a["L0_c"]).then_inc(c_in, 16)
                sp.dma_start(c_rows[:, 1, :], a["L1_c"]).then_inc(c_in, 16)
                sp.dma_start(wmod[:, 0], a["L0_wmod"].rearrange("(k p) n -> p k n", p=P)).then_inc(wmod_in[0], 16)
                sp.dma_start(wmod[:, 1], a["L1_wmod"].rearrange("(k p) n -> p k n", p=P)).then_inc(wmod_in[1], 16)
                sp.dma_start(g.x[:], a["L0_attn_x"].rearrange("b (t p) d -> p (b t) d", p=P)).then_inc(x_in, 16)
                for l in range(2):
                    sp.wait_ge(rows_done, l + 1)
                    sp.dma_start(g.mod_dram[l], rows[:, l].rearrange("b s d -> b (s d)")).then_inc(rows_out, 16)
                    if l == 0:
                        sp.wait_ge(rows_out, 16)
                        sp.dma_start(g.modb[:], g.mod_dram[0].partition_broadcast(P)).then_inc(g.modb_in, 16)
                sp.wait_ge(rows_out, 32)
                sp.wait_ge(x_in, 16)

            @block.scalar
            def _(act):
                act.dma_start(g.wqkv[:], a["L0_attn_w_qkv"].rearrange("(j p) c -> p j c", p=P)).then_inc(w_in, 16)
                act.dma_start(g.wconv[:], a["L0_attn_w_conv1"].rearrange("(j p) -> p j", p=P),
                              allow_slow_non_contiguous=True).then_inc(w_in, 16)
                act.wait_ge(c_in, 32)
                act.activation(c_exp[:], c_rows[:], ACT.Exp, scale=-1.0).then_inc(exp_done, 1)
                act.wait_ge(w_in, 32)

            @block.gpsimd
            def _(pool):
                pool.memset(g.ident[:], 0.0).then_inc(zeroed, 1)
                pool.memset(g.flip[:], 0.0).then_inc(zeroed, 1)
                pool.memset(g.ones[:], 1.0)
                pool.memset(g.minus_half[:], -0.5)
                pool.memset(g.eye_b[:], 0.0).then_inc(zeroed, 1)
                pool.wait_ge(zeroed, 3)
                pool.affine_select(out=g.ident[:], in_=g.ident[:], compare_op=ALU.not_equal, fill=1.0, base=0,
                                   pattern=[[-1, P]], channel_multiplier=1).then_inc(ident_done, 1)
                pool.affine_select(out=g.flip[:], in_=g.flip[:], compare_op=ALU.not_equal, fill=1.0, base=1 - P,
                                   pattern=[[1, P]], channel_multiplier=1).then_inc(ident_done, 1)
                pool.affine_select(out=g.eye_b[:], in_=g.eye_b[:], compare_op=ALU.not_equal, fill=1.0, base=0,
                                   pattern=[[1, B], [-1, B]], channel_multiplier=0).then_inc(ident_done, 1)
                pool.wait_ge(ident_done, 3)

            @block.vector
            def _(dve):
                v = Steps(dve, own)
                dve.wait_ge(exp_done, 1)
                v(dve.tensor_scalar(c_exp[:], c_exp[:], 1.0, None, ALU.add))
                v(dve.reciprocal(c_exp[:], c_exp[:]))
                dve.tensor_tensor(c_silu[:], c_rows[:], c_exp[:], ALU.mult).then_inc(silu_done, 1)
                dve.wait_ge(cT_done, 1)
                dve.tensor_copy(cT[:], cT_ps[:]).then_inc(cT_copied, 1)
                gates, shifts = rows[:, :, GA::3, :], rows[:, :, CA::3, :]
                for l in range(2):
                    dve.wait_ge(mod_done, l + 1)
                    v(dve.tensor_copy(rows[:, l].rearrange("b s d -> b (s d)"), mod_ps[0:B, l]))
                    v.mark(dve.tensor_scalar(shifts[:, l], shifts[:, l], 1.0, None, ALU.add))
                    v.mark(dve.scalar_tensor_tensor(size[:, l], gates[:, l], -1.0, gates[:, l], ALU.mult, ALU.max))
                    v.mark(dve.tensor_scalar(sign[:, l], gates[:, l], 0.0, 2.0, ALU.is_ge, ALU.mult))
                    v.sync()
                    v(dve.tensor_scalar(size[:, l], size[:, l], GATE_MIN, None, ALU.max))
                    v(dve.scalar_tensor_tensor(gates[:, l], sign[:, l], -1.0, size[:, l], ALU.add, ALU.mult))
                    dve.sem_inc(rows_done, 1)

            @block.tensor
            def _(pe):
                pe.wait_ge(ident_done, 1)
                pe.wait_ge(silu_done, 1)
                for l in range(2):
                    for k in range(KD):
                        last = pe.transpose(cT_ps[:, l, k, :], c_silu[:, l, k * P:(k + 1) * P], g.ident[0:B, 0:B])
                last.then_inc(cT_done, 1)
                pe.wait_ge(cT_copied, 1)
                for l in range(2):
                    pe.wait_ge(wmod_in[l], 16)
                    for n in range(3):
                        cols = slice(n * 512, (n + 1) * 512)
                        for k in range(KD):
                            last = pe.matmul(mod_ps[0:B, l, cols], cT[:, l, k, :], wmod[:, l, k, cols],
                                             start=(k == 0), stop=(k == KD - 1))
                    last.then_inc(mod_done, 1)


def agent_attention(nc, mk, g):
    with ExitStack() as ctx:
        t = Maker(nc, ctx)
        h = t.sb("h0", [P, NT, D])
        prod = t.sb("prod", [P, TB, D])
        st, mv, var, rstd = (t.sb("st0", [P, TB, 6]), t.sb("mv0", [P, TB, 2]), t.sb("var0", [P, TB]),
                             t.sb("rstd0", [P, TB]))
        wconv_b = t.sb("wconv_b", [P, KD, P])
        wkT, wvT = t.sb("wkT", [P, KD, D]), t.sb("wvT", [P, KD, D])
        probe = t.sb("probe", [P, D])
        agent = t.sb("agent", [P, NT])
        score = t.sb("score", [P, NT])
        tok = t.sb("tok", [P, NT])
        masked = t.sb("masked", [P, 2, TB, B])
        mix = t.sb("mix", [B, D])
        mixT = t.sb("mixT", [P, KD, B])
        mixT_b = t.sb("mixT_b", [P, KD, B, P])
        keys = t.sb("keys", [B, D])
        small = t.sb("small", [P, 8])
        value_probe = t.sb("value_probe", [P, B, D])
        peak, peak_diag, neg_peak = t.sb("peak", [P, B]), t.sb("peak_diag", [B, B]), t.sb("neg_peak", [P, B])
        peak_row = t.sb("peak_row", [B, 1])
        part_sum, inv_sum = t.sb("part_sum", [P, B]), t.sb("inv_sum", [P, B])
        gated = t.sb("gated", [P, B, D])
        w_ps = t.ps("w_ps", [P, 2, 512])
        probe_ps = t.ps("probe_ps", [P, 512])
        mix_ps = t.ps("mix_ps", [P, B, D])
        wide_ps = t.ps("wide_ps", [P, B, D])
        tiny_ps = t.ps("tiny_ps", [P, 512])

        own, wb = mk.sem("aa_dve"), mk.sem("wconv_b_done")
        w_done, w_copied, probe_done = mk.sem("wT_done"), mk.sem("wT_copied"), mk.sem("probe_done")
        var_ready, rstd_ready, masked_ready, mix_done = (mk.sem("aa_var"), mk.sem("aa_rstd"), mk.sem("aa_masked"),
                                                         mk.sem("aa_mix"))
        normalised, scaled, rows_ready = mk.sem("aa_normalised"), mk.sem("aa_scaled"), mk.sem("aa_rows")
        mod = g.modb[:].rearrange("p b (s d) -> p b s d", s=6)

        with nc.Block() as block:
            @block.vector
            def _(dve):
                v = Steps(dve, own)
                for k in range(KD):
                    v.mark(dve.tensor_scalar(wconv_b[:, k, :], g.ones[:], g.wconv[:, k:k + 1], None, ALU.mult))
                v.sync()
                dve.sem_inc(wb, 1)
                dve.wait_ge(probe_done, 1)
                v(dve.tensor_copy(probe[:], probe_ps[:, 0:D]))

                def normalise(v, b):
                    layer_norm_stats(v, g.spare, st, mv, var, TB, lambda j: g.x[:, bass.ds(b * TB + j, 1), :], LN_EPS, var_ready)
                    dve.wait_ge(rstd_ready, b + 1)
                    for j in range(TB):
                        v.mark(dve.tensor_scalar(h[:, bass.ds(b * TB + j, 1), :], g.x[:, bass.ds(b * TB + j, 1), :],
                                                 mv[:, j, 0:1], rstd[:, j:j + 1], ALU.subtract, ALU.mult))
                    v.sync()
                    dve.sem_inc(normalised, 1)

                normalise(v, 0)
                per = 3 * TB + 3
                first = v.n

                def body(b, last):
                    v.start(b * per + first)
                    if not last:
                        normalise(v, b + 1)
                    rows = h[:, bass.ds(b * TB, TB), :]
                    dve.wait_ge(rows_ready, b + 1)
                    v(dve.tensor_tensor(prod[:], rows, probe[:].unsqueeze(1).to_broadcast([P, TB, D]), ALU.mult))
                    v(dve.tensor_reduce(agent[:, bass.ds(b * TB, TB)], prod[:], AX.X, ALU.add))
                    v(dve.tensor_tensor(masked[:, 0], agent[:, bass.ds(b * TB, TB)].unsqueeze(2).to_broadcast([P, TB, B]),
                                        g.eye_b[:, bass.ds(b, 1), :].to_broadcast([P, TB, B]), ALU.mult))
                    dve.wait_ge(mix_done, b + 1)
                    dve.tensor_scalar(masked[:, 1], masked[:, 0], float(D) ** -0.5, None, ALU.mult).then_inc(masked_ready, 1)
                    assert last or v.n == per, v.n

                dve.sem_inc(mix_done, 1)
                batches(dve, body)
                dve.wait_ge(mix_done, B + 1)
                dve.tensor_reduce(mix[:], mix_ps[0:B].rearrange("p b d -> p d b"), AX.X, ALU.add)

            @block.gpsimd
            def _(pool):
                pool.wait_ge(g.modb_in, 16)
                with pool.Fori(0, B) as b:
                    pool.wait_ge(var_ready, b + 1)
                    rsqrt_rows(pool, rstd, var, g.minus_half, TB, rstd_ready)
                    rows = h[:, bass.ds(b * TB, TB), :]
                    pool.wait_ge(normalised, b + 1)
                    pool.tensor_tensor(rows, rows, mod[:, bass.ds(b, 1), CA, :].to_broadcast([P, TB, D]), ALU.mult).then_inc(scaled, 1)
                    pool.wait_ge(scaled, b + 1)
                    pool.tensor_tensor(rows, rows, mod[:, bass.ds(b, 1), SA, :].to_broadcast([P, TB, D]), ALU.add).then_inc(rows_ready, 1)

            @block.scalar
            def _(act):
                act.wait_ge(w_done, 1)
                act.activation(wkT[:], w_ps[:, 0, :].rearrange("p (k d) -> p k d", k=KD), ACT.Copy).then_inc(w_copied, 1)
                act.activation(wvT[:], w_ps[:, 1, :].rearrange("p (k d) -> p k d", k=KD), ACT.Copy).then_inc(w_copied, 1)

            @block.tensor
            def _(pe):
                for half in range(2):
                    for k in range(KD):
                        for j in range(KD):
                            last = pe.transpose(w_ps[:, half, k * D + j * P:k * D + (j + 1) * P],
                                                g.wqkv[:, 2 + 2 * half + j, k * P:(k + 1) * P], g.ident[:])
                last.then_inc(w_done, 1)
                pe.wait_ge(wb, 1)
                for k in range(KD):
                    last = pe.matmul(probe_ps[:, 0:D], wconv_b[:, k, :], g.wqkv[:, k, :], start=(k == 0), stop=(k == KD - 1))
                last.then_inc(probe_done, 1)
                with pe.Fori(0, B) as b:
                    pe.wait_ge(masked_ready, b + 1)
                    for j in range(TB):
                        last = pe.matmul(mix_ps[0:B, bass.ds(b, 1), :], masked[:, 1, j, :], h[:, bass.ds(b * TB + j, 1), :],
                                         start=(j == 0), stop=(j == TB - 1))
                    last.then_inc(mix_done, 1)

        own = mk.sem("ab_dve")
        tp_done, tp_copied, keys_done, exp_done, attn_done, attnT_done = (
            mk.sem("mixT_done"), mk.sem("mixT_copied"), mk.sem("keys_done"), mk.sem("keys_exp"), mk.sem("attn_done"),
            mk.sem("attnT_done"))
        spread_done, probe2_done = mk.sem("spread_done"), mk.sem("value_probe_done")
        score_max, row_max, peak_ready, peak_done, neg_ready, score_exp, sums_done, masked2, mix2 = (
            mk.sem("score_max"), mk.sem("row_max"), mk.sem("peak_ready"), mk.sem("peak_done"), mk.sem("neg_ready"),
            mk.sem("score_exp"), mk.sem("sums_done"), mk.sem("masked2"), mk.sem("mix2"))
        mixT2_done, spread2_done, value_done, tok_exp = (
            mk.sem("mixT2_done"), mk.sem("spread2_done"), mk.sem("value_done"), mk.sem("tok_exp"))

        def spread(v, dve):
            for k in range(KD):
                v.mark(dve.tensor_copy(mixT_b[:, k], mixT[:, k, :].unsqueeze(2).to_broadcast([P, B, P])))
            v.sync()

        with nc.Block() as block:
            @block.vector
            def _(dve):
                v = Steps(dve, own)
                dve.sem_inc(mix2, 1)
                dve.wait_ge(tp_done, 1)
                dve.tensor_copy(mixT[:], tiny_ps[:, 0:KD * B].rearrange("p (k b) -> p k b", k=KD)).then_inc(tp_copied, 1)
                dve.wait_ge(keys_done, 1)
                v(dve.reduce_max(small[0:B, 0:1], wide_ps[0:B, 0, :], AX.X))
                v(dve.tensor_scalar(small[0:B, 1:2], small[0:B, 0:1], -1.0, None, ALU.mult))
                dve.sem_inc(attn_done, 1)
                dve.wait_ge(exp_done, 1)
                v(dve.reciprocal(small[0:B, 3:4], small[0:B, 2:3]))
                v(dve.tensor_scalar(keys[:], keys[:], small[0:B, 3:4], None, ALU.mult))
                dve.sem_inc(attn_done, 1)
                dve.wait_ge(attnT_done, 1)
                v(dve.tensor_copy(mixT[:], tiny_ps[:, 0:KD * B].rearrange("p (k b) -> p k b", k=KD)))
                spread(v, dve)
                dve.sem_inc(spread_done, 1)
                dve.wait_ge(probe2_done, 1)
                v(dve.tensor_copy(value_probe[:], wide_ps[:]))
                first = v.n
                with dve.Fori(0, B) as b:
                    v = Steps(dve, own, b * 3 + first)
                    v(dve.tensor_tensor(prod[:], h[:, bass.ds(b * TB, TB), :],
                                        value_probe[:, bass.ds(b, 1), :].to_broadcast([P, TB, D]), ALU.mult))
                    v(dve.tensor_reduce(score[:, bass.ds(b * TB, TB)], prod[:], AX.X, ALU.add))
                    v(dve.tensor_reduce(peak[:, bass.ds(b, 1)], score[:, bass.ds(b * TB, TB)], AX.X, ALU.max))
                v = Steps(dve, own, first + 3 * B)
                dve.sem_inc(score_max, 1)
                dve.wait_ge(row_max, 1)
                v(dve.reduce_max(peak_row[:], tiny_ps[0:B, 128:256], AX.X))
                v(dve.tensor_scalar(peak_diag[:], g.ident[0:B, 0:B], peak_row[:], -1.0, ALU.mult, ALU.mult))
                dve.sem_inc(peak_ready, 1)
                dve.wait_ge(peak_done, 1)
                v(dve.tensor_copy(neg_peak[:], tiny_ps[:, 256:256 + B]))
                v(dve.tensor_tensor(tok[:], agent[:], agent[:], ALU.subtract))
                dve.sem_inc(neg_ready, 1)
                dve.wait_ge(score_exp, 1)
                v(dve.tensor_reduce(part_sum[:], score[:].rearrange("p (b t) -> p b t", b=B), AX.X, ALU.add))
                dve.sem_inc(sums_done, 1)
                with dve.Fori(0, B) as b:
                    dve.wait_ge(mix2, b + 1)
                    dve.tensor_tensor(masked[:, 0], score[:, bass.ds(b * TB, TB)].unsqueeze(2).to_broadcast([P, TB, B]),
                                      g.eye_b[:, bass.ds(b, 1), :].to_broadcast([P, TB, B]), ALU.mult).then_inc(masked2, 1)
                dve.wait_ge(mix2, B + 1)
                v(dve.tensor_reduce(mix[:], mix_ps[0:B].rearrange("p b d -> p d b"), AX.X, ALU.add))
                dve.sem_inc(sums_done, 1)
                dve.wait_ge(mixT2_done, 1)
                v(dve.tensor_copy(mixT[:], tiny_ps[:, 0:KD * B].rearrange("p (k b) -> p k b", k=KD)))
                v(dve.reciprocal(inv_sum[:], tiny_ps[:, 260:260 + B]))
                spread(v, dve)
                dve.sem_inc(spread2_done, 1)
                dve.wait_ge(tok_exp, 1)
                v(dve.reciprocal(score[:], tok[:]))
                v(dve.tensor_tensor(tok[:], tok[:], score[:], ALU.mult))
                dve.wait_ge(value_done, 1)
                for b in range(B):
                    v.mark(dve.scalar_tensor_tensor(gated[:, b, :], wide_ps[:, b, :], inv_sum[:, b:b + 1],
                                                    mod[:, b, GA, :], ALU.mult, ALU.mult))
                v.sync()
                with dve.Fori(0, B) as b:
                    for j in range(TB):
                        rows = g.x[:, bass.ds(b * TB + j, 1), :]
                        dve.scalar_tensor_tensor(rows, gated[:, bass.ds(b, 1), :], tok[:, bass.ds(b * TB + j, 1)], rows,
                                                 ALU.mult, ALU.add)

            @block.scalar
            def _(act):
                act.wait_ge(attn_done, 1)
                act.activation(keys[:], wide_ps[0:B, 0, :], ACT.Exp, bias=small[0:B, 1:2],
                               accum_out=small[0:B, 2:3]).then_inc(exp_done, 1)
                act.wait_ge(neg_ready, 1)
                for b in range(B):
                    last = act.activation(score[:, b * TB:(b + 1) * TB], score[:, b * TB:(b + 1) * TB], ACT.Exp,
                                          bias=neg_peak[:, b:b + 1])
                last.then_inc(score_exp, 1)
                act.activation(tok[:], tok[:], ACT.Exp).then_inc(tok_exp, 1)

            @block.tensor
            def _(pe):
                def mixT_of(rows, done):
                    for k in range(KD):
                        last = pe.transpose(tiny_ps[:, k * B:(k + 1) * B], rows[:, k * P:(k + 1) * P], g.ident[0:B, 0:B])
                    last.then_inc(done, 1)

                mixT_of(mix, tp_done)
                pe.wait_ge(tp_copied, 1)
                for k in range(KD):
                    last = pe.matmul(wide_ps[0:B, 0, :], mixT[:, k, :], wkT[:, k, :], start=(k == 0), stop=(k == KD - 1))
                last.then_inc(keys_done, 1)
                pe.wait_ge(attn_done, 2)
                mixT_of(keys, attnT_done)
                pe.wait_ge(spread_done, 1)
                for b in range(B):
                    for k in range(KD):
                        last = pe.matmul(wide_ps[:, b, :], mixT_b[:, k, b, :], g.wqkv[:, 4 + k, :],
                                         start=(k == 0), stop=(k == KD - 1))
                last.then_inc(probe2_done, 1)
                pe.wait_ge(score_max, 1)
                pe.transpose(tiny_ps[0:B, 128:256], peak[:], g.ident[:]).then_inc(row_max, 1)
                pe.wait_ge(peak_ready, 1)
                pe.matmul(tiny_ps[:, 256:256 + B], g.ones[0:B, :], peak_diag[:], start=True, stop=True).then_inc(peak_done, 1)
                pe.wait_ge(neg_ready, 1)
                pe.wait_ge(sums_done, 1)
                pe.matmul(tiny_ps[:, 260:260 + B], g.ones[:], part_sum[:], start=True, stop=True)
                with pe.Fori(0, B) as b:
                    pe.wait_ge(masked2, b + 1)
                    for j in range(TB):
                        last = pe.matmul(mix_ps[0:B, bass.ds(b, 1), :], masked[:, 0, j, :], h[:, bass.ds(b * TB + j, 1), :],
                                         start=(j == 0), stop=(j == TB - 1))
                    last.then_inc(mix2, 1)
                pe.wait_ge(sums_done, 2)
                mixT_of(mix, mixT2_done)
                pe.wait_ge(spread2_done, 1)
                for b in range(B):
                    for k in range(KD):
                        last = pe.matmul(wide_ps[:, b, :], mixT_b[:, k, b, :], wvT[:, k, :],
                                         start=(k == 0), stop=(k == KD - 1))
                last.then_inc(value_done, 1)


RING = 8
TOP = 8


def expert_choice(nc, mk, g, a):
    HALF = T // 2
    LOW = 64
    ROWS = LOW + E
    with ExitStack() as ctx:
        t = Maker(nc, ctx)
        w1 = t.sb("w1", [P, RING, S, KD, M])
        w2 = t.sb("w2", [P, RING, S, KD, KS])
        b2_row = t.sb("b2_row", [1, RING, D])
        b1T = t.sb("b1T", [P, E * S, KD])
        index = t.sb("index", [P, E], U32)
        weight = t.sb("weight", [P, E])
        h_dram = nc.dram_tensor("h_dram", (T, D), F32, kind="Internal").ap()
        sum_dram = nc.dram_tensor("sum_dram", (T, D), F32, kind="Internal").ap()
        w_in = [mk.sem(f"w_in{q}") for q in range(RING)]
        mod = g.modb[:].rearrange("p b (s d) -> p b s d", s=6)

        def load_expert(eng, e, q):
            eng.dma_start(w1[:, q], a["L0_ffn_W1"][bass.ds(e, 1)].rearrange("a s (p k) m -> p (a s) k m", k=KD)).then_inc(w_in[q], 16)
            eng.dma_start(w2[:, q], a["L0_ffn_W2"][bass.ds(e, 1)].rearrange("a s (p k) n -> p (a s) k n", k=KD)).then_inc(w_in[q], 16)
            eng.dma_start(b2_row[:, q, :], a["L0_ffn_b2"][bass.ds(e, 1)].rearrange("a s n -> a (s n)")).then_inc(w_in[q], 16)

        with ExitStack() as c2:
            r = Maker(nc, c2)
            logits = r.sb("logits", [ROWS, HALF])
            with ExitStack() as c3:
                t = Maker(nc, c3)
                hg = t.sb("hg", [P, 2, G, D])
                hT = t.sb("hT", [P, 2, KD, GT])
                wr = t.sb("wr", [E, D])
                wrT = t.sb("wrT", [P, KD, E])
                b1_rows = t.sb("b1_rows", [2 * E, 2, M])
                zero = t.sb("zero", [P, 2048])
                st, mv, var, rstd = (t.sb("st1", [P, G, 6]), t.sb("mv1", [P, G, 2]), t.sb("var1", [P, G]),
                                     t.sb("rstd1", [P, G]))
                tp = t.ps("tp1", [P, 2, KD, GT])
                lp = t.ps("lp1", [P, 2, GT])
                own, var_ready, rstd_ready, h_ready = (mk.sem("ec_dve"), mk.sem("ec_var"), mk.sem("ec_rstd"),
                                                       mk.sem("ec_h"))
                turned, hT_ready, logits_done, logits_out = (mk.sem("ec_turned"), mk.sem("ec_hT"), mk.sem("ec_logits"),
                                                             mk.sem("ec_logits_out"))
                normalised = mk.sem("ec_normalised")
                h_out = [mk.sem("ec_h_out0"), mk.sem("ec_h_out1")]
                small_in, zeroed, zero_out, wrT_done, wrT_copied = (mk.sem("ec_small_in"), mk.sem("ec_zeroed"),
                                                                    mk.sem("ec_zero_out"), mk.sem("ec_wrT"),
                                                                    mk.sem("ec_wrT_copied"))
                with nc.Block() as block:
                    @block.sync
                    def _(sp):
                        with sp.Fori(0, B) as b:
                            for k in range(2):
                                sp.wait_ge(h_ready, 2 * b + k + 1)
                                sp.dma_start(h_dram[bass.ds((2 * b + k) * GT, GT), :].rearrange("(t p) d -> p t d", p=P),
                                             hg[:, k]).then_inc(h_out[k], 16)
                        for k in range(2):
                            sp.wait_ge(h_out[k], 16 * (B + 1))

                    @block.scalar
                    def _(act):
                        act.dma_start(wr[:], a["L0_ffn_Wr"]).then_inc(small_in, 16)
                        act.dma_start(b1_rows[:], a["L0_ffn_b1"].rearrange("e s m -> (e s) m").rearrange("(i r) m -> r i m", i=2)).then_inc(small_in, 16)
                        act.wait_ge(zeroed, 2)
                        for i in range(4):
                            act.dma_start(sum_dram.rearrange("(i p r) d -> i p (r d)", i=4, p=P)[i], zero[:]).then_inc(zero_out, 16)
                        act.wait_ge(wrT_done, 1)
                        act.activation(wrT[:], lp[:, 0, 0:KD * E].rearrange("p (k e) -> p k e", k=KD), ACT.Copy).then_inc(wrT_copied, 1)
                        act.activation(b1T[:].rearrange("p (i r) k -> p k i r", i=2),
                                       tp[:, 1, 0, 0:2 * 2 * 2 * E].rearrange("p (k i r) -> p k i r", k=KD, i=2),
                                       ACT.Copy).then_inc(wrT_copied, 1)
                        for half in range(2):
                            with act.Fori(0, B // 2) as i:
                                for k in range(2):
                                    n = 2 * i + k + half * NG // 2
                                    act.wait_ge(turned, n + 1 + 2)
                                    act.activation(hT[:, k], tp[:, k], ACT.Copy).then_inc(hT_ready, 1)
                                    act.wait_ge(logits_done, n + 1)
                                    rows = slice(LOW * half, LOW * half + E)
                                    act.activation(logits[rows, bass.ds((2 * i + k) * GT, GT)], lp[rows, k, :],
                                                   ACT.Copy).then_inc(logits_out, 1)
                        act.wait_ge(zero_out, 64)

                    @block.gpsimd
                    def _(pool):
                        pool.memset(zero[:], 0.0).then_inc(zeroed, 1)
                        with pool.Fori(0, NG) as n:
                            pool.wait_ge(var_ready, n + 1)
                            rsqrt_rows(pool, rstd, var, g.minus_half, G, rstd_ready)
                            b = n // (NG // B)
                            rows = hg[:, bass.ds(n % 2, 1)].rearrange("p a t d -> p (a t) d")
                            pool.wait_ge(normalised, n + 1)
                            pool.tensor_tensor(rows, rows, mod[:, bass.ds(b, 1), SB, :].to_broadcast([P, G, D]), ALU.add).then_inc(h_ready, 1)

                    @block.vector
                    def _(dve):
                        dve.memset(logits[32:64, :], LOWEST).then_inc(zeroed, 1)
                        dve.sem_inc(turned, 2)
                        dve.sem_inc(h_out[0], 16)
                        dve.sem_inc(h_out[1], 16)
                        per = 3 * G + 1
                        with dve.Fori(0, B) as b:
                            for k in range(2):
                                v = Steps(dve, own, (2 * b + k) * per)
                                tile = lambda j: g.x[:, bass.ds(b * TB + k * G + j, 1), :]
                                layer_norm_stats(v, g.spare, st, mv, var, G, tile, LN_EPS, var_ready)
                                dve.wait_ge(rstd_ready, 2 * b + k + 1)
                                dve.wait_ge(h_out[k], 16 * (b + 1))
                                dve.wait_ge(turned, 2 * b + k + 1)
                                for j in range(G):
                                    v.mark(dve.tensor_scalar(hg[:, k, j:j + 1, :], tile(j), mv[:, j, 0:1], rstd[:, j:j + 1],
                                                             ALU.subtract, ALU.mult))
                                v.sync()
                                v(dve.tensor_tensor(hg[:, k], hg[:, k], mod[:, bass.ds(b, 1), CB, :].to_broadcast([P, G, D]), ALU.mult))
                                dve.sem_inc(normalised, 1)
                                assert v.n == per

                    @block.tensor
                    def _(pe):
                        pe.wait_ge(small_in, 32)
                        for k in range(KD):
                            pe.transpose(lp[:, 0, k * E:(k + 1) * E], wr[:, k * P:(k + 1) * P], g.ident[0:E, 0:E])
                            for i in range(2):
                                last = pe.transpose(tp[:, 1, 0, (2 * k + i) * 2 * E:(2 * k + i + 1) * 2 * E],
                                                    b1_rows[:, i, k::KD], g.ident[0:2 * E, 0:2 * E])
                        last.then_inc(wrT_done, 1)
                        pe.wait_ge(wrT_copied, 2)
                        for half in range(2):
                            with pe.Fori(0, B // 2) as i:
                                for k in range(2):
                                    n = 2 * i + k + half * NG // 2
                                    pe.wait_ge(h_ready, n + 1)
                                    for j in range(G):
                                        for c in range(KD):
                                            last = pe.transpose(tp[:, k, c, j * P:(j + 1) * P], hg[:, k, j, c * P:(c + 1) * P],
                                                                g.ident[:])
                                    last.then_inc(turned, 1)
                                    pe.wait_ge(hT_ready, n + 1)
                                    for c in range(KD):
                                        last = pe.matmul(lp[LOW * half:LOW * half + E, k, :], wrT[:, c, :], hT[:, k, c, :],
                                                         start=(c == 0), stop=(c == KD - 1))
                                    last.then_inc(logits_done, 1)

            with ExitStack() as c3:
                t = Maker(nc, c3)
                top = t.sb("top", [ROWS, CAP])
                at = t.sb("at", [ROWS, CAP], U32)
                at_f = t.sb("at_f", [ROWS, CAP])
                both = t.sb("both", [P, 2, ROWS])
                rank0 = t.sb("rank0", [P, P])
                low = t.sb("low", [P, 2, E])
                take, best, chosen = t.sb("take", [P, E]), t.sb("best", [P, E]), t.sb("chosen", [P, E])
                rank_ps, low_ps, peak_ps, sum_ps = (t.ps("rank_ps", [P, 512]), t.ps("low_ps", [P, 512]),
                                                    t.ps("peak_ps", [P, 512]), t.ps("sum_ps", [P, 512]))
                own, found, ranked, copied, lowered, expd, expd_done, summed, row0 = (
                    mk.sem("top_dve"), mk.sem("top_found"), mk.sem("top_ranked"), mk.sem("top_copied"), mk.sem("top_lowered"),
                    mk.sem("top_shifted"), mk.sem("top_exp"), mk.sem("top_sum"), mk.sem("top_rank0"))
                with nc.Block() as block:
                    @block.sync
                    def _(sp):
                        for e in range(RING):
                            load_expert(sp, e, e)

                    @block.gpsimd
                    def _(pool):
                        pool.memset(rank0[:], 0.0).then_inc(row0, 1)
                        pool.wait_ge(row0, 1)
                        pool.memset(rank0[0:1, :], 1.0).then_inc(row0, 1)

                    @block.vector
                    def _(dve):
                        v = Steps(dve, own)
                        for n in range(CAP // TOP):
                            cols = slice(n * TOP, (n + 1) * TOP)
                            v(dve.max(top[:, cols], logits[:]))
                            v(dve.max_index(at[:, cols], top[:, cols], logits[:]))
                            if n < CAP // TOP - 1:
                                v(dve.match_replace(logits[:], top[:, cols], logits[:], LOWEST))
                        v(dve.tensor_copy(at_f[:], at[:]))
                        v(dve.tensor_scalar(at_f[LOW:ROWS, :], at_f[LOW:ROWS, :], float(HALF), None, ALU.add))
                        dve.sem_inc(found, 1)
                        dve.wait_ge(ranked, 1)
                        v(dve.tensor_copy(both[:], rank_ps[:, 0:2 * ROWS].rearrange("p (i r) -> p i r", i=2)))
                        dve.sem_inc(copied, 1)
                        dve.wait_ge(lowered, 1)
                        v(dve.tensor_copy(low[:], low_ps[:, 0:2 * E].rearrange("p (i e) -> p i e", i=2)))
                        v(dve.tensor_tensor(take[:], both[:, 0, 0:E], low[:, 0, :], ALU.is_ge))
                        v(dve.tensor_tensor(best[:], both[:, 0, 0:E], low[:, 0, :], ALU.max))
                        v(dve.tensor_tensor(chosen[:], both[:, 1, 0:E], low[:, 1, :], ALU.subtract))
                        v(dve.tensor_tensor(chosen[:], chosen[:], take[:], ALU.mult))
                        v(dve.tensor_tensor(chosen[:], chosen[:], low[:, 1, :], ALU.add))
                        v(dve.tensor_copy(index[:], chosen[:]))
                        v(dve.tensor_copy(take[:], peak_ps[:, 0:E]))
                        v(dve.tensor_tensor(take[:], take[:], peak_ps[:, E:2 * E], ALU.max))
                        v(dve.tensor_tensor(best[:], best[:], take[:], ALU.subtract))
                        dve.sem_inc(expd, 1)
                        dve.wait_ge(summed, 1)
                        v(dve.reciprocal(take[:], sum_ps[:, 0:E]))
                        v(dve.tensor_tensor(weight[:], best[:], take[:], ALU.mult))

                    @block.scalar
                    def _(act):
                        act.wait_ge(expd, 1)
                        act.activation(best[:], best[:], ACT.Exp).then_inc(expd_done, 1)

                    @block.tensor
                    def _(pe):
                        pe.wait_ge(found, 1)
                        pe.transpose(rank_ps[:, 0:ROWS], top[:], g.ident[0:ROWS, 0:ROWS])
                        pe.transpose(rank_ps[:, ROWS:2 * ROWS], at_f[:], g.ident[0:ROWS, 0:ROWS]).then_inc(ranked, 1)
                        pe.wait_ge(copied, 1)
                        pe.wait_ge(row0, 2)
                        pe.matmul(peak_ps[:, 0:E], rank0[:], both[:, 0, 0:E], start=True, stop=True)
                        pe.matmul(peak_ps[:, E:2 * E], rank0[:], both[:, 0, LOW:ROWS], start=True, stop=True)
                        pe.matmul(low_ps[:, 0:E], g.flip[:], both[:, 0, LOW:ROWS], start=True, stop=True)
                        pe.matmul(low_ps[:, E:2 * E], g.flip[:], both[:, 1, LOW:ROWS], start=True, stop=True).then_inc(lowered, 1)
                        pe.wait_ge(expd_done, 1)
                        pe.matmul(sum_ps[:, 0:E], g.ones[:], best[:], start=True, stop=True).then_inc(summed, 1)

        with ExitStack() as c2:
            t = Maker(nc, c2)
            XG = 8
            slot = t.sb("slot", [P, XG, 1], U32)
            xg = t.sb("xg", [P, XG, D])
            xT = t.sb("xT", [P, 2, KD, P])
            pre = t.sb("pre", [P, 2, S * KD, P])
            act_h = t.sb("act_h", [P, 2, S * KD, P])
            y = t.sb("y", [P, 2, D])
            x_ps = t.ps("x_ps", [P, 2, 512])
            h_ps = t.ps("h_ps", [P, 2, S * KD, P])
            y_ps = t.ps("y_ps", [P, 2, 512])
            xg_in = [mk.sem(f"xg_in{q}") for q in range(XG)]
            slot_set, turned, xT_ready, up_done, biased, gelu_done, down_done, y_ready, added = (
                mk.sem("slot_set"), mk.sem("xg_turned"), mk.sem("xT_ready"), mk.sem("up_done"), mk.sem("biased"),
                mk.sem("gelu_done"), mk.sem("down_done"), mk.sem("y_ready"), mk.sem("added"))
            carried, y_free = mk.sem("pool_carried"), mk.sem("y_free")
            LAST = E // RING - 1

            def bodies(eng, body):
                with eng.Fori(0, LAST) as i:
                    for q in range(RING):
                        body(i * RING + q, q, False)
                for q in range(RING):
                    body(LAST * RING + q, q, True)

            with nc.Block() as block:
                @block.sync
                def _(sp):
                    with sp.Fori(0, LAST) as i:
                        for q in range(RING):
                            e = i * RING + q
                            sp.wait_ge(down_done, e + 1)
                            load_expert(sp, e + RING, q)

                @block.gpsimd
                def _(pool):
                    def carry_wait(n):
                        pool.wait_ge(carried, n + 1)
                        pool.tensor_tensor(g.pool_spare[:], g.minus_half[:, 0:1], g.minus_half[:, 0:1],
                                           ALU.add).then_inc(carried, 1)

                    def gather(e, q, n):
                        pool.tensor_copy(slot[:, q], index[:, bass.ds(e, 1)]).then_inc(slot_set, 1)
                        pool.wait_ge(slot_set, e + 1)
                        carry_wait(n)
                        pool.indirect_dma_start(out=xg[:, q, :], out_offset=None, in_=h_dram,
                                                in_offset=bass.IndirectOffsetOnAxis(ap=slot[:, q], axis=0)).then_inc(xg_in[q], 16)

                    pool.sem_inc(carried, 1)
                    pool.sem_inc(y_free, 2)
                    pool.sem_inc(turned, 1)
                    for e in range(XG - 1):
                        gather(e, e, e)

                    def body(e, q, last):
                        pool.wait_ge(y_ready, e + 1)
                        carry_wait(XG - 1 + 2 * e - (max(0, q + XG - 1 - RING) if last else 0))
                        pool.indirect_dma_start(out=sum_dram, out_offset=bass.IndirectOffsetOnAxis(ap=slot[:, q % XG], axis=0),
                                                in_=y[:, q % 2, :], in_offset=None, compute_op=ALU.add).then_inc(added, 16)
                        if not last or q + XG - 1 < RING:
                            pool.wait_ge(turned, e + 1)
                            gather(e + XG - 1, (q + XG - 1) % XG, XG + 2 * e)
                        pool.wait_ge(added, 16 * (e + 1))
                        pool.sem_inc(y_free, 1)

                    bodies(pool, body)
                    pool.wait_ge(added, 16 * E)

                @block.scalar
                def _(act):
                    def x_copy(e, q):
                        act.wait_ge(turned, e + 2)
                        act.activation(xT[:, q % 2], x_ps[:, q % 2, 0:D].rearrange("p (k n) -> p k n", k=KD), ACT.Copy).then_inc(xT_ready, 1)

                    x_copy(0, 0)

                    def body(e, q, last):
                        if not last or q + 1 < RING:
                            x_copy(e + 1, q + 1)
                        act.wait_ge(biased, e + 1)
                        act.activation(act_h[:, q % 2], pre[:, q % 2], ACT.Gelu).then_inc(gelu_done, 1)

                    bodies(act, body)

                @block.vector
                def _(dve):
                    def bias(e, q):
                        dve.wait_ge(up_done, e + 1)
                        dve.tensor_tensor(pre[:, q % 2], h_ps[:, q % 2],
                                          b1T[:, bass.ds(e * S, S), :].rearrange("p s k -> p (s k)").unsqueeze(2)
                                          .to_broadcast([P, S * KD, P]), ALU.add).then_inc(biased, 1)

                    bias(0, 0)

                    def body(e, q, last):
                        if not last or q + 1 < RING:
                            bias(e + 1, q + 1)
                        dve.wait_ge(down_done, e + 1)
                        dve.wait_ge(y_free, e + 1)
                        dve.tensor_scalar(y[:, q % 2, :], y_ps[:, q % 2, 0:D], weight[:, bass.ds(e, 1)], None,
                                          ALU.mult).then_inc(y_ready, 1)

                    bodies(dve, body)

                @block.tensor
                def _(pe):
                    def turn(e, q):
                        pe.wait_ge(xg_in[q % XG], 16 * (q // XG + 1) + (e - q) * (16 // XG))
                        for k in range(KD):
                            last = pe.transpose(x_ps[:, q % 2, k * P:(k + 1) * P], xg[:, q % XG, k::KD], g.ident[:])
                        last.then_inc(turned, 1)

                    def up(e, q):
                        pe.wait_ge(w_in[q], 48 + (e - q) * (48 // RING))
                        pe.wait_ge(xT_ready, e + 1)
                        for s in range(S):
                            for c in range(KD):
                                for k in range(KD):
                                    last = pe.matmul(h_ps[:, q % 2, s * KD + c, :], w1[:, q, s, k, c::KD], xT[:, q % 2, k, :],
                                                     start=(k == 0), stop=(k == KD - 1))
                        last.then_inc(up_done, 1)

                    def down(e, q):
                        pe.wait_ge(gelu_done, e + 1)
                        pe.matmul(y_ps[:, q % 2, 0:D], g.ones[0:1, :], b2_row[:, q, :], start=True, stop=False)
                        for s in range(S):
                            cols = slice(s * KS, (s + 1) * KS)
                            for c in range(KD):
                                last = pe.matmul(y_ps[:, q % 2, cols], act_h[:, q % 2, s * KD + c, :], w2[:, q, s, c, :],
                                                 start=False, stop=(s == S - 1 and c == KD - 1))
                        last.then_inc(down_done, 1)

                    turn(0, 0)
                    up(0, 0)
                    turn(1, 1)

                    def body(e, q, last):
                        if not last or q + 1 < RING:
                            up(e + 1, (q + 1) % RING)
                        if not last or q + 2 < RING:
                            turn(e + 2, (q + 2) % RING)
                        down(e, q)

                    bodies(pe, body)

        with ExitStack() as c2:
            t = Maker(nc, c2)
            PARTS = 4
            part = t.sb("part", [P, PARTS, G, D])
            part_in = [mk.sem(f"part_in{i}") for i in range(PARTS)]
            used, own = mk.sem("part_used"), mk.sem("part_dve")
            with nc.Block() as block:
                @block.sync
                def _(sp):
                    sp.sem_inc(used, PARTS)
                    with sp.Fori(0, NG // PARTS) as r:
                        for i in range(PARTS):
                            n = r * PARTS + i
                            sp.wait_ge(used, n + 1)
                            sp.dma_start(part[:, i], sum_dram[bass.ds(n * GT, GT), :]
                                         .rearrange("(t p) d -> p t d", p=P)).then_inc(part_in[i], 16)

                @block.vector
                def _(dve):
                    with dve.Fori(0, NG // PARTS) as r:
                        for i in range(PARTS):
                            n, b = r * PARTS + i, r * (PARTS // 2) + i // 2
                            v = Steps(dve, own, n)
                            dve.wait_ge(part_in[i], 16 * (r + 1))
                            v(dve.tensor_tensor(part[:, i], part[:, i], mod[:, bass.ds(b, 1), GB, :].to_broadcast([P, G, D]), ALU.mult))
                            rows = g.x[:, bass.ds(n * G, G), :]
                            dve.tensor_tensor(rows, rows, part[:, i], ALU.add).then_inc(used, 1)
        mk.clear_signals()


class Heads:

    USES = KD + CH
    SQ = 4

    def __init__(self, mk, t, tag):
        sem = lambda n: mk.sem(f"{tag}_{n}")
        pair = lambda n, shape: (t.sb(f"{tag}_{n}_hi", shape, F32R), t.sb(f"{tag}_{n}_lo", shape, F32R))
        self.turned, self.w = pair("turned", [P, KD, GT]), pair("w", [P, KD, HD])
        self.scaled = t.sb(f"{tag}_scaled", [P, CH, GT])
        self.squares = t.sb(f"{tag}_squares", [P, self.SQ, GT])
        self.half_diag = t.sb(f"{tag}_half_diag", [P, 2, G, H])
        self.ring = t.ps(f"{tag}_ring", [P, 2, 512])
        self.diag_ps = t.ps(f"{tag}_diag_ps", [P, 512])
        self.full, self.free, self.turned_high = sem("full"), sem("free"), sem("turned_high")
        self.diag_done, self.diag_copied = sem("diag_done"), sem("diag_copied")
        self.w_in, self.w_high, self.w_low = sem("w_in"), sem("w_high"), sem("w_low")
        self.raw = self.scaled[:, 0:KD * HD // GT, :].rearrange("p a n -> p (a n)")

    def flat(self, part):
        return part[:].rearrange("p k n -> p (k n)")

    def load(self, sp, w):
        sp.dma_start(self.raw.rearrange("p (k n) -> p k n", k=KD), w.rearrange("(k p) h d -> p k (h d)", p=P)).then_inc(self.w_in, 16)

    def start_act(self, act):
        act.sem_inc(self.free, 2)
        act.sem_inc(self.diag_copied, 1)
        act.sem_inc(self.diag_done, 1)
        act.wait_ge(self.w_in, 16)
        act.activation(self.flat(self.w[0]), self.raw, ACT.Copy).then_inc(self.w_high, 1)

    def copy(self, act, n, k):
        uses = n * self.USES
        for c in range(KD):
            act.wait_ge(self.full, uses + c + 1)
            act.activation(self.turned[0][:, c, :], self.ring[:, c, :], ACT.Copy).then_inc(self.turned_high, 1)
        for c in range(CH):
            act.wait_ge(self.full, uses + KD + c + 1)
            act.activation(self.scaled[:, c, :], self.ring[:, c % 2, :], ACT.Copy, scale=DN)
            act.wait_ge(self.diag_done, n * CH + max(c - self.SQ + 1, 0) + 1)
            act.activation(self.squares[:, c % self.SQ, :], self.ring[:, c % 2, :], ACT.Square, scale=DN).then_inc(self.free, 1)

    def copy_diag(self, act, n, k):
        act.wait_ge(self.diag_done, (n + 1) * CH + 1)
        act.activation(self.half_diag[:, k].rearrange("p j h -> p (j h)"), self.diag_ps[:, 0:G * H], ACT.Copy).then_inc(self.diag_copied, 1)

    def weights_low(self, dve):
        dve.wait_ge(self.w_high, 1)
        dve.tensor_tensor(self.flat(self.w[1]), self.raw, self.flat(self.w[0]).bitcast(F32), ALU.subtract).then_inc(self.w_low, 1)

    def turned_low(self, dve, n):
        for c in range(KD):
            dve.wait_ge(self.turned_high, n * KD + c + 1)
            dve.tensor_tensor(self.turned[1][:, c, :], self.ring[:, c, :], self.turned[0][:, c, :].bitcast(F32),
                              ALU.subtract).then_inc(self.free, 1)

    def diag(self, pe, n, c, half_heads):
        pe.wait_ge(self.free, n * self.USES + KD + c + 1 + 2)
        if c == 0:
            pe.wait_ge(self.diag_copied, n + 1)
        for j in range(G):
            last = pe.matmul(self.diag_ps[:, j * H + 2 * c:j * H + 2 * c + 2], self.squares[:, c % self.SQ, j * P:(j + 1) * P],
                             half_heads, start=True, stop=True)
        last.then_inc(self.diag_done, 1)

    def project(self, pe, n, rows, ident, half_heads, before=None):
        uses = n * self.USES

        def take(i):
            if i < 2 and before:
                before(i)
            pe.wait_ge(self.free, uses + i + 1)

        for c in range(KD):
            take(c)
            for j in range(G):
                last = pe.transpose(self.ring[:, c, j * P:(j + 1) * P], rows[:, j, c * P:(c + 1) * P], ident)
            last.then_inc(self.full, 1)
        pe.wait_ge(self.free, uses + KD + 2)
        for c in range(CH):
            take(KD + c)
            for k in range(KD):
                w, x, out = [w[:, k, c * P:(c + 1) * P] for w in self.w], [x[:, k, :] for x in self.turned], self.ring[:, c % 2, :]
                pe.matmul(out, w[0], x[0], start=(k == 0), stop=False)
                pe.matmul(out, w[0], x[1], start=False, stop=False)
                last = pe.matmul(out, w[1], x[0], start=False, stop=(k == KD - 1))
            last.then_inc(self.full, 1)
            if c >= 2:
                self.diag(pe, n, c - 2, half_heads)

    def rest_of_diag(self, pe, n, half_heads):
        for c in (CH - 2, CH - 1):
            self.diag(pe, n, c, half_heads)


def random_features(pe, dash, scaled, j, features):
    for c in range(CH):
        last = pe.matmul(dash[:, c * P:(c + 1) * P], scaled[:, c, j * P:(j + 1) * P], features, start=True, stop=True)
    return last


def performer(nc, mk, g, a):
    USES = Heads.USES
    with ExitStack() as ctx:
        t = Maker(nc, ctx)
        h_dram = nc.dram_tensor("h1_dram", (T, D), F32, kind="Internal").ap()
        y_dram = nc.dram_tensor("y1_dram", (T, D), F32, kind="Internal").ap()
        kv_out = t.sb("kv_out", [P, B, CH, D])
        wide = t.sb("wide", [P, TB, HD])
        k_dash, ksum, q_dash, qn = wide, wide[:, 0:B, :], wide[:, B:B + 2, :], wide[:, B + 2:B + 4, :]
        features = t.sb("features", [P, P])
        half_heads = t.sb("half_heads", [P, 2])
        mod = g.modb[:].rearrange("p b (s d) -> p b s d", s=6)
        wide_in = mk.sem("pf_weights_in")

        with ExitStack() as c1:
            r = Maker(nc, c1)
            wv = r.sb("wv", [P, KD, HD])
            a_sum = kv_out
            k_sum = r.sb("k_sum", [P, B, CH])
            h_sum = r.sb("h_sum", [P, B, D + 1])
            peak = r.sb("key_peak", [P, B])
            with ExitStack() as c2:
                t = Maker(nc, c2)
                RING = 4
                hk = t.sb("hk", [P, RING, G, D + 1])
                heads = Heads(mk, t, "k")
                kT, ring, free = heads.scaled, heads.ring, heads.free
                dash = k_dash
                proj2 = t.sb("proj2", [MF, 2, DH])
                row_peak, tile_peak = t.sb("row_peak", [P, G]), t.sb("tile_peak", [P, 1])
                neg_peak, ratio = t.sb("neg_peak1", [P, 1]), t.sb("ratio", [P, 1])
                st, mv, var, rstd = (t.sb("st2", [P, G, 6]), t.sb("mv2", [P, G, 2]), t.sb("var2", [P, G]),
                                     t.sb("rstd2", [P, G]))
                dash_ps = t.ps("k_dash_ps", [P, 2, HD])
                h_sum_ps = t.ps("h_sum_ps", [P, 512])
                own, var_ready, rstd_ready, h_ready = mk.sem("pk_dve"), mk.sem("pk_var"), mk.sem("pk_rstd"), mk.sem("pk_h")
                dash_done, dash_used = mk.sem("k_dash_done"), mk.sem("k_dash_used")
                h_out = [mk.sem(f"h1_out{i}") for i in range(RING)]
                mod_in, proj_in, proj_done, const_done = mk.sem("mod1_in"), mk.sem("proj_in"), mk.sem("proj_turned"), mk.sem("pk_const")
                carried, sums_done, sums_used = mk.sem("pk_carried"), mk.sem("k_sums_done"), mk.sem("k_sums_used")
                peak_part, peak_all, neg_ready, exp_done, h_sum_done, h_sum_used = (
                    mk.sem("peak_part"), mk.sem("peak_all"), mk.sem("neg_peak_ready"), mk.sem("k_exp"), mk.sem("h_sum_done"),
                    mk.sem("h_sum_used"))
                TURNS = NG // RING

                def groups(eng, body):
                    with eng.Fori(0, TURNS - 1) as r:
                        for i in range(RING):
                            body(r * RING + i, i, r, False)
                    for i in range(RING):
                        body((TURNS - 1) * RING + i, i, TURNS - 1, True)

                with nc.Block() as block:
                    @block.sync
                    def _(sp):
                        for k in range(2):
                            sp.dma_start(proj2[:, k, :], a["L1_attn_proj"]).then_inc(proj_in, 16)
                        sp.dma_start(g.modb[:], g.mod_dram[1].partition_broadcast(P)).then_inc(mod_in, 16)
                        heads.load(sp, a["L1_attn_Wk"])
                        sp.dma_start(wv[:], a["L1_attn_Wv"].rearrange("(k p) h d -> p k (h d)", p=P)).then_inc(wide_in, 16)
                        with sp.Fori(0, TURNS) as r:
                            for i in range(RING):
                                n = r * RING + i
                                sp.wait_ge(h_ready, n + 1)
                                sp.dma_start(h_dram[bass.ds(n * GT, GT), :].rearrange("(t p) d -> p t d", p=P),
                                             hk[:, i, :, 0:D]).then_inc(h_out[i], 16)
                        for i in range(RING):
                            sp.wait_ge(h_out[i], 16 * (TURNS + 1))
                        sp.wait_ge(wide_in, 16)

                    @block.gpsimd
                    def _(pool):
                        def power(n):
                            pool.wait_ge(var_ready, n + 1)
                            rsqrt_rows(pool, rstd, var, g.minus_half, G, rstd_ready)

                        def keys(n):
                            pool.wait_ge(carried, n + 1)
                            pool.wait_ge(peak_part, n + 1)
                            pool.tensor_tensor(g.pool_spare[:], tile_peak[:], tile_peak[:], ALU.add).then_inc(carried, 1)
                            pool.partition_all_reduce(g.pool_max[:], tile_peak[:], P, bass.bass_isa.ReduceOp.max).then_inc(peak_all, 1)

                        pool.sem_inc(carried, 1)
                        power(0)
                        power(1)
                        keys(0)

                        def body(n, i, r, last):
                            if not last or i + 2 < RING:
                                power(n + 2)
                            if not last or i + 1 < RING:
                                keys(n + 1)

                        groups(pool, body)

                    @block.vector
                    def _(dve):
                        v = Steps(dve, own)
                        dve.sem_inc(dash_used, 2)
                        dve.sem_inc(sums_used, 2)
                        dve.sem_inc(h_sum_used, 1)
                        for i in range(RING):
                            dve.sem_inc(h_out[i], 16)
                        v.mark(dve.memset(features[:], 0.0))
                        v.mark(dve.memset(half_heads[:], 0.0))
                        v.mark(dve.memset(hk[:].rearrange("p i t d -> p (i t) d")[:, :, D:D + 1], 1.0))
                        v.sync()
                        v.mark(dve.memset(half_heads[0:DH, 0:1], 0.5))
                        v.mark(dve.memset(half_heads[DH:P, 1:2], 0.5))
                        dve.wait_ge(proj_done, 1)
                        for i in range(2):
                            at = slice(i * DH, (i + 1) * DH)
                            v.mark(dve.tensor_copy(features[at, i * MF:(i + 1) * MF], ring[at, 0, 0:MF]))
                        v.sync()
                        dve.sem_inc(const_done, 1)

                        def prepare(v, n, i, r, b):
                            tile = lambda j: g.x[:, bass.ds(n * G + j, 1), :]
                            layer_norm_stats(v, g.spare, st, mv, var, G, tile, LN_EPS, var_ready)
                            dve.wait_ge(rstd_ready, n + 1)
                            dve.wait_ge(h_out[i], 16 * (r + 1))
                            for j in range(G):
                                v.mark(dve.tensor_scalar(hk[:, i, j:j + 1, 0:D], tile(j), mv[:, j, 0:1], rstd[:, j:j + 1],
                                                         ALU.subtract, ALU.mult))
                            v.sync()
                            dve.wait_ge(mod_in, 16)
                            rows = hk[:, i, :, 0:D]
                            v(dve.tensor_tensor(rows, rows, mod[:, bass.ds(b, 1), CA, :].to_broadcast([P, G, D]), ALU.mult))
                            dve.tensor_tensor(rows, rows, mod[:, bass.ds(b, 1), SA, :].to_broadcast([P, G, D]),
                                              ALU.add).then_inc(h_ready, 1)

                        def shift(v, n, k):
                            for j in range(G):
                                dve.wait_ge(dash_done, n * G + j + 1)
                                v.mark(dve.reduce_max(row_peak[:, j:j + 1], dash_ps[:, j % 2, :], AX.X))
                                if j == 0:
                                    dve.wait_ge(heads.diag_copied, n + 2)
                                v.mark(dve.tensor_tensor(dash[:, k * G + j, :].rearrange("p (h m) -> p h m", h=H),
                                                         dash_ps[:, j % 2, :].rearrange("p (h m) -> p h m", h=H),
                                                         heads.half_diag[:, k, j, :].unsqueeze(2).to_broadcast([P, H, MF]), ALU.subtract))
                                v.sync()
                                dve.sem_inc(dash_used, 1)
                            v(dve.reduce_max(tile_peak[:], row_peak[:], AX.X))
                            dve.sem_inc(peak_part, 1)

                        def refer(v, n, k, b):
                            so_far = peak[:, bass.ds(b, 1)]
                            dve.wait_ge(peak_all, n + 1)
                            if k == 0:
                                v(dve.tensor_copy(so_far, g.pool_max[:]))
                            else:
                                v(dve.tensor_copy(neg_peak[:], so_far))
                                v(dve.tensor_tensor(so_far, so_far, g.pool_max[:], ALU.max))
                                v(dve.tensor_tensor(ratio[:], neg_peak[:], so_far, ALU.subtract))
                            dve.tensor_scalar(neg_peak[:], so_far, -1.0, None, ALU.mult).then_inc(neg_ready, 1)

                        def add_sums(v, n, k, b, ref=None):
                            for c in range(CH):
                                if c == 2 and ref:
                                    ref()
                                a_out = a_sum[:, bass.ds(b, 1), c, :]
                                k_out = k_sum[:, bass.ds(b, 1), c:c + 1]
                                a_in, k_in = ring[:, c % 2, 0:D].unsqueeze(1), ring[:, c % 2, D:D + 1].unsqueeze(1)
                                dve.wait_ge(sums_done, n * CH + c + 1)
                                if k == 0:
                                    v.mark(dve.tensor_copy(a_out, a_in))
                                    v.mark(dve.tensor_copy(k_out, k_in))
                                else:
                                    v.mark(dve.scalar_tensor_tensor(a_out, a_out, ratio[:], a_in, ALU.mult, ALU.add))
                                    v.mark(dve.scalar_tensor_tensor(k_out, k_out, ratio[:], k_in, ALU.mult, ALU.add))
                                v.sync()
                                dve.sem_inc(sums_used, 1)
                            if k:
                                dve.wait_ge(h_sum_done, b + 1)
                                v(dve.tensor_copy(h_sum[:, bass.ds(b, 1), :], h_sum_ps[:, 0:D + 1].unsqueeze(1)))
                                dve.sem_inc(h_sum_used, 1)

                        prepare(v, 0, 0, 0, 0)
                        heads.weights_low(dve)
                        heads.turned_low(dve, 0)
                        prepare(v, 1, 1, 0, 0)
                        shift(v, 0, 0)
                        refer(v, 0, 0, 0)
                        first = v.n
                        PREP, SHIFT, SUMS = 3 * G + 1, 2 * G + 1, 2 * CH
                        per = RING * (PREP + SHIFT + SUMS) + RING // 2 * (1 + 3 + 1)

                        def body(n, i, r, last):
                            b = r * (RING // 2) + i // 2
                            if i == 0:
                                v.start(r * per + first)
                            if not last or i + 1 < RING:
                                heads.turned_low(dve, n + 1)
                            if not last or i + 2 < RING:
                                prepare(v, n + 2, (i + 2) % RING, r + (i + 2) // RING, b + 1)
                            more = not last or i + 1 < RING
                            if more:
                                shift(v, n + 1, (i + 1) % 2)
                            add_sums(v, n, i % 2, b, (lambda: refer(v, n + 1, (i + 1) % 2, b + i % 2)) if more else None)
                            assert last or i < RING - 1 or v.n == per, (v.n, per)

                        groups(dve, body)

                    @block.scalar
                    def _(act):
                        heads.start_act(act)

                        def keys(n, k):
                            heads.copy(act, n, k)
                            heads.copy_diag(act, n, k)

                        def exps(n, k):
                            act.wait_ge(neg_ready, n + 1)
                            if k:
                                act.activation(ratio[:], ratio[:], ACT.Exp)
                            for j in range(k * G, k * G + G):
                                last = act.activation(dash[:, j, :], dash[:, j, :], ACT.Exp, bias=neg_peak[:])
                            last.then_inc(exp_done, 1)

                        keys(0, 0)
                        exps(0, 0)

                        def body(n, i, r, last):
                            if not last or i + 1 < RING:
                                keys(n + 1, (i + 1) % 2)
                                exps(n + 1, (i + 1) % 2)

                        groups(act, body)

                    @block.tensor
                    def _(pe):
                        pe.wait_ge(proj_in, 32)
                        pe.transpose(ring[:, 0, 0:MF], proj2[:].rearrange("m i d -> m (i d)"), g.ident[0:MF, 0:MF]).then_inc(proj_done, 1)
                        pe.wait_ge(const_done, 1)
                        pe.wait_ge(heads.w_low, 1)

                        def keys(n, i, before):
                            pe.wait_ge(h_ready, n + 1)
                            heads.project(pe, n, hk[:, i], g.ident[:], half_heads[:], before)
                            pe.wait_ge(free, (n + 1) * USES + 2)
                            for j in range(G):
                                if j == 2:
                                    heads.rest_of_diag(pe, n, half_heads[:])
                                pe.wait_ge(dash_used, n * G + j + 1)
                                random_features(pe, dash_ps[:, j % 2], kT, j, features[:]).then_inc(dash_done, 1)

                        def sums(n, i, b, alone):
                            k = i % 2
                            pe.wait_ge(exp_done, n + 1)
                            if k == 0:
                                pe.wait_ge(h_sum_used, b + 1)
                            for c in range(CH):
                                if c < 2 and not alone:
                                    pe.wait_ge(free, (n + 1) * USES + CH + c + 1 + 2)
                                else:
                                    pe.wait_ge(sums_used, n * CH + c + 1)
                                for j in range(G):
                                    last = pe.matmul(ring[:, c % 2, 0:D + 1], dash[:, k * G + j, c * P:(c + 1) * P], hk[:, i, j, :],
                                                     start=(j == 0), stop=(j == G - 1))
                                last.then_inc(sums_done, 1)
                            for j in range(G):
                                last = pe.matmul(h_sum_ps[:, 0:D + 1], g.ones[:], hk[:, i, j, :],
                                                 start=(k == 0 and j == 0), stop=(k == 1 and j == G - 1))
                            if k:
                                last.then_inc(h_sum_done, 1)

                        keys(0, 0, None)

                        def body(n, i, r, last):
                            more = not last or i + 1 < RING
                            if more:
                                keys(n + 1, (i + 1) % RING, lambda c: pe.wait_ge(sums_used, n * CH + c + 1))
                            sums(n, i, r * (RING // 2) + i // 2, not more)

                        groups(pe, body)

            with ExitStack() as c2:
                t = Maker(nc, c2)
                wo = t.sb("wo", [P, CH, D])
                sums = t.sb("sums", [P, CH, D])
                sumsT = t.sb("sumsT", [P, CH, KD, P])
                h_eps, k_col, k_diag = t.sb("h_eps", [P, D + 1]), t.sb("k_col", [P, CH]), t.sb("k_diag", [P, CH, P])
                kv = t.sb("kv", [P, CH, P])
                common, alpha = t.sb("common", [P, 1]), t.sb("alpha", [P, B])
                big_ps = t.ps("big_ps", [P, CH, KD, P])
                kv_ps = t.ps("kv_ps", [P, CH, P])
                ks_ps = t.ps("ks_ps", [P, CH, P])
                own, alpha_in, alpha_done, sums_ready, turned, turned_out, kv_done, kv_ready, out_done, out_copied = (
                    mk.sem("kc_dve"), mk.sem("alpha_in"), mk.sem("alpha_done"), mk.sem("kc_sums"), mk.sem("kc_turned"),
                    mk.sem("kc_turned_out"), mk.sem("kc_kv_done"), mk.sem("kc_kv_ready"), mk.sem("kc_out_done"),
                    mk.sem("kc_out_copied"))
                diag_ready, ks_done, wo_in = mk.sem("kc_diag"), mk.sem("kc_ks_done"), mk.sem("wo_in")
                with nc.Block() as block:
                    @block.sync
                    def _(sp):
                        sp.dma_start(wo[:], a["L1_attn_Wo"].rearrange("h d o -> (h d) o").rearrange("(c p) o -> p c o", p=P)).then_inc(wo_in, 16)

                    @block.vector
                    def _(dve):
                        v = Steps(dve, own)
                        v.mark(dve.memset(kv[:], 0.0))
                        v(dve.reduce_max(common[:], peak[:], AX.X))
                        v(dve.tensor_scalar(alpha[:], peak[:], common[:], None, ALU.subtract))
                        dve.sem_inc(alpha_in, 1)
                        dve.wait_ge(alpha_done, 1)

                        def sums_of(v, b):
                            scale = alpha[:, bass.ds(b, 1)]
                            v.mark(dve.tensor_scalar(h_eps[:], h_sum[:, bass.ds(b, 1), :].rearrange("p a d -> p (a d)"), KERN_EPS,
                                                     None, ALU.mult))
                            v.mark(dve.tensor_scalar(sums[:], a_sum[:, bass.ds(b, 1)].rearrange("p a c d -> p (a c) d"), scale, None, ALU.mult))
                            v.mark(dve.tensor_scalar(k_col[:], k_sum[:, bass.ds(b, 1), :].rearrange("p a c -> p (a c)"), scale, None, ALU.mult))
                            v.sync()
                            v.mark(dve.tensor_tensor(sums[:], sums[:], h_eps[:, 0:D].unsqueeze(1).to_broadcast([P, CH, D]), ALU.add))
                            v.mark(dve.tensor_scalar(k_col[:], k_col[:], h_eps[:, D:D + 1], None, ALU.add))
                            v.sync()
                            dve.sem_inc(sums_ready, 1)
                            v(dve.tensor_tensor(k_diag[:], g.ident[:].unsqueeze(1).to_broadcast([P, CH, P]),
                                                k_col[:].unsqueeze(2).to_broadcast([P, CH, P]), ALU.mult))
                            dve.sem_inc(diag_ready, 1)

                        sums_of(v, 0)
                        first, per = v.n, 7

                        def body(b, last):
                            v.start(b * per + first)
                            dve.wait_ge(turned, b + 1)
                            dve.tensor_copy(sumsT[:, CH // 2:], big_ps[:, CH // 2:]).then_inc(turned_out, 1)
                            dve.wait_ge(ks_done, b + 1)
                            v(dve.tensor_copy(ksum[:, bass.ds(b, 1), :].rearrange("p a n -> p (a n)"), ks_ps[:].rearrange("p c n -> p (c n)")))
                            if not last:
                                sums_of(v, b + 1)
                            dve.wait_ge(out_done, b + 1)
                            dve.tensor_copy(kv_out[:, bass.ds(b, 1), CH // 2:, :].rearrange("p a c n -> p (a c n)"),
                                            big_ps[:, CH // 2:].rearrange("p c k n -> p (c k n)")).then_inc(out_copied, 1)
                            assert last or v.n == per, v.n

                        batches(dve, body)

                    @block.scalar
                    def _(act):
                        act.wait_ge(alpha_in, 1)
                        act.activation(alpha[:], alpha[:], ACT.Exp).then_inc(alpha_done, 1)
                        with act.Fori(0, B) as b:
                            act.wait_ge(turned, b + 1)
                            act.activation(sumsT[:, 0:CH // 2], big_ps[:, 0:CH // 2], ACT.Copy).then_inc(turned_out, 1)
                            act.wait_ge(kv_done, b + 1)
                            act.activation(kv[0:DH, :, 0:MF], kv_ps[0:DH, :, 0:MF], ACT.Copy).then_inc(kv_ready, 1)
                            act.activation(kv[DH:P, :, MF:P], kv_ps[DH:P, :, MF:P], ACT.Copy).then_inc(kv_ready, 1)
                            act.wait_ge(out_done, b + 1)
                            act.activation(kv_out[:, bass.ds(b, 1), 0:CH // 2, :].rearrange("p a c n -> p (a c n)"),
                                           big_ps[:, 0:CH // 2].rearrange("p c k n -> p (c k n)"), ACT.Copy).then_inc(out_copied, 1)

                    @block.tensor
                    def _(pe):
                        pe.sem_inc(out_copied, 2)
                        pe.wait_ge(wo_in, 16)
                        with pe.Fori(0, B) as b:
                            pe.wait_ge(sums_ready, b + 1)
                            pe.wait_ge(out_copied, 2 * b + 2)
                            for c in range(CH):
                                for k in range(KD):
                                    last = pe.transpose(big_ps[:, c, k, :], sums[:, c, k * P:(k + 1) * P], g.ident[:])
                            last.then_inc(turned, 1)
                            pe.wait_ge(diag_ready, b + 1)
                            for c in range(CH):
                                last = pe.matmul(ks_ps[:, c, :], g.ones[:], k_diag[:, c, :], start=True, stop=True)
                            last.then_inc(ks_done, 1)
                            pe.wait_ge(turned_out, 2 * b + 2)
                            for c in range(CH):
                                for k in range(KD):
                                    last = pe.matmul(kv_ps[:, c, :], wv[:, k, c * P:(c + 1) * P], sumsT[:, c, k, :],
                                                     start=(k == 0), stop=(k == KD - 1))
                            last.then_inc(kv_done, 1)
                            pe.wait_ge(kv_ready, 2 * b + 2)
                            for c in range(CH):
                                last = pe.matmul(big_ps[:, c].rearrange("p k n -> p (k n)"), kv[:, c, :], wo[:, c, :],
                                                 start=True, stop=True)
                            last.then_inc(out_done, 1)

        with ExitStack() as c2:
            t = Maker(nc, c2)
            hq = t.sb("hq", [P, 2, G, D])
            kept = mk.sem("hq_kept")
            heads = Heads(mk, t, "q")
            qT, free = heads.scaled, heads.free
            dash = q_dash
            prod = t.sb("q_prod", [P, HD])
            qnT = t.sb("qnT", [P, 2, CH, P])
            y = t.sb("y1", [P, 2, G, D])
            top, shift, total, inv = t.sb("q_top", [P, H]), t.sb("q_shift", [P, H]), t.sb("q_total", [P, H]), t.sb("q_inv", [P, H])
            dash_ps = t.ps("q_dash_ps", [P, HD])
            turn_ps = t.ps("q_turn_ps", [P, CH, P])
            out_ps = t.ps("q_out_ps", [P, 512])
            own, dash_done, dash_used, shifted, exp_done = (mk.sem("pq_dve"), mk.sem("q_dash_done"), mk.sem("q_dash_used"),
                                                            mk.sem("q_shifted"), mk.sem("q_exp"))
            qn_ready, turned, turned_out, out_done, out_copied = (
                mk.sem("qn_ready"), mk.sem("qn_turned"), mk.sem("qnT_ready"), mk.sem("q_out_done"), mk.sem("q_out_copied"))
            h_in, passed = [mk.sem("hq_in0"), mk.sem("hq_in1")], mk.sem("hq_passed")
            y_out = [mk.sem("y1_out0"), mk.sem("y1_out1")]

            with nc.Block() as block:
                @block.sync
                def _(sp):
                    def load(n, k):
                        sp.dma_start(hq[:, k], h_dram[bass.ds(n * GT, GT), :].rearrange("(t p) d -> p t d", p=P)).then_inc(h_in[k], 16)

                    load(0, 0)
                    heads.load(sp, a["L1_attn_Wq"])
                    load(1, 1)

                    def body(b, last):
                        for k in range(2):
                            n = 2 * b + k
                            if not last:
                                wait_apart(sp, heads.full, n * USES + KD, passed)
                                wait_apart(sp, kept, n + 1, passed)
                                load(n + 2, k)
                            wait_apart(sp, out_copied, (n + 1) * G + 1, passed)
                            sp.dma_start(y_dram[bass.ds(n * GT, GT), :].rearrange("(t p) d -> p t d", p=P), y[:, k]).then_inc(y_out[k], 16)

                    batches(sp, body)
                    for k in range(2):
                        sp.wait_ge(y_out[k], 16 * (B + 1))

                @block.gpsimd
                def _(pool):
                    def keep(n, k, turn):
                        pool.wait_ge(y_out[k], 16 * (turn + 1))
                        wait_apart(pool, h_in[k], 16 * (turn + 1), passed)
                        pool.tensor_copy(y[:, k], hq[:, k]).then_inc(kept, 1)

                    for k in range(2):
                        pool.sem_inc(y_out[k], 16)
                    keep(0, 0, 0)
                    keep(1, 1, 0)
                    with pool.Fori(0, B - 1) as b:
                        for k in range(2):
                            keep(2 * b + k + 2, k, b + 1)

                @block.vector
                def _(dve):
                    dve.sem_inc(dash_used, 1)
                    by_head = lambda ap: ap.rearrange("p (h m) -> p h m", h=H)
                    v = Steps(dve, own)
                    PER = 6

                    def shift_tile(n, j, group):
                        dve.wait_ge(dash_done, n + 1)
                        v(dve.tensor_reduce(top[:], by_head(dash_ps[:]), AX.X, ALU.max))
                        if j % G == 0:
                            dve.wait_ge(heads.diag_copied, group + 2)
                        v(dve.tensor_tensor(shift[:], top[:], heads.half_diag[:, j // G % 2, j % G, :], ALU.add))
                        v(dve.tensor_tensor(by_head(dash[:, j % 2, :]), by_head(dash_ps[:]),
                                            shift[:].unsqueeze(2).to_broadcast([P, H, MF]), ALU.subtract))
                        dve.sem_inc(dash_used, 1)
                        dve.sem_inc(shifted, 1)

                    def normalise_tile(n, j, b):
                        dve.wait_ge(exp_done, n + 1)
                        v(dve.scalar_tensor_tensor(prod[:], dash[:, j % 2, :], KERN_EPS,
                                                   ksum[:, bass.ds(b, 1), :].rearrange("p a n -> p (a n)"), ALU.add, ALU.mult))
                        v(dve.tensor_reduce(total[:], by_head(prod[:]), AX.X, ALU.add))
                        v(dve.reciprocal(inv[:], total[:]))
                        dve.wait_ge(turned, n + 1)
                        dve.scalar_tensor_tensor(by_head(qn[:, j % 2, :]), by_head(dash[:, j % 2, :]), KERN_EPS,
                                                 inv[:].unsqueeze(2).to_broadcast([P, H, MF]), ALU.add, ALU.mult).then_inc(qn_ready, 1)

                    def finish(b, j):
                        dve.wait_ge(kept, 2 * b + j // G + 1)
                        dve.wait_ge(out_done, b * TB + j + 1)
                        row = y[:, j // G, j % G, :]
                        dve.tensor_tensor(row, out_ps[:, 0:D], row, ALU.add).then_inc(out_copied, 1)

                    dve.sem_inc(turned, 2)
                    heads.weights_low(dve)
                    heads.turned_low(dve, 0)
                    shift_tile(0, 0, 0)
                    shift_tile(1, 1, 0)
                    normalise_tile(0, 0, 0)
                    first = v.n

                    def body(b, last):
                        for j in range(TB):
                            n = b * TB + j
                            v.start(n * PER + first)
                            if j % G == 1 and (not last or j + 3 < TB):
                                heads.turned_low(dve, 2 * b + j // G + 1)
                            if not last or j + 2 < TB:
                                shift_tile(n + 2, j + 2, 2 * b + (j + 2) // G)
                            if not last or j + 1 < TB:
                                normalise_tile(n + 1, j + 1, b + (j + 1) // TB)
                            if j:
                                finish(b, j - 1)
                        finish(b, TB - 1)

                    batches(dve, body)

                @block.scalar
                def _(act):
                    heads.start_act(act)
                    act.sem_inc(out_copied, 1)
                    act.sem_inc(turned_out, 1)

                    def exp(n, j):
                        act.wait_ge(shifted, n + 1)
                        act.activation(dash[:, j % 2, :], dash[:, j % 2, :], ACT.Exp).then_inc(exp_done, 1)

                    heads.copy(act, 0, 0)
                    heads.copy_diag(act, 0, 0)
                    for j in range(2):
                        exp(j, j)

                    def body(b, last):
                        for j in range(TB):
                            n = b * TB + j
                            new_group = j % G == 1 and (not last or j + 3 < TB)
                            if new_group:
                                group, place = 2 * b + j // G + 1, 1 - j // G
                                heads.copy(act, group, place)
                            act.wait_ge(turned, n + 1 + 2)
                            act.activation(qnT[:, j % 2], turn_ps[:], ACT.Copy).then_inc(turned_out, 1)
                            if not last or j + 2 < TB:
                                exp(n + 2, j)
                            if new_group:
                                heads.copy_diag(act, group, place)

                    batches(act, body)

                @block.tensor
                def _(pe):
                    def project(n, k, uses):
                        pe.wait_ge(h_in[k], uses)
                        heads.project(pe, n, hq[:, k], g.ident[:], half_heads[:])

                    def products(n, j, group):
                        if j == 0:
                            pe.wait_ge(free, (group + 1) * USES + 2)
                            heads.rest_of_diag(pe, group, half_heads[:])
                        pe.wait_ge(dash_used, n + 1)
                        random_features(pe, dash_ps, qT, j, features[:]).then_inc(dash_done, 1)

                    def outputs(b, j):
                        n = b * TB + j
                        pe.wait_ge(turned_out, n + 2)
                        pe.wait_ge(out_copied, n + 1)
                        for c in range(CH):
                            last = pe.matmul(out_ps[:, 0:D], qnT[:, j % 2, c, :],
                                             kv_out[:, bass.ds(b, 1), c, :].rearrange("p a n -> p (a n)"),
                                             start=(c == 0), stop=(c == CH - 1))
                        last.then_inc(out_done, 1)

                    pe.wait_ge(heads.w_low, 1)
                    project(0, 0, 16)
                    for j in range(3):
                        products(j, j, 0)

                    def body(b, last):
                        for j in range(TB):
                            n = b * TB + j
                            ahead = not last or j + 3 < TB
                            if j % G == 1 and ahead:
                                k = j // G
                                project(2 * b + k + 1, 1 - k, 16 * (b + k + 1))
                            pe.wait_ge(qn_ready, n + 1)
                            pe.wait_ge(turned_out, n + 1)
                            for c in range(CH):
                                turn = pe.transpose(turn_ps[:, c, :], qn[:, j % 2, c * P:(c + 1) * P], g.ident[:])
                            turn.then_inc(turned, 1)
                            if j:
                                outputs(b, j - 1)
                            if ahead:
                                products(n + 3, (j + 3) % G, 2 * b + (j + 3) // G)
                        outputs(b, TB - 1)

                    batches(pe, body)

    mk.clear_signals()
    elu_ffn(nc, mk, g, a, y_dram)


RINGS = 4
PLACES = KD + CF


class Ffn:

    WORK = 4
    HID_CREDIT = 2

    def __init__(self, nc, mk, t, tag):
        sb, ps, sem = (lambda n, *s: t.sb(f"{tag}_{n}", *s)), (lambda n, *s: t.ps(f"{tag}_{n}", *s)), (lambda n: mk.sem(f"{tag}_{n}"))
        pair = lambda n, shape: (sb(n + "_hi", shape, F32R), sb(n + "_lo", shape, F32R))
        self.rows = sb("rows", [P, 2, G, D])
        self.rowsT, self.hid = pair("rowsT", [P, KD, GT]), pair("hid", [P, 2, CF, GT])
        self.w1, self.w2 = pair("w1", [P, KD, DFF]), pair("w2", [P, CF, D])
        self.work = sb("work", [P, self.WORK, GT])
        self.raw = sb("raw", [P, 2, G, D])
        self.back = sb("back", [P, G, D])
        self.st, self.mv, self.var, self.rstd = sb("st", [P, G, 6]), sb("mv", [P, G, 2]), sb("var", [P, G]), sb("rstd", [P, G])
        self.ring = ps("ring", [P, RINGS, GT])
        self.down = ps("down", [P, G, 512])
        self.own, self.var_ready, self.rstd_ready = sem("dve"), sem("var"), sem("rstd_ready")
        self.weights_in, self.rows_ready, self.full = sem("weights_in"), sem("rows_ready"), sem("full")
        self.act_free, self.dve_free, self.hid_ready = sem("act_free"), sem("dve_free"), sem("hid_ready")
        self.down_done, self.down_used = sem("down_done"), sem("down_used")
        self.hid_high, self.hid_low = sem("hid_high"), sem("hid_low")
        self.weights_high, self.weights_low = sem("weights_high"), sem("weights_low")
        self.back_ready = sem("back_ready")
        self.normed, self.gated, self.back_used, self.passed = sem("normed"), sem("gated"), sem("back_used"), sem("passed")

    def place(self, k, i):
        return (k * PLACES + i) % RINGS

    def raw_weights(self):
        w1, w2 = self.work[:].rearrange("p a n -> p (a n)"), self.raw[:].rearrange("p a t d -> p (a t d)")
        return [(raw, *(x[:].rearrange("p a n -> p (a n)") for x in w)) for raw, w in ((w1, self.w1), (w2, self.w2))]

    def load_weights(self, sp, w1, w2):
        (raw1, *_), (raw2, *_) = self.raw_weights()
        sp.dma_start(raw1.rearrange("p (k n) -> p k n", k=KD), w1.rearrange("(k p) n -> p k n", p=P)).then_inc(self.weights_in, 16)
        sp.dma_start(raw2.rearrange("p (c n) -> p c n", c=CF), w2.rearrange("(c p) n -> p c n", p=P)).then_inc(self.weights_in, 16)

    def weights_high_part(self, act):
        act.wait_ge(self.weights_in, 32)
        for raw, high, _ in self.raw_weights():
            act.activation(high, raw, ACT.Copy).then_inc(self.weights_high, 1)

    def weights_low_part(self, dve, i):
        raw, high, low = self.raw_weights()[i]
        dve.wait_ge(self.weights_high, i + 1)
        dve.tensor_tensor(low, raw, high.bitcast(F32), ALU.subtract).then_inc(self.weights_low, 1)

    def products(self, pe, out, w, x, start, stop):
        pe.matmul(out, w[0], x[0], start=start, stop=False)
        pe.matmul(out, w[0], x[1], start=False, stop=False)
        return pe.matmul(out, w[1], x[0], start=False, stop=stop)

    def take(self, pe, n, i):
        pe.wait_ge(self.act_free, n * PLACES + i + 1)
        pe.wait_ge(self.dve_free, n * PLACES + i + 1)

    def turn(self, pe, n, k, ident):
        pe.wait_ge(self.rows_ready, n + 1)
        for i in range(KD):
            self.take(pe, n, i)
            for j in range(G):
                last = pe.transpose(self.ring[:, self.place(k, i), j * P:(j + 1) * P], self.rows[:, k, j, i * P:(i + 1) * P], ident)
            last.then_inc(self.full, 1)

    def up(self, pe, n, k, down=()):
        down = iter(down)
        pe.wait_ge(self.dve_free, n * PLACES + KD + RINGS)
        for c in range(CF):
            self.take(pe, n, KD + c)
            for d in range(KD):
                last = self.products(pe, self.ring[:, self.place(k, KD + c), :], [w[:, d, c * P:(c + 1) * P] for w in self.w1],
                                     [x[:, d, :] for x in self.rowsT], d == 0, d == KD - 1)
            last.then_inc(self.full, 1)
            if c % 2 and c > 1:
                next(down, None)

    def back_down(self, pe, n, k):
        pe.wait_ge(self.hid_low, (n + 1) * CF + self.WORK)
        for j in range(G):
            pe.wait_ge(self.down_used, n * G + j + 1)
            for c in range(CF):
                last = self.products(pe, self.down[:, j, 0:D], [h[:, k, c, j * P:(j + 1) * P] for h in self.hid],
                                     [w[:, c, :] for w in self.w2], c == 0, c == CF - 1)
            last.then_inc(self.down_done, 1)
            yield

    def tensor_program(self, pe, ident, b_loop):
        self.turn(pe, 0, 0, ident)
        pe.wait_ge(self.weights_low, 1)
        self.up(pe, 0, 0)
        self.turn(pe, 1, 1, ident)
        pe.wait_ge(self.weights_low, 2)

        def body(b, last):
            for k in range(2):
                n = 2 * b + k
                down = self.back_down(pe, n, k)
                if k == 0 or not last:
                    self.up(pe, n + 1, 1 - k, down)
                if not last:
                    self.turn(pe, n + 2, k, ident)
                for _ in down:
                    pass

        b_loop(pe, body)

    def turned_high(self, act, n, k):
        for i in range(KD):
            act.wait_ge(self.full, n * PLACES + i + 1)
            act.activation(self.rowsT[0][:, i, :], self.ring[:, self.place(k, i), :], ACT.Copy).then_inc(self.act_free, 1)

    def turned_low(self, dve, n, k):
        for i in range(KD):
            dve.wait_ge(self.act_free, n * PLACES + i + 1 + RINGS)
            dve.tensor_tensor(self.rowsT[1][:, i, :], self.ring[:, self.place(k, i), :], self.rowsT[0][:, i, :].bitcast(F32),
                              ALU.subtract).then_inc(self.dve_free, 1)

    def hidden_high(self, act, n, k, c):
        act.wait_ge(self.hid_ready, n * CF + c + 1 + self.HID_CREDIT)
        act.activation(self.hid[0][:, k, c, :], self.work[:, c % self.WORK, :], ACT.Copy).then_inc(self.hid_high, 1)

    def hidden_low(self, pool, n, k, meanwhile={}):
        for c in range(CF):
            if c in meanwhile:
                meanwhile[c]()
            pool.wait_ge(self.hid_high, n * CF + c + 1)
            pool.tensor_tensor(self.hid[1][:, k, c, :], self.work[:, c % self.WORK, :], self.hid[0][:, k, c, :].bitcast(F32),
                               ALU.subtract).then_inc(self.hid_low, 1)


def columns(ap):
    return ap.rearrange("(c p) -> p c", p=P)


def elu_ffn(nc, mk, g, a, y_dram):
    with ExitStack() as ctx:
        t = Maker(nc, ctx)
        f = Ffn(nc, mk, t, "elu")
        y = t.sb("elu_y", [P, 2, G, D])
        base = f.raw
        e, r = t.sb("elu_e", [P, 2, GT]), f.work
        b1, b1_less = t.sb("elu_b1", [P, CF]), t.sb("elu_b1_less", [P, CF])
        vec = t.sb("elu_vec", [P, 5, D])
        LN1_G, LN1_B, B2, LN2_G, LN2_B = range(5)
        y_in = [mk.sem("elu_y_in0"), mk.sem("elu_y_in1")]
        small_in, base_ready, base_used = mk.sem("elu_small_in"), mk.sem("elu_base_ready"), mk.sem("elu_base_used")
        mod = g.modb[:].rearrange("p b (s d) -> p b s d", s=6)
        gate_g, gate_b = mod[:, :, CA, :], mod[:, :, SA, :]
        gained, shifted = mk.sem("elu_gained"), mk.sem("elu_shifted")
        spread = lambda i: vec[:, i:i + 1, :].to_broadcast([P, G, D])

        with nc.Block() as block:
            @block.sync
            def _(sp):
                def load(n, k):
                    sp.dma_start(y[:, k], y_dram[bass.ds(n * GT, GT), :].rearrange("(t p) d -> p t d", p=P)).then_inc(y_in[k], 16)

                load(0, 0)
                for i, name in enumerate(("ln1_g", "ln1_b", "b2", "ln2_g", "ln2_b")):
                    sp.dma_start(vec[:, i, :], a[f"L1_attn_{name}"].partition_broadcast(P)).then_inc(small_in, 16)
                sp.dma_start(b1[:], columns(a["L1_attn_b1"]), allow_slow_non_contiguous=True).then_inc(small_in, 16)
                load(1, 1)
                f.load_weights(sp, a["L1_attn_W1"], a["L1_attn_W2"])
                with sp.Fori(0, B - 1) as b:
                    for k in range(2):
                        sp.wait_ge(f.rows_ready, 2 * b + k + 1)
                        load(2 * b + k + 2, k)

            @block.gpsimd
            def _(pool):
                pool.wait_ge(small_in, 96)

                def power(norms):
                    pool.wait_ge(f.var_ready, norms + 1)
                    rsqrt_rows(pool, f.rstd, f.var, g.minus_half, G, f.rstd_ready)

                def gain(n, k):
                    pool.wait_ge(f.normed, n + 1)
                    pool.tensor_tensor(f.rows[:, k], f.rows[:, k], spread(LN1_G), ALU.mult).then_inc(gained, 1)

                def shift(n, k):
                    pool.wait_ge(gained, n + 1)
                    pool.tensor_tensor(f.rows[:, k], f.rows[:, k], spread(LN1_B), ALU.add).then_inc(f.rows_ready, 1)

                def finish(n, k, b):
                    wait_apart(pool, f.gated, n + 1, f.passed)
                    pool.tensor_tensor(f.back[:], f.back[:], gate_b[:, bass.ds(b, 1), :].to_broadcast([P, G, D]), ALU.add).then_inc(shifted, 1)
                    wait_apart(pool, shifted, n + 1, f.passed)
                    x = g.x[:, bass.ds(b * TB + k * G, G), :]
                    pool.tensor_tensor(x, x, f.back[:], ALU.add).then_inc(f.back_used, 1)

                def add_bias(n, k):
                    pool.wait_ge(base_used, n + 1)
                    pool.wait_ge(f.rows_ready, n + 1)
                    pool.tensor_tensor(base[:, k], f.rows[:, k], spread(B2), ALU.add).then_inc(base_ready, 1)

                power(0)
                power(1)
                for k in range(2):
                    gain(k, k)
                    shift(k, k)
                pool.wait_ge(f.weights_low, 2)
                add_bias(0, 0)
                f.hidden_low(pool, 0, 0)

                def body(b, last):
                    for k in range(2):
                        n = 2 * b + k
                        if not last:
                            f.hidden_low(pool, n + 1, 1 - k, {0: lambda: power(2 + 2 * n), 2: lambda: gain(n + 2, k),
                                                              4: lambda: shift(n + 2, k)})
                            add_bias(n + 1, 1 - k)
                            power(3 + 2 * n)
                            finish(n, k, b)
                        else:
                            if k == 0:
                                f.hidden_low(pool, n + 1, 1 - k)
                                add_bias(n + 1, 1 - k)
                            power(2 + 2 * n - k)
                            finish(n, k, b)

                batches(pool, body)

            @block.scalar
            def _(act):
                act.wait_ge(small_in, 96)
                act.sem_inc(f.act_free, RINGS)
                f.weights_high_part(act)

                def up(n, k):
                    f.turned_high(act, n, k)
                    for c in range(CF):
                        act.wait_ge(f.dve_free, n * PLACES + KD + c + 1 + RINGS)
                        act.wait_ge(f.hid_ready, n * CF + c + 1)
                        act.activation(e[:, c % 2, :], f.ring[:, f.place(k, KD + c), :], ACT.Exp,
                                       bias=b1[:, c:c + 1]).then_inc(f.act_free, 1)
                        if c:
                            f.hidden_high(act, n, k, c - 1)
                    f.hidden_high(act, n, k, CF - 1)

                up(0, 0)

                def body(b, last):
                    up(2 * b + 1, 1)
                    if not last:
                        up(2 * b + 2, 0)

                batches(act, body)

            @block.vector
            def _(dve):
                v = Steps(dve, f.own)
                dve.sem_inc(f.dve_free, RINGS)
                dve.sem_inc(f.down_used, G)
                dve.sem_inc(f.hid_ready, f.HID_CREDIT)
                dve.sem_inc(f.hid_low, f.WORK)
                dve.sem_inc(f.back_used, 1)
                dve.sem_inc(base_used, 2)

                def prepare(v, n, k, b, norms, based=None):
                    dve.wait_ge(y_in[k], 16 * (b + 1))
                    if based is not None:
                        dve.wait_ge(base_ready, based)
                    layer_norm_stats(v, g.spare, f.st, f.mv, f.var, G, lambda j: y[:, k, j, :], ENC_EPS, f.var_ready)
                    yield
                    dve.wait_ge(f.rstd_ready, norms + 1)
                    for j in range(G):
                        v.mark(dve.tensor_scalar(f.rows[:, k, j, :], y[:, k, j, :], f.mv[:, j, 0:1], f.rstd[:, j:j + 1],
                                                 ALU.subtract, ALU.mult))
                    v.sync()
                    dve.sem_inc(f.normed, 1)

                def hidden(v, n, k, meanwhile=()):
                    meanwhile = iter(meanwhile)
                    for c in range(CF + 1):
                        if c < CF:
                            dve.wait_ge(f.full, n * PLACES + KD + c + 1)
                            dve.wait_ge(f.hid_low, n * CF + c + 1)
                            dve.tensor_scalar(r[:, c % f.WORK, :], f.ring[:, f.place(k, KD + c), :], b1_less[:, c:c + 1], -1.0,
                                              ALU.add, ALU.max).then_inc(f.dve_free, 1)
                        if c:
                            dve.wait_ge(f.dve_free, n * PLACES + KD + c + RINGS)
                            dve.wait_ge(f.act_free, n * PLACES + KD + c + RINGS)
                            part = r[:, (c - 1) % f.WORK, :]
                            dve.scalar_tensor_tensor(part, e[:, (c - 1) % 2, :], 1.0, part, ALU.min, ALU.add).then_inc(f.hid_ready, 1)
                        if c in (0, 2):
                            next(meanwhile, None)
                    for _ in meanwhile:
                        pass

                def result(v, n, k, b, norms):
                    dve.wait_ge(f.back_used, n + 1)
                    dve.wait_ge(base_ready, n + 1)
                    for j in range(G):
                        dve.wait_ge(f.down_done, n * G + j + 1)
                        v.mark(dve.tensor_tensor(f.back[:, j, :], f.down[:, j, 0:D], base[:, k, j, :], ALU.add))
                    v.sync()
                    dve.sem_inc(f.down_used, G)
                    dve.sem_inc(base_used, 1)
                    layer_norm_stats(v, g.spare, f.st, f.mv, f.var, G, lambda j: f.back[:, j, :], ENC_EPS, f.var_ready)
                    dve.wait_ge(f.rstd_ready, norms + 1)
                    for j in range(G):
                        v.mark(dve.tensor_scalar(f.back[:, j, :], f.back[:, j, :], f.mv[:, j, 0:1], f.rstd[:, j:j + 1],
                                                 ALU.subtract, ALU.mult))
                    v.sync()
                    dve.tensor_tensor(f.back[:], f.back[:], gate_g[:, bass.ds(b, 1), :].to_broadcast([P, G, D]),
                                      ALU.mult).then_inc(f.gated, 1)

                for k in range(2):
                    for _ in prepare(v, k, k, 0, k):
                        pass
                dve.wait_ge(small_in, 96)
                v.mark(dve.tensor_scalar(b1_less[:], b1[:], -1.0, None, ALU.add))
                v.sync()
                f.weights_low_part(dve, 0)
                f.turned_low(dve, 0, 0)
                f.weights_low_part(dve, 1)
                hidden(v, 0, 0)
                v.mark(dve.tensor_tensor(gate_g, mod[:, :, GA, :], vec[:, LN2_G:LN2_G + 1, :].to_broadcast([P, B, D]), ALU.mult))
                v.mark(dve.tensor_tensor(gate_b, mod[:, :, GA, :], vec[:, LN2_B:LN2_B + 1, :].to_broadcast([P, B, D]), ALU.mult))
                v.sync()
                f.turned_low(dve, 1, 1)
                first = v.n
                PREP, RES = 3 * G, 4 * G
                per = 2 * (PREP + RES)

                def body(b, last):
                    v = Steps(dve, f.own, b * per + first)
                    for k in range(2):
                        n = 2 * b + k
                        if not last:
                            hidden(v, n + 1, 1 - k, prepare(v, n + 2, k, b + 1, 2 + 2 * n, n + 1))
                            f.turned_low(dve, n + 2, k)
                        elif k == 0:
                            hidden(v, n + 1, 1 - k)
                        result(v, n, k, b, 2 + 2 * n - k if last else 3 + 2 * n)
                    assert last or v.n == per, (v.n, per)

                batches(dve, body)

            @block.tensor
            def _(pe):
                f.tensor_program(pe, g.ident[:], batches)
        mk.clear_signals()


def wave_ffn(nc, mk, g, a, out):
    TURN = 1.0 / (2.0 * 3.141592653589793)
    FULL = 6.283185
    with ExitStack() as ctx:
        t = Maker(nc, ctx)
        f = Ffn(nc, mk, t, "wave")
        whole, turns, wave, u = (t.sb("wave_whole", [P, 2, GT]), t.sb("wave_turns", [P, 2, GT]), t.sb("wave_sine", [P, 2, GT]),
                                 t.sb("wave_u", [P, 2, GT]))
        vec = t.sb("wave_vec", [P, 8, CF])
        B1, THETA, W_RE, W_IM, OFFSET, AMP, SINE, COSINE = range(8)
        part = t.sb("wave_part", [P, 2, CF])
        b2 = t.sb("wave_b2", [P, D])
        small_in, consts, angles, sines = mk.sem("wave_small_in"), mk.sem("wave_consts"), mk.sem("wave_angles"), mk.sem("wave_sines")
        turns_ready, sine_ready, gained, x_ready, x_out = (mk.sem("wave_turns_ready"), mk.sem("wave_sine_ready"),
                                                           mk.sem("wave_gained"), mk.sem("wave_x_ready"), mk.sem("x_out"))
        mod = g.modb[:].rearrange("p b (s d) -> p b s d", s=6)

        with nc.Block() as block:
            @block.sync
            def _(sp):
                for i, name in ((B1, "b1"), (THETA, "quantum_phases"), (W_RE, "quantum_weights_real"), (W_IM, "quantum_weights_imag")):
                    sp.dma_start(vec[:, i, :], columns(a[f"L1_ffn_{name}"]), allow_slow_non_contiguous=True).then_inc(small_in, 16)
                sp.dma_start(b2[:], a["L1_ffn_b2"].partition_broadcast(P)).then_inc(small_in, 16)
                f.load_weights(sp, a["L1_ffn_W1"], a["L1_ffn_W2"])
                rows = out.rearrange("b (t p) d -> p (b t) d", p=P)
                with sp.Fori(0, NG) as n:
                    sp.wait_ge(x_ready, n + 2)
                    sp.dma_start(rows[:, bass.ds(n * G, G), :], g.x[:, bass.ds(n * G, G), :]).then_inc(x_out, 16)
                sp.wait_ge(x_out, 16 * NG)

            @block.gpsimd
            def _(pool):
                spread = lambda i, b: mod[:, bass.ds(b, 1), i, :].to_broadcast([P, G, D])

                def power(n):
                    pool.wait_ge(f.var_ready, n + 1)
                    rsqrt_rows(pool, f.rstd, f.var, g.minus_half, G, f.rstd_ready)

                def gain(n, k, b):
                    wait_apart(pool, f.normed, n + 1, f.passed)
                    pool.tensor_tensor(f.rows[:, k], f.rows[:, k], spread(CB, b), ALU.mult).then_inc(gained, 1)

                def shift(n, k, b):
                    wait_apart(pool, gained, n + 1, f.passed)
                    pool.tensor_tensor(f.rows[:, k], f.rows[:, k], spread(SB, b), ALU.add).then_inc(f.rows_ready, 1)

                def finish(n, k, b):
                    wait_apart(pool, f.back_ready, n + 1, f.passed)
                    pool.tensor_tensor(f.back[:], f.back[:], spread(GB, b), ALU.mult).then_inc(f.gated, 1)
                    wait_apart(pool, f.gated, n + 1, f.passed)
                    x = g.x[:, bass.ds(b * TB + k * G, G), :]
                    pool.tensor_tensor(x, x, f.back[:], ALU.add).then_inc(x_ready, 1)

                power(0)
                power(1)
                for k in range(2):
                    gain(k, k, 0)
                    shift(k, k, 0)
                f.hidden_low(pool, 0, 0)

                def body(b, last):
                    for k in range(2):
                        n = 2 * b + k
                        if not last:
                            power(n + 2)
                            gain(n + 2, k, b + 1)
                            f.hidden_low(pool, n + 1, 1 - k, {1: lambda: shift(n + 2, k, b + 1)})
                        elif k == 0:
                            f.hidden_low(pool, n + 1, 1 - k)
                        finish(n, k, b)

                batches(pool, body)

            @block.scalar
            def _(act):
                act.sem_inc(f.act_free, RINGS)
                f.weights_high_part(act)
                act.wait_ge(angles, 1)
                act.activation(vec[:, SINE, :], part[:, 0, :], ACT.Sin, scale=FULL)
                act.activation(vec[:, COSINE, :], part[:, 1, :], ACT.Sin, scale=FULL).then_inc(sines, 1)
                act.wait_ge(consts, 1)

                def up(n, k):
                    f.turned_high(act, n, k)
                    used = lambda c: act.wait_ge(f.dve_free, n * PLACES + KD + c + 1 + RINGS)
                    for c in range(CF + 4):
                        if c < CF:
                            act.wait_ge(f.full, n * PLACES + KD + c + 1)
                            act.wait_ge(sine_ready, n * CF + c + 1)
                            act.activation(turns[:, c % 2, :], f.ring[:, f.place(k, KD + c), :], ACT.Identity, scale=0.1 * TURN,
                                           bias=vec[:, OFFSET, c:c + 1]).then_inc(f.act_free, 1)
                        if 1 <= c <= CF:
                            act.wait_ge(turns_ready, n * CF + c)
                            if c >= 3:
                                used(c - 3)
                            act.activation(wave[:, (c - 1) % 2, :], turns[:, (c - 1) % 2, :], ACT.Sin, scale=FULL).then_inc(sine_ready, 1)
                        if 3 <= c < CF + 3:
                            used(c - 3)
                            act.wait_ge(f.hid_low, n * CF + c - 3 + 1)
                            act.activation(f.work[:, (c - 3) % f.WORK, :], u[:, (c - 3) % 2, :], ACT.Relu,
                                           bias=vec[:, B1, c - 3:c - 2]).then_inc(f.hid_ready, 1)
                        if c >= 4:
                            f.hidden_high(act, n, k, c - 4)

                up(0, 0)

                def body(b, last):
                    up(2 * b + 1, 1)
                    if not last:
                        up(2 * b + 2, 0)

                batches(act, body)

            @block.vector
            def _(dve):
                v = Steps(dve, f.own)
                dve.sem_inc(f.dve_free, RINGS)
                dve.sem_inc(f.down_used, G)
                dve.sem_inc(f.hid_ready, f.HID_CREDIT)
                dve.sem_inc(f.hid_low, f.WORK)
                dve.sem_inc(sine_ready, 2)
                dve.sem_inc(x_ready, 1)

                def prepare(v, n, k, b):
                    tile = lambda j: g.x[:, bass.ds(b * TB + k * G + j, 1), :]
                    layer_norm_stats(v, g.spare, f.st, f.mv, f.var, G, tile, LN_EPS, f.var_ready)
                    yield
                    dve.wait_ge(f.rstd_ready, n + 1)
                    for j in range(G):
                        v.mark(dve.tensor_scalar(f.rows[:, k, j:j + 1, :], tile(j), f.mv[:, j, 0:1], f.rstd[:, j:j + 1],
                                                 ALU.subtract, ALU.mult))
                    v.sync()
                    dve.sem_inc(f.normed, 1)

                def hidden(v, n, k, meanwhile=()):
                    meanwhile = iter(meanwhile)
                    for c in range(CF + 2):
                        if c < CF:
                            i = c % 2
                            dve.wait_ge(f.act_free, n * PLACES + KD + c + 1 + RINGS)
                            v(dve.tensor_scalar(whole[:, i, :], turns[:, i, :], ROUND, ROUND, ALU.add, ALU.subtract))
                            dve.tensor_tensor(turns[:, i, :], turns[:, i, :], whole[:, i, :], ALU.subtract).then_inc(turns_ready, 1)
                        if c >= 2:
                            z, i = f.ring[:, f.place(k, KD + c - 2), :], c % 2
                            dve.wait_ge(sine_ready, n * CF + c - 1 + 2)
                            dve.wait_ge(f.hid_ready, n * CF + max(c - 3, 0) + f.HID_CREDIT)
                            dve.scalar_tensor_tensor(u[:, i, :], wave[:, i, :], vec[:, AMP, c - 2:c - 1], z, ALU.mult,
                                                     ALU.add).then_inc(f.dve_free, 1)
                        if c in (0, 2):
                            next(meanwhile, None)
                    for _ in meanwhile:
                        pass

                def result(v, n):
                    dve.wait_ge(x_ready, n + 1)
                    for j in range(G):
                        dve.wait_ge(f.down_done, n * G + j + 1)
                        v.mark(dve.tensor_tensor(f.back[:, j, :], f.down[:, j, 0:D], b2[:], ALU.add))
                    v.sync()
                    dve.sem_inc(f.down_used, G)
                    dve.sem_inc(f.back_ready, 1)

                for k in range(2):
                    for _ in prepare(v, k, k, 0):
                        pass
                dve.wait_ge(small_in, 80)
                v(dve.tensor_scalar(part[:, 0, :], vec[:, THETA, :], TURN, None, ALU.mult))
                v(dve.tensor_scalar(part[:, 0, :], part[:, 0, :], ROUND, ROUND, ALU.add, ALU.subtract))
                v(dve.scalar_tensor_tensor(vec[:, THETA, :], part[:, 0, :], -PI2_HI, vec[:, THETA, :], ALU.mult, ALU.add))
                v(dve.scalar_tensor_tensor(vec[:, THETA, :], part[:, 0, :], -PI2_LO, vec[:, THETA, :], ALU.mult, ALU.add))
                v(dve.tensor_scalar(vec[:, THETA, :], vec[:, THETA, :], TURN, None, ALU.mult))
                for i, ahead in ((0, 0.0), (1, 0.25)):
                    v(dve.tensor_scalar(part[:, i, :], vec[:, THETA, :], ahead, ROUND, ALU.add, ALU.add))
                    v(dve.tensor_scalar(part[:, i, :], part[:, i, :], ROUND, ahead, ALU.subtract, ALU.subtract))
                    v(dve.tensor_tensor(part[:, i, :], vec[:, THETA, :], part[:, i, :], ALU.subtract))
                dve.sem_inc(angles, 1)
                v(dve.scalar_tensor_tensor(vec[:, OFFSET, :], vec[:, B1, :], 0.1 * TURN, vec[:, THETA, :], ALU.mult, ALU.add))
                dve.wait_ge(sines, 1)
                v.mark(dve.tensor_tensor(vec[:, COSINE, :], vec[:, COSINE, :], vec[:, W_RE, :], ALU.mult))
                v.mark(dve.tensor_tensor(vec[:, SINE, :], vec[:, SINE, :], vec[:, W_IM, :], ALU.mult))
                v.sync()
                v(dve.tensor_tensor(vec[:, AMP, :], vec[:, COSINE, :], vec[:, SINE, :], ALU.add))
                v(dve.scalar_tensor_tensor(vec[:, AMP, :], vec[:, AMP, :], 0.1, vec[:, W_IM, :], ALU.mult, ALU.mult))
                dve.sem_inc(consts, 1)
                f.weights_low_part(dve, 0)
                f.turned_low(dve, 0, 0)
                f.weights_low_part(dve, 1)
                hidden(v, 0, 0)
                f.turned_low(dve, 1, 1)
                first = v.n
                per = 2 * (3 * G + CF + G)

                def body(b, last):
                    v = Steps(dve, f.own, b * per + first)
                    for k in range(2):
                        n = 2 * b + k
                        if not last:
                            hidden(v, n + 1, 1 - k, prepare(v, n + 2, k, b + 1))
                            f.turned_low(dve, n + 2, k)
                        elif k == 0:
                            hidden(v, n + 1, 1 - k)
                        result(v, n)
                    assert last or v.n == per, (v.n, per)

                batches(dve, body)

            @block.tensor
            def _(pe):
                f.tensor_program(pe, g.ident[:], batches)
        mk.clear_signals()


class Chip:
    pass


def program(nc, a, out):
    with ExitStack() as ctx:
        mk = Maker(nc, ctx)
        g = Chip()
        g.x = mk.sb("x", [P, NT, D])
        g.modb = mk.sb("modb", [P, B, 6 * D])
        g.ident, g.flip, g.ones = mk.sb("ident", [P, P]), mk.sb("flip", [P, P]), mk.sb("ones", [P, P])
        g.minus_half, g.eye_b = mk.sb("minus_half", [P, TB]), mk.sb("eye_b", [P, B, B])
        g.spare, g.pool_spare, g.pool_max = mk.sb("spare", [P, 1]), mk.sb("pool_spare", [P, 1]), mk.sb("pool_max", [P, 1])
        g.mod_dram = nc.dram_tensor("mod_dram", (2, B, 6 * D), F32, kind="Internal").ap()
        with ExitStack() as c:
            w = Maker(nc, c)
            g.wqkv, g.wconv = w.sb("wqkv", [P, 6, D]), w.sb("wconv", [P, KD])
            setup(nc, mk, g, a)
            agent_attention(nc, mk, g)
            mk.clear_signals()
        expert_choice(nc, mk, g, a)
        performer(nc, mk, g, a)
        wave_ffn(nc, mk, g, a, out)


_INS = ["L0_attn_x", "L0_attn_w_qkv", "L0_attn_w_conv1", "L0_ffn_Wr", "L0_ffn_W1", "L0_ffn_b1", "L0_ffn_W2", "L0_ffn_b2",
        "L0_c", "L0_wmod", "L1_attn_Wq", "L1_attn_Wk", "L1_attn_Wv", "L1_attn_Wo", "L1_attn_proj", "L1_attn_W1",
        "L1_attn_b1", "L1_attn_W2", "L1_attn_b2", "L1_attn_ln1_g", "L1_attn_ln1_b", "L1_attn_ln2_g", "L1_attn_ln2_b",
        "L1_ffn_W1", "L1_ffn_b1", "L1_ffn_quantum_phases", "L1_ffn_quantum_weights_real", "L1_ffn_quantum_weights_imag",
        "L1_ffn_W2", "L1_ffn_b2", "L1_c", "L1_wmod"]


def kernel(**inputs):
    import numpy as _np
    import concourse.bacc as _bacc
    from concourse import mybir as _mybir
    from concourse.bass_utils import run_bass_kernel_spmd as _run

    nc = _bacc.Bacc("TRN2", target_bir_lowering=False, num_devices=1)
    arrays, args = {}, {}
    for name in _INS:
        a = _np.ascontiguousarray(inputs[name])
        arrays[f"in_{name}_dram"] = a
        args[name] = nc.dram_tensor(f"in_{name}_dram", a.shape, _mybir.dt.from_np(a.dtype), kind="ExternalInput").ap()
    out = nc.dram_tensor("out_0_dram", (B, N, D), F32, kind="ExternalOutput").ap()
    program(nc, args, out)
    r = _run(nc, [arrays], core_ids=[0])
    return r.results[0]["out_0_dram"]
```
